# Optimizing a Trainium2 kernel written in Bass

```python
import numpy as np
import jax
import jax.numpy as jnp

def _softmax(x, axis=-1):
    return jax.nn.softmax(x, axis=axis)

def _gelu(x):
    return jax.nn.gelu(x, approximate=True)

def _silu(x):
    return jax.nn.silu(x)

def _sigmoid(x):
    return jax.nn.sigmoid(x)

def _layernorm(x, axis=-1, eps=1e-05):
    m = jnp.mean(x, axis=axis, keepdims=True)
    v = jnp.var(x, axis=axis, keepdims=True)
    return (x - m) / jnp.sqrt(v + eps)

def _scatter_add(tgt, idx, src, axis=0):
    return tgt.at[idx].add(src)

def _segment_sum(src, seg, n):
    return jax.ops.segment_sum(src, seg, n)
kernel_name = 'mk_flamingo_gated_d2_seqx_r8_f4b7b9'

def setup_inputs(seed: int=0):
    np.random.seed(seed)
    _w = jnp.asarray

    def _rec_inputs():
        import jax
        import jax.numpy as jnp
        _rk = jax.random.key(seed)
        x = -0.000125 + 0.9999 * jax.random.normal(jax.random.fold_in(_rk, 1), (8, 256, 128), jnp.float32)
        _lenS = 256 - jax.random.randint(jax.random.fold_in(_rk, 7), (8,), 0, max(1, 256 // 4) + 1, jnp.int32)
        _lenS2 = 512 - jax.random.randint(jax.random.fold_in(_rk, 8), (8,), 0, max(1, 512 // 4) + 1, jnp.int32)
        _ctx_768P = jax.random.normal(jax.random.fold_in(_rk, 11), (8, 16, 96), jnp.float32)
        _ctx_768c = jax.random.dirichlet(jax.random.fold_in(_rk, 511), 0.3 * jnp.ones((16,), jnp.float32), (8, 512))
        _ctx_768t = jnp.einsum('bsk,bkd->bsd', _ctx_768c, _ctx_768P)
        _ctx_768t = _ctx_768t * jax.lax.rsqrt(jnp.mean(jnp.square(_ctx_768t)) + 1e-12) * 0.953939
        ctx_768 = 0.00243539 + 0.99952 * (_ctx_768t + 0.3 * jax.random.normal(jax.random.fold_in(_rk, 611), (8, 512, 96), jnp.float32))
        _g = jax.random.normal(jax.random.fold_in(_rk, 9001), (2, 2), jnp.float32)
        _g = jnp.sign(_g) * jnp.maximum(jnp.abs(_g), 1.0) + (_g == 0) * 1.0
        g_xattn = _g[0]
        g_ffn = _g[1]
        return (x, ctx_768, g_xattn, g_ffn)
    x, ctx_768, g_xattn, g_ffn = _rec_inputs()

    def _L0_xattn_setup():
        import jax, jax.numpy as jnp
        import numpy as np
        HEADS = 16
        DIM_HEAD = 64
        RANK = 32
        LORA_W = 1.0
        IPA_SCALE = 1.0
        IPA_TOKENS = 4
        SCALE = DIM_HEAD ** (-0.5)

        def _split_heads(t):
            b, n, _ = t.shape
            return t.reshape(b, n, HEADS, DIM_HEAD).transpose(0, 2, 1, 3)

        def _merge_heads(t):
            b, h, n, d = t.shape
            return t.transpose(0, 2, 1, 3).reshape(b, n, h * d)

        def _attention(q_in, k_in, v_in):
            q = _split_heads(q_in)
            k = _split_heads(k_in)
            v = _split_heads(v_in)
            s = jnp.einsum('bhid,bhjd->bhij', q, k) * SCALE
            p = jax.nn.softmax(s, axis=-1)
            o = jnp.einsum('bhij,bhjd->bhid', p, v)
            return _merge_heads(o)

        def _lora(t, down, up, alpha):
            return t @ down @ up * (LORA_W * alpha[0] / RANK)
        key = jax.random.key(seed)
        ks = jax.random.split(key, 20)
        B, N, QD, CD, ID = (8, 512, 128, 96, HEADS * DIM_HEAD)
        CTX = 77 + IPA_TOKENS
        s = 0.02
        return {'x': jax.random.normal(ks[0], (B, N, QD), jnp.float32), 'context': jax.random.normal(ks[1], (B, CTX, CD), jnp.float32), 'Wq': jax.random.normal(ks[2], (QD, ID), jnp.float32) * s, 'Wk': jax.random.normal(ks[3], (CD, ID), jnp.float32) * s, 'Wv': jax.random.normal(ks[4], (CD, ID), jnp.float32) * s, 'Wo': jax.random.normal(ks[5], (ID, QD), jnp.float32) * s, 'bo': jnp.zeros((QD,), jnp.float32), 'q_down': jax.random.normal(ks[6], (QD, RANK), jnp.float32) * s, 'q_up': jax.random.normal(ks[7], (RANK, ID), jnp.float32) * s, 'q_alpha': jnp.ones((1,), jnp.float32) * RANK, 'k_down': jax.random.normal(ks[8], (CD, RANK), jnp.float32) * s, 'k_up': jax.random.normal(ks[9], (RANK, ID), jnp.float32) * s, 'k_alpha': jnp.ones((1,), jnp.float32) * RANK, 'v_down': jax.random.normal(ks[10], (CD, RANK), jnp.float32) * s, 'v_up': jax.random.normal(ks[11], (RANK, ID), jnp.float32) * s, 'v_alpha': jnp.ones((1,), jnp.float32) * RANK, 'o_down': jax.random.normal(ks[12], (ID, RANK), jnp.float32) * s, 'o_up': jax.random.normal(ks[13], (RANK, QD), jnp.float32) * s, 'o_alpha': jnp.ones((1,), jnp.float32) * RANK, 'Wk_ipa': jax.random.normal(ks[14], (CD, ID), jnp.float32) * s, 'Wv_ipa': jax.random.normal(ks[15], (CD, ID), jnp.float32) * s}
    _L0_xattn_all = _L0_xattn_setup()
    _L0_xattn_in = {k: v for k, v in _L0_xattn_all.items() if k in ('Wq', 'Wk', 'Wv', 'Wo', 'bo', 'q_down', 'q_up', 'q_alpha', 'k_down', 'k_up', 'k_alpha', 'v_down', 'v_up', 'v_alpha', 'o_down', 'o_up', 'o_alpha', 'Wk_ipa', 'Wv_ipa')}
    del _L0_xattn_all

    def _L0_ffn_setup():
        import jax, jax.numpy as jnp
        import numpy as np
        B, T, D = (2, 256, 128)
        E, DFF, TOPK = (8, 512, 2)
        TEMPERATURE = 1.0
        key = jax.random.key(seed)
        k_x, k_w1, k_w2, k_r = jax.random.split(key, 4)
        x = jax.random.normal(k_x, (B, T, D), dtype=jnp.float32)
        W1 = jax.random.normal(k_w1, (E, DFF, D), dtype=jnp.float32) * 0.02
        W2 = jax.random.normal(k_w2, (E, D, DFF), dtype=jnp.float32) * 0.02
        Wr = jax.random.normal(k_r, (E, D), dtype=jnp.float32) * 0.02
        return {'x': x, 'W1': W1, 'W2': W2, 'Wr': Wr}
    _L0_ffn_all = _L0_ffn_setup()
    _L0_ffn_in = {k: v for k, v in _L0_ffn_all.items() if k in ('W1', 'W2', 'Wr')}
    del _L0_ffn_all

    def _L1_xattn_setup():
        import jax, jax.numpy as jnp
        import numpy as np
        N_HEADS = 8
        D_EMBED = 128
        D_CROSS = 96
        D_HEAD = D_EMBED // N_HEADS
        key = jax.random.key(seed)
        ks = jax.random.split(key, 10)
        B, SQ, SKV = (8, 512, 77)
        scale_e = 1.0 / np.sqrt(D_EMBED)
        scale_c = 1.0 / np.sqrt(D_CROSS)
        return {'x': jax.random.normal(ks[0], (B, SQ, D_EMBED), dtype=jnp.float32), 'y': jax.random.normal(ks[1], (B, SKV, D_CROSS), dtype=jnp.float32), 'Wq': jax.random.normal(ks[2], (D_EMBED, D_EMBED), dtype=jnp.float32) * scale_e, 'bq': jnp.zeros((D_EMBED,), dtype=jnp.float32), 'Wk': jax.random.normal(ks[3], (D_CROSS, D_EMBED), dtype=jnp.float32) * scale_c, 'bk': jnp.zeros((D_EMBED,), dtype=jnp.float32), 'Wv': jax.random.normal(ks[4], (D_CROSS, D_EMBED), dtype=jnp.float32) * scale_c, 'bv': jnp.zeros((D_EMBED,), dtype=jnp.float32), 'Wo': jax.random.normal(ks[5], (D_EMBED, D_EMBED), dtype=jnp.float32) * scale_e, 'bo': jnp.zeros((D_EMBED,), dtype=jnp.float32)}
    _L1_xattn_all = _L1_xattn_setup()
    _L1_xattn_in = {k: v for k, v in _L1_xattn_all.items() if k in ('Wq', 'bq', 'Wk', 'bk', 'Wv', 'bv', 'Wo', 'bo')}
    del _L1_xattn_all

    def _L1_ffn_setup():
        import jax, jax.numpy as jnp
        import numpy as np
        NUM_NOD = 6
        MAX_PREV = 5
        NUM_EDGE = 20
        D = 128
        H = 8
        LN_EPS = 1e-06

        def _layernorm(x, g, b):
            mu = jnp.mean(x, axis=-1, keepdims=True)
            var = jnp.mean(jnp.square(x - mu), axis=-1, keepdims=True)
            return (x - mu) * jax.lax.rsqrt(var + LN_EPS) * g + b

        def _mha(q, k, v, wq, wk, wv, wo):
            B, S, d = q.shape
            dh = d // H
            qh = (q @ wq).reshape(B, S, H, dh)
            kh = (k @ wk).reshape(B, S, H, dh)
            vh = (v @ wv).reshape(B, S, H, dh)
            scores = jnp.einsum('bqhd,bkhd->bhqk', qh, kh) / jnp.sqrt(jnp.asarray(dh, q.dtype))
            attn = jax.nn.softmax(scores, axis=-1)
            ctx = jnp.einsum('bhqk,bkhd->bqhd', attn, vh).reshape(B, S, d)
            return ctx @ wo
        key = jax.random.key(seed)
        ks = jax.random.split(key, 12)
        B, S = (8, 128)
        scale = 1.0 / np.sqrt(D)
        return {'inputs': jax.random.normal(ks[0], (B, S, D), jnp.float32), 'ew': jax.random.uniform(ks[1], (NUM_NOD, 3), jnp.float32), 'act_w': jax.random.uniform(ks[2], (NUM_NOD,), jnp.float32), 'We': jax.random.normal(ks[3], (NUM_EDGE, D, D), jnp.float32) * scale, 'be': jnp.zeros((NUM_EDGE, D), jnp.float32), 'Wq': jax.random.normal(ks[4], (NUM_NOD, D, D), jnp.float32) * scale, 'Wk': jax.random.normal(ks[5], (NUM_NOD, D, D), jnp.float32) * scale, 'Wv': jax.random.normal(ks[6], (NUM_NOD, D, D), jnp.float32) * scale, 'Wo': jax.random.normal(ks[7], (NUM_NOD, D, D), jnp.float32) * scale, 'ln_g': jnp.ones((D,), jnp.float32), 'ln_b': jnp.zeros((D,), jnp.float32)}
    _L1_ffn_all = _L1_ffn_setup()
    _L1_ffn_in = {k: v for k, v in _L1_ffn_all.items() if k in ('ew', 'act_w', 'We', 'be', 'Wq', 'Wk', 'Wv', 'Wo', 'ln_g', 'ln_b')}
    del _L1_ffn_all
    return {'x': x, 'ctx_768': ctx_768, 'g_xattn': g_xattn, 'g_ffn': g_ffn, 'L0_xattn_Wq': _L0_xattn_in['Wq'], 'L0_xattn_Wk': _L0_xattn_in['Wk'], 'L0_xattn_Wv': _L0_xattn_in['Wv'], 'L0_xattn_Wo': _L0_xattn_in['Wo'], 'L0_xattn_bo': _L0_xattn_in['bo'], 'L0_xattn_q_down': _L0_xattn_in['q_down'], 'L0_xattn_q_up': _L0_xattn_in['q_up'], 'L0_xattn_q_alpha': _L0_xattn_in['q_alpha'], 'L0_xattn_k_down': _L0_xattn_in['k_down'], 'L0_xattn_k_up': _L0_xattn_in['k_up'], 'L0_xattn_k_alpha': _L0_xattn_in['k_alpha'], 'L0_xattn_v_down': _L0_xattn_in['v_down'], 'L0_xattn_v_up': _L0_xattn_in['v_up'], 'L0_xattn_v_alpha': _L0_xattn_in['v_alpha'], 'L0_xattn_o_down': _L0_xattn_in['o_down'], 'L0_xattn_o_up': _L0_xattn_in['o_up'], 'L0_xattn_o_alpha': _L0_xattn_in['o_alpha'], 'L0_xattn_Wk_ipa': _L0_xattn_in['Wk_ipa'], 'L0_xattn_Wv_ipa': _L0_xattn_in['Wv_ipa'], 'L0_ffn_W1': _L0_ffn_in['W1'], 'L0_ffn_W2': _L0_ffn_in['W2'], 'L0_ffn_Wr': _L0_ffn_in['Wr'], 'L1_xattn_Wq': _L1_xattn_in['Wq'], 'L1_xattn_bq': _L1_xattn_in['bq'], 'L1_xattn_Wk': _L1_xattn_in['Wk'], 'L1_xattn_bk': _L1_xattn_in['bk'], 'L1_xattn_Wv': _L1_xattn_in['Wv'], 'L1_xattn_bv': _L1_xattn_in['bv'], 'L1_xattn_Wo': _L1_xattn_in['Wo'], 'L1_xattn_bo': _L1_xattn_in['bo'], 'L1_ffn_ew': _L1_ffn_in['ew'], 'L1_ffn_act_w': _L1_ffn_in['act_w'], 'L1_ffn_We': _L1_ffn_in['We'], 'L1_ffn_be': _L1_ffn_in['be'], 'L1_ffn_Wq': _L1_ffn_in['Wq'], 'L1_ffn_Wk': _L1_ffn_in['Wk'], 'L1_ffn_Wv': _L1_ffn_in['Wv'], 'L1_ffn_Wo': _L1_ffn_in['Wo'], 'L1_ffn_ln_g': _L1_ffn_in['ln_g'], 'L1_ffn_ln_b': _L1_ffn_in['ln_b']}

def reference(x, ctx_768, g_xattn, g_ffn, L0_xattn_Wq, L0_xattn_Wk, L0_xattn_Wv, L0_xattn_Wo, L0_xattn_bo, L0_xattn_q_down, L0_xattn_q_up, L0_xattn_q_alpha, L0_xattn_k_down, L0_xattn_k_up, L0_xattn_k_alpha, L0_xattn_v_down, L0_xattn_v_up, L0_xattn_v_alpha, L0_xattn_o_down, L0_xattn_o_up, L0_xattn_o_alpha, L0_xattn_Wk_ipa, L0_xattn_Wv_ipa, L0_ffn_W1, L0_ffn_W2, L0_ffn_Wr, L1_xattn_Wq, L1_xattn_bq, L1_xattn_Wk, L1_xattn_bk, L1_xattn_Wv, L1_xattn_bv, L1_xattn_Wo, L1_xattn_bo, L1_ffn_ew, L1_ffn_act_w, L1_ffn_We, L1_ffn_be, L1_ffn_Wq, L1_ffn_Wk, L1_ffn_Wv, L1_ffn_Wo, L1_ffn_ln_g, L1_ffn_ln_b):
    import jax
    import jax.numpy as jnp

    def _L0_xattn_ref(x, context, Wq, Wk, Wv, Wo, bo, q_down, q_up, q_alpha, k_down, k_up, k_alpha, v_down, v_up, v_alpha, o_down, o_up, o_alpha, Wk_ipa, Wv_ipa):
        import jax, jax.numpy as jnp
        import numpy as np
        HEADS = 16
        DIM_HEAD = 64
        RANK = 32
        LORA_W = 1.0
        IPA_SCALE = 1.0
        IPA_TOKENS = 4
        SCALE = DIM_HEAD ** (-0.5)

        def _split_heads(t):
            b, n, _ = t.shape
            return t.reshape(b, n, HEADS, DIM_HEAD).transpose(0, 2, 1, 3)

        def _merge_heads(t):
            b, h, n, d = t.shape
            return t.transpose(0, 2, 1, 3).reshape(b, n, h * d)

        def _attention(q_in, k_in, v_in):
            q = _split_heads(q_in)
            k = _split_heads(k_in)
            v = _split_heads(v_in)
            s = jnp.einsum('bhid,bhjd->bhij', q, k) * SCALE
            p = jax.nn.softmax(s, axis=-1)
            o = jnp.einsum('bhij,bhjd->bhid', p, v)
            return _merge_heads(o)

        def _lora(t, down, up, alpha):
            return t @ down @ up * (LORA_W * alpha[0] / RANK)
        q_in = x @ Wq + _lora(x, q_down, q_up, q_alpha)
        end = context.shape[1] - IPA_TOKENS
        org_ctx = context[:, :end, :]
        ipa_ctx = context[:, end:, :]
        k_in = org_ctx @ Wk + _lora(org_ctx, k_down, k_up, k_alpha)
        v_in = org_ctx @ Wv + _lora(org_ctx, v_down, v_up, v_alpha)
        out = _attention(q_in, k_in, v_in)
        ipa_k = ipa_ctx @ Wk_ipa
        ipa_v = ipa_ctx @ Wv_ipa
        out_ipa = _attention(q_in, ipa_k, ipa_v)
        out = out + IPA_SCALE * out_ipa
        return out @ Wo + bo + _lora(out, o_down, o_up, o_alpha)

    def _L0_ffn_ref(x, W1, W2, Wr):
        import jax, jax.numpy as jnp
        import numpy as np
        B, T, D = (2, 256, 128)
        E, DFF, TOPK = (8, 512, 2)
        TEMPERATURE = 1.0
        logits = jnp.einsum('btd,ed->bte', x, Wr)
        probs = jax.nn.softmax(logits / TEMPERATURE, axis=-1)
        topk_vals, topk_idx = jax.lax.top_k(probs, TOPK)
        router_weights = topk_vals / topk_vals.sum(-1, keepdims=True)
        one_hot = jax.nn.one_hot(topk_idx, E, dtype=x.dtype)
        gate = jnp.einsum('btk,btke->bte', router_weights, one_hot)
        h = jax.nn.silu(jnp.einsum('btd,efd->btef', x, W1))
        y = jnp.einsum('btef,edf->bted', h, W2)
        out = jnp.einsum('bte,bted->btd', gate, y)
        return out

    def _L1_xattn_ref(x, y, Wq, bq, Wk, bk, Wv, bv, Wo, bo):
        import jax, jax.numpy as jnp
        import numpy as np
        N_HEADS = 8
        D_EMBED = 128
        D_CROSS = 96
        D_HEAD = D_EMBED // N_HEADS
        B, SQ, _ = x.shape
        q = x @ Wq + bq
        k = y @ Wk + bk
        v = y @ Wv + bv
        q = q.reshape(B, SQ, N_HEADS, D_HEAD).transpose(0, 2, 1, 3)
        k = k.reshape(B, -1, N_HEADS, D_HEAD).transpose(0, 2, 1, 3)
        v = v.reshape(B, -1, N_HEADS, D_HEAD).transpose(0, 2, 1, 3)
        scale = 1.0 / jnp.sqrt(jnp.asarray(D_HEAD, dtype=q.dtype))
        weight = jnp.einsum('bhqd,bhkd->bhqk', q, k) * scale
        weight = jax.nn.softmax(weight, axis=-1)
        out = jnp.einsum('bhqk,bhkd->bhqd', weight, v)
        out = out.transpose(0, 2, 1, 3).reshape(B, SQ, D_EMBED)
        return out @ Wo + bo

    def _L1_ffn_ref(inputs, ew, act_w, We, be, Wq, Wk, Wv, Wo, ln_g, ln_b):
        import jax, jax.numpy as jnp
        import numpy as np
        NUM_NOD = 6
        MAX_PREV = 5
        NUM_EDGE = 20
        D = 128
        H = 8
        LN_EPS = 1e-06

        def _layernorm(x, g, b):
            mu = jnp.mean(x, axis=-1, keepdims=True)
            var = jnp.mean(jnp.square(x - mu), axis=-1, keepdims=True)
            return (x - mu) * jax.lax.rsqrt(var + LN_EPS) * g + b

        def _mha(q, k, v, wq, wk, wv, wo):
            B, S, d = q.shape
            dh = d // H
            qh = (q @ wq).reshape(B, S, H, dh)
            kh = (k @ wk).reshape(B, S, H, dh)
            vh = (v @ wv).reshape(B, S, H, dh)
            scores = jnp.einsum('bqhd,bkhd->bhqk', qh, kh) / jnp.sqrt(jnp.asarray(dh, q.dtype))
            attn = jax.nn.softmax(scores, axis=-1)
            ctx = jnp.einsum('bhqk,bkhd->bqhd', attn, vh).reshape(B, S, d)
            return ctx @ wo
        nodes = {-1: inputs}
        lind = 0
        for c in range(NUM_NOD):
            nsrc = min(c + 1, MAX_PREV)
            snode = c - nsrc
            eq, ek, ev = (lind + nsrc - 1, lind, lind + nsrc // 2)
            in_q, in_k, in_v = (c - 1, snode, snode + nsrc // 2)
            q = ew[c, 0] * (nodes[in_q] @ We[eq] + be[eq])
            k = ew[c, 1] * (nodes[in_k] @ We[ek] + be[ek])
            v = ew[c, 2] * (nodes[in_v] @ We[ev] + be[ev])
            o = _mha(q, k, v, Wq[c], Wk[c], Wv[c], Wo[c])
            nodes[c] = act_w[c] * o + q
            lind += nsrc
        out = nodes[NUM_NOD - 1]
        return _layernorm(out, ln_g, ln_b)
    x = x + jnp.tanh(g_xattn[0]) * _L0_xattn_ref(_layernorm(x, axis=-1), ctx_768, L0_xattn_Wq, L0_xattn_Wk, L0_xattn_Wv, L0_xattn_Wo, L0_xattn_bo, L0_xattn_q_down, L0_xattn_q_up, L0_xattn_q_alpha, L0_xattn_k_down, L0_xattn_k_up, L0_xattn_k_alpha, L0_xattn_v_down, L0_xattn_v_up, L0_xattn_v_alpha, L0_xattn_o_down, L0_xattn_o_up, L0_xattn_o_alpha, L0_xattn_Wk_ipa, L0_xattn_Wv_ipa)
    x = x + jnp.tanh(g_ffn[0]) * _L0_ffn_ref(_layernorm(x, axis=-1), L0_ffn_W1, L0_ffn_W2, L0_ffn_Wr)
    x = x + jnp.tanh(g_xattn[1]) * _L1_xattn_ref(_layernorm(x, axis=-1), ctx_768, L1_xattn_Wq, L1_xattn_bq, L1_xattn_Wk, L1_xattn_bk, L1_xattn_Wv, L1_xattn_bv, L1_xattn_Wo, L1_xattn_bo)
    x = x + jnp.tanh(g_ffn[1]) * _L1_ffn_ref(_layernorm(x, axis=-1), L1_ffn_ew, L1_ffn_act_w, L1_ffn_We, L1_ffn_be, L1_ffn_Wq, L1_ffn_Wk, L1_ffn_Wv, L1_ffn_Wo, L1_ffn_ln_g, L1_ffn_ln_b)
    return x

_drawn_inputs = setup_inputs


def setup_inputs(seed=0):
    import zlib

    import numpy as np

    out = dict(_drawn_inputs(seed))
    spreads = {'g_ffn': (-1.0, 0.6),
     'L0_xattn_bo': (0.0, 0.535),
     'L1_xattn_bq': (0.0, 2.0),
     'L1_xattn_bk': (0.0, 2.0),
     'L1_xattn_bv': (0.0, 0.451),
     'L1_xattn_bo': (0.0, 0.454),
     'L1_ffn_be': (0.0, 0.1),
     'L1_ffn_ln_g': (1.0, 0.2),
     'L1_ffn_ln_b': (0.0, 0.489)}
    factors = {'L0_xattn_Wq': 8.0,
     'L0_xattn_Wk': 8.0,
     'L0_xattn_q_down': 8.0,
     'L0_xattn_q_up': 8.0,
     'L0_xattn_k_down': 8.0,
     'L0_xattn_k_up': 8.0,
     'L0_xattn_v_down': 8.0,
     'L0_xattn_v_up': 8.0,
     'L0_xattn_o_down': 8.0,
     'L0_xattn_o_up': 7.519,
     'L0_xattn_Wk_ipa': 8.0,
     'L0_ffn_W1': 9.926,
     'L0_ffn_Wr': 12.725,
     'L1_ffn_Wq': 200.0,
     'L1_ffn_Wk': 200.0,
     'L0_ffn_W2': 3.492}
    for name, (base, spread) in spreads.items():
        noise = np.random.default_rng([zlib.crc32(name.encode()), seed]).standard_normal(out[name].shape)
        drawn = base * np.exp(spread * noise) if base else spread * noise
        out[name] = jnp.asarray(drawn.astype(out[name].dtype))
    for name, factor in factors.items():
        out[name] = (out[name] * factor).astype(out[name].dtype)
    return out
```

```python
from contextlib import ExitStack

import numpy as np
import concourse.bass as bass
from concourse import mybir

ALU = mybir.AluOpType
ACT = mybir.ActivationFunctionType
AX = mybir.AxisListType
F32 = mybir.dt.float32
F32R = mybir.dt.float32r
U32 = mybir.dt.uint32

B, N, D, S, CD = 8, 256, 128, 512, 96
TT = N // 128
IPA = 4
SM = S - IPA
H0, DH0 = 16, 64
ID0 = H0 * DH0
PAIRS = H0 // 2
H1, DH1 = 8, 16
KT = S // 128
SCALE0, SCALE1 = DH0 ** -0.5, DH1 ** -0.5
RANK = 32
E, DFF = 8, 512
NODES, MAX_PREV = 6, 5
GH = 4
LNS = 4
EPS_LN, EPS_OUT = 1e-5, 1e-6

C_GX, C_GF, C_QA, C_KA, C_VA, C_OA = 0, 2, 4, 5, 6, 7
C_EW, C_AW = 8, 26
C_BQ, C_BK, C_BV = 32, 33, 34
C_BE = 35
C_WR = 56
C_BO0, C_BO1, C_LG, C_LB = 64, 192, 320, 448
C_ALL = 576


def edges():
    out, lind = [], 0
    for c in range(NODES):
        nsrc = min(c + 1, MAX_PREV)
        s = c - nsrc
        out.append(((lind + nsrc - 1, lind, lind + nsrc // 2), (c, s + 1, s + nsrc // 2 + 1)))
        lind += nsrc
    return out


def at(turn, per_turn, k):
    return k if turn is None else turn * per_turn + k


def wait_apart(eng, tally, sem, value):
    eng.wait_ge(sem, value)
    eng.sem_inc(tally, 1)


def node_schedule():
    out = [("proj", 0, 0), ("proj", 1, 0), ("max", 0, 0)]
    for c in range(NODES):
        out += [("attend", 0, c), ("max", 1, c), ("node", 0, c)]
        if c + 1 < NODES:
            out += [("proj", 0, c + 1)]
        out += [("attend", 1, c)]
        if c + 1 < NODES:
            out += [("max", 0, c + 1)]
        out += [("node", 1, c)]
        if c + 1 < NODES:
            out += [("proj", 1, c + 1)]
    return out


ORDER8 = (0, 2, 4, 6, 1, 3, 5, 7)


def build(nc, T, out):
    EDGES = edges()
    ctx = ExitStack()
    with ctx:
        def sb(name, shape, dt=F32, stack=ctx):
            return stack.enter_context(nc.sbuf_tensor(name, shape, dt))

        def sem(name):
            return ctx.enter_context(nc.semaphore(name))

        def dram(name, shape):
            return nc.dram_tensor(name, shape, F32, kind="Internal").ap()

        ps = ctx.enter_context(nc.psum_tensor("ps", [128, 8, 512], F32))

        vw_dram = dram("vw_dram", (B, H0 * IPA, D))
        qx_dram = dram("qx_dram", (128, 2, N))
        kx_dram = dram("kx_dram", (128, 2, S))
        qk_dram = [dram(f"qk_dram{r}", (128, 2, 2, N)) for r in range(2)]

        cst = sb("cst", [128, C_ALL])
        ident = sb("ident", [128, 128])
        x_all = sb("x_all", [128, B * TT, D])
        x3T_all = sb("x3T_all", [128, B, N])
        tanh_g = sb("tanh_g", [128, 4])
        sel8 = sb("sel8", [64, H1, 128], F32R)
        sumsel = sb("sumsel", [128, 2, 32])
        sel8f = sb("sel8f", [64, H1, 128])
        ones = sb("ones", [128, 128])
        pow_c = sb("pow_c", [128, 2])
        gb = sb("gb", [128, 2, D])
        mv = sb("mv", [128, TT, 2])
        st6 = sb("st6", [128, TT, 6])
        rstd = sb("rstd", [128, TT])
        var_e = sb("var_e", [128, TT])

        w_in = sem("w_in")
        apart_tally = sem("apart_tally")
        w_moe_in = sem("w_moe_in")
        w_b_in = sem("w_b_in")
        pool_const = sem("pool_const")
        dve_const = sem("dve_const")
        dve_chain = sem("dve_chain")
        act_chain = sem("act_chain")
        pool_chain = sem("pool_chain")
        gates_tanh = sem("gates_tanh")
        fold_psum = sem("fold_psum")
        fold_done = sem("fold_done")
        vw_out = sem("vw_out")
        ctx_in = sem("ctx_in")
        ctx_used = sem("ctx_used")
        ln_var = sem("ln_var")
        ln_rstd = sem("ln_rstd")
        xn_ready = sem("xn_ready")
        xnT_psum = sem("xnT_psum")
        xnT_ready = sem("xnT_ready")
        fill_full = sem("fill_full")
        hi_done = sem("hi_done")
        lo_done = sem("lo_done")
        max_full = sem("max_full")
        max_done = sem("max_done")
        nm_parts = sem("nm_parts")
        nmT_psum = sem("nmT_psum")
        nmT_ready = sem("nmT_ready")
        score_full = sem("score_full")
        probs_ready = sem("probs_ready")
        pv_head = sem("pv_head")
        pair_out = sem("pair_out")
        ipa_scores = sem("ipa_scores")
        ipa_shifted = sem("ipa_shifted")
        ipa_exp = sem("ipa_exp")
        ipa_probs = sem("ipa_probs")
        ipa_T = sem("ipa_T")
        ipa_ready = sem("ipa_ready")
        y_full = sem("y_full")
        logits_full = sem("logits_full")
        gap_ready = sem("gap_ready")
        gap_exp = sem("gap_exp")
        h_full = sem("h_full")
        tanh_done = sem("tanh_done")
        hs_ready = sem("hs_ready")
        w2_done = sem("w2_done")
        ye_full = sem("ye_full")
        x_proj = sem("x_proj")
        x_hi = sem("x_hi")
        x_lo = sem("x_lo")
        x_v = sem("x_v")
        x_parts_out = sem("x_parts_out")
        x_stacks_in = sem("x_stacks_in")
        x_max_full = sem("x_max_full")
        x_max_done = sem("x_max_done")
        x_nm_parts = sem("x_nm_parts")
        x_nmT_psum = sem("x_nmT_psum")
        x_nmT_ready = sem("x_nmT_ready")
        x_score_full = sem("x_score_full")
        x_probs_ready = sem("x_probs_ready")
        x_pv = sem("x_pv")
        x_ctxo = sem("x_ctxo")
        x_y = sem("x_y")
        x3_ready = sem("x3_ready")
        x3T_psum = sem("x3T_psum")
        x3T_done = sem("x3T_done")
        loop_a_done = sem("loop_a_done")
        fb_psum = sem("fb_psum")
        fb_done = sem("fb_done")
        b_node0 = sem("b_node0")
        two = lambda name: [sem(f"{name}_{r}") for r in range(2)]
        n_proj, n_hi, n_lo, n_v = two("n_proj"), two("n_hi"), two("n_lo"), two("n_v")
        n_v_full = two("n_v_full")
        n_parts_out, n_stacks_in = two("n_parts_out"), two("n_stacks_in")
        n_max_full, n_max_done = two("n_max_full"), two("n_max_done")
        n_nm_parts, n_nmT_psum, n_nmT_ready = two("n_nm_parts"), two("n_nmT_psum"), two("n_nmT_ready")
        n_score_full, n_probs = two("n_score_full"), two("n_probs")
        n_pv, n_ctxo, n_wo, n_node = two("n_pv"), two("n_ctxo"), two("n_wo"), two("n_node")
        n_last_T, n_var, n_rstd, n_out, n_stored = two("n_last_T"), two("n_var"), two("n_rstd"), two("n_out"), two("n_stored")

        sa = ExitStack()
        wq = sb("wq", [128, ID0], stack=sa)
        wk = sb("wk", [96, ID0], stack=sa)
        wv = sb("wv", [96, ID0], stack=sa)
        wo = sb("wo", [128, PAIRS, D], stack=sa)
        w1T = sb("w1T", [128, E * DFF], stack=sa)
        w2T = sb("w2T", [128, E * DFF // 128, D], stack=sa)
        xw = sb("xw", [128, 4, D], stack=sa)
        q12 = sb("q12", [128, 2, PAIRS, N], F32R, stack=sa)
        k12 = sb("k12", [128, 2, PAIRS, S], F32R, stack=sa)
        v0 = sb("v0", [128, KT, ID0], stack=sa)
        probs = sb("probs", [128, 2, KT * N], stack=sa)
        outT = sb("outT", [128, PAIRS, N], stack=sa)
        g_ipa = sb("g_ipa", [128, B, H0 * IPA], stack=sa)
        vw = sb("vw", [64, D], stack=sa)
        ctxT = sb("ctxT", [96, S], stack=sa)
        ctx0 = sb("ctx0", [96, S], stack=sa)
        xn = sb("xn", [128, TT, D], stack=sa)
        xnT = sb("xnT", [128, N], stack=sa)
        nm = sb("nm", [128, TT, H0], stack=sa)
        mxs = sb("mxs", [128, TT, 128], F32R, stack=sa)
        nmT = sb("nmT", [128, N], F32R, stack=sa)
        sel4f = sb("sel4f", [128, GH, 128], stack=sa)
        sel4 = sb("sel4", [128, GH, 128], F32R, stack=sa)
        rsum = sb("rsum", [128, N], stack=sa)
        pi = sb("pi", [128, TT, H0 * IPA], stack=sa)
        pis = sb("pis", [128, 2, TT * H0], stack=sa)
        piT = sb("piT", [64, N], stack=sa)
        xs = sb("xs", [128, TT, D], stack=sa)
        lg = sb("lg", [128, TT, E], stack=sa)
        top = sb("top", [128, TT, 8], stack=sa)
        topi = sb("topi", [128, TT, 8], U32, stack=sa)
        topf = sb("topf", [128, TT, 8], stack=sa)
        iota8 = sb("iota8", [128, E], stack=sa)
        gw = sb("gw", [128, 6, TT], stack=sa)
        gate = sb("gate", [128, TT, E], stack=sa)
        gate2 = sb("gate2", [128, TT, E], stack=sa)
        th = sb("th", [128, 2, 2 * N], stack=sa)
        hs = sb("hs", [128, 3, 2, N], stack=sa)
        vpx = sb("vpx", [128, KT, H1, 32], stack=sa)
        qx12 = sb("qx12", [128, 2, N], F32R, stack=sa)
        kx12 = sb("kx12", [128, 2, S], F32R, stack=sa)
        xrow = sb("xrow", [128, D], stack=sa)
        boT = sb("boT", [128, D], stack=sa)
        tmp128 = sb("tmp128", [128, D], stack=sa)
        wki = v0[0:96, 0, :]
        wvi = v0[0:96, 1, :]
        up = v0[0:32, 2, :]
        kup = v0[0:32, 3, :]
        vup = probs[0:32, 0, :]
        odT = probs[0:32, 1, :]
        smallw = outT[0:32, 0:3, :].rearrange("p a b -> p (a b)")
        kblk = x3T_all[:, 0:2, :].rearrange("p a b -> p (a b)").rearrange("p (j s c) -> p j s c", s=2, j=PAIRS)
        vblk = x3T_all[:, 2:4, :].rearrange("p a b -> p (a b)").rearrange("p (j s c) -> p j s c", s=2, j=PAIRS)
        wqT = x3T_all[:, 4:8, :].rearrange("p a b -> p (a b)").rearrange("p (j c) -> p j c", j=PAIRS)
        ctx_ipa = xnT[0:96, 0:32]
        vwsb = hs[0:64, 0:2, :, :].rearrange("p a b c -> p (a b c)").rearrange("p (j d) -> p j d", j=PAIRS)
        qst = q12[0:64, 1, :, :]
        kst = k12[0:64, 1, :, :]

        def place_b():
            sa.close()
            sb_ = ExitStack()
            ctx.enter_context(sb_)
            t = {}
            def s2(name, shape, dt=F32):
                t[name] = [sb(f"{name}{r}", shape, dt, stack=sb_) for r in range(2)]
            t["raw"] = sb("raw_b", [128, NODES, 8, D], stack=sb_)
            t["fw"] = sb("fw", [128, NODES, 5, D], stack=sb_)
            t["fb"] = sb("fb", [128, NODES, 5], stack=sb_)
            s2("nodes", [128, NODES + 1, N])
            s2("qk12", [128, 2, 2, N], F32R)
            s2("bqst", [64, H1, N], F32R)
            s2("bkst", [64, H1, N], F32R)
            s2("vpad", [128, TT, H1, 32])
            s2("qn", [128, N])
            s2("bprobs", [128, H1, TT * N])
            s2("bnm", [128, TT, H1])
            s2("bmxs", [128, TT, 64], F32R)
            s2("bnmT", [64, N], F32R)
            s2("brs", [128, N])
            s2("bctx", [128, N])
            s2("o", [128, TT, D])
            s2("bmv", [128, TT, 2])
            s2("bst", [128, TT, 6])
            s2("brstd", [128, TT])
            s2("bvar", [128, TT])
            return t

        TB = place_b()
        assert TB is not None

        CH_DVE_A = 44
        block = ctx.enter_context(nc.Block())

        N_W, N_MOE, N_B = 22, 2, 8 * NODES

        @block.sync
        def _(sp):
            for dst, src in (
                (cst[:], T["cst"]), (x_all[:, :, :], T["x"].rearrange("b (t p) d -> p (b t) d", p=128)),
                (smallw[:, 0:128], T["q_downT"]), (up, T["q_up"]), (wq[:], T["Wq"]),
                (smallw[:, 128:224], T["k_downT"]), (kup, T["k_up"]), (wk[:], T["Wk"]),
                (smallw[:, 224:320], T["v_downT"]), (vup, T["v_up"]), (wv[:], T["Wv"]),
                (smallw[:, 320:448], T["o_up"]), (odT, T["o_downT"]),
                (wo[:, :, :], T["Wo"].rearrange("(j p) d -> p j d", p=128)),
                (wki, T["Wk_ipa"]), (wvi, T["Wv_ipa"]), (ctx_ipa, T["ctx_ipaT"]),
                (xw[:, 0, :], T["xWq"]), (xw[0:96, 1, :], T["xWk"]), (xw[0:96, 2, :], T["xWv"]),
                (xw[:, 3, :], T["xWo"]), (ident[:], T["ident"]),
            ):
                sp.dma_start(dst, src).then_inc(w_in, 16)

            def load_ctx(b):
                src = T["ctxT"][bass.ds(b, 1)].rearrange("a c s -> (a c) s")
                sp.dma_start(ctxT[:], src).then_inc(ctx_in, 16)
                sp.dma_start(ctx0[:, 0:SM], src[:, 0:SM]).then_inc(ctx_in, 16)
                sp.dma_start(ctx0[:, SM:S], src[:, SM - IPA:SM]).then_inc(ctx_in, 16)
                sp.dma_start(vw[:], vw_dram[bass.ds(b, 1)].rearrange("a c s -> (a c) s")).then_inc(ctx_in, 16)

            sp.dma_start(w1T[:], T["W1T"]).then_inc(w_moe_in, 16)
            sp.dma_start(w2T[:, :, :], T["W2T"].rearrange("(c p) d -> p c d", p=128)).then_inc(w_moe_in, 16)
            sp.wait_ge(fold_done, 15)
            for s in range(2):
                sp.dma_start(vw_dram.rearrange("b (t j s) d -> s (b t) j d", s=2, t=IPA)[s],
                             vwsb[32 * s:32 * s + 32, :, :]).then_inc(vw_out, 16)
            sp.wait_ge(vw_out, 32)
            load_ctx(0)

            def bounce(i, last):
                sp.wait_ge(x_lo, at(i, 2, 2))
                sp.dma_start(qx_dram, qx12[:, :, :].bitcast(F32)).then_inc(x_parts_out, 16)
                sp.dma_start(kx_dram, kx12[:, :, :].bitcast(F32)).then_inc(x_parts_out, 16)
                sp.wait_ge(x_parts_out, at(i, 32, 32))
                for s in range(2):
                    for r in range(2):
                        sp.dma_start(qst[32 * s + 16 * r:32 * s + 16 * r + 16].bitcast(F32),
                                     qx_dram[:, s].rearrange("(h d) q -> d h q", h=H1)).then_inc(x_stacks_in, 16)
                        sp.dma_start(kst[32 * r + 16 * s:32 * r + 16 * s + 16].bitcast(F32),
                                     kx_dram[:, s].rearrange("(h d) q -> d h q", h=H1)).then_inc(x_stacks_in, 16)

            with sp.Fori(0, B - 1) as i:
                bounce(i, False)
                sp.wait_ge(ctx_used, at(i, 1, 1))
                load_ctx(i + 1)
            bounce(B - 1, True)

            sp.wait_ge(loop_a_done, 3)
            raw = TB["raw"]
            for c, ((eq, ek, ev), _src) in enumerate(EDGES):
                for n, src in enumerate((T["WeT"][eq], T["WeT"][ek], T["WeT"][ev], T["We"][eq],
                                         T["bWq"][c], T["bWk"][c], T["bWv"][c], T["bWo"][c])):
                    sp.dma_start(raw[:, c, n, :], src).then_inc(w_b_in, 16)

            with sp.Fori(0, B // 2) as i:
                for stage, r, c in node_schedule():
                    if stage != "proj":
                        continue
                    sp.wait_ge(n_lo[r], at(i, NODES, c + 1))
                    sp.dma_start(qk_dram[r], TB["qk12"][r][:, :, :, :].bitcast(F32)).then_inc(n_parts_out[r], 16)
                    sp.wait_ge(n_parts_out[r], at(i, 16 * NODES, 16 * (c + 1)))
                    for s in range(2):
                        for k in range(2):
                            sp.dma_start(TB["bqst"][r][32 * s + 16 * k:32 * s + 16 * k + 16].bitcast(F32),
                                         qk_dram[r][:, s, 0].rearrange("(h d) q -> d h q", h=H1)).then_inc(n_stacks_in[r], 16)
                            sp.dma_start(TB["bkst"][r][32 * k + 16 * s:32 * k + 16 * s + 16].bitcast(F32),
                                         qk_dram[r][:, s, 1].rearrange("(h d) q -> d h q", h=H1)).then_inc(n_stacks_in[r], 16)
                for r in range(2):
                    sp.wait_ge(n_out[r], at(i, 1, 1))
                    sp.dma_start(out[bass.ds(2 * i + r, 1)].rearrange("a (t p) d -> p (a t) d", p=128),
                                 TB["o"][r][:, :, :]).then_inc(n_stored[r], 16)
            for r in range(2):
                sp.wait_ge(n_stored[r], 16 * (B // 2))

        @block.gpsimd
        def _(pool):
            g = nc.gpsimd
            g.memset(mxs[:, :, :].bitcast(F32), 0.0)
            g.memset(vpx[:, :, :, :], 0.0)
            g.memset(ones[:], 1.0)
            g.memset(sumsel[:, :, :], 0.0)
            g.memset(pow_c[:], -0.5)
            g.memset(sel4f[:, :, :], 0.0)
            g.memset(sel8f[:, :, :], 0.0)
            g.iota(topi[:, 0, :], [[1, E]], base=0, channel_multiplier=0).then_inc(pool_const, 1)
            pool.wait_ge(pool_const, 1)
            g.tensor_copy(iota8[:], topi[:, 0, :])
            g.memset(sumsel[:, 0, 0:16], 1.0)
            g.memset(sumsel[:, 1, 16:32], 1.0)
            for base in (0, 32, 64, 96):
                last = g.affine_select(out=sel4f[:, :, :], in_=sel4f[:, :, :], compare_op=ALU.not_equal, fill=1.0,
                                       base=-base, pattern=[[-1, GH], [0, 128]], channel_multiplier=1)
                last.then_inc(pool_chain, 1)
                pool.wait_ge(pool_chain, base // 32 + 1)
            for n, base in enumerate((0, 32)):
                last = g.affine_select(out=sel8f[:, :, :], in_=sel8f[:, :, :], compare_op=ALU.not_equal, fill=1.0,
                                       base=-base, pattern=[[-1, H1], [0, 128]], channel_multiplier=1)
                last.then_inc(pool_chain, 1)
                pool.wait_ge(pool_chain, 5 + n)
            g.tensor_copy(sel8[:, :, :], sel8f[:, :, :])
            g.tensor_copy(sel4[:, :, :], sel4f[:, :, :]).then_inc(pool_const, 1)

            with pool.Fori(0, B) as i:
                for l in range(LNS):
                    wait_apart(pool, apart_tally, ln_var, at(i, LNS, l + 1))
                    g.tensor_scalar(var_e[:], mv[:, :, 1], EPS_LN, None, ALU.add).then_inc(pool_chain, 1)
                    pool.wait_ge(pool_chain, at(i, LNS, 6 + l + 1))
                    g.tensor_tensor(rstd[:], var_e[:], pow_c[:], ALU.pow).then_inc(ln_rstd, 1)
            pool.wait_ge(loop_a_done, 3)
            for r in range(2):
                g.memset(TB["bmxs"][r][:, :, :].bitcast(F32), 0.0)
                last = g.memset(TB["vpad"][r][:, :, :, :], 0.0)
            last.then_inc(pool_const, 1)
            with pool.Fori(0, B // 2) as i:
                for r in range(2):
                    wait_apart(pool, apart_tally, n_var[r], at(i, 1, 1))
                    g.tensor_scalar(TB["bvar"][r][:], TB["bmv"][r][:, :, 1], EPS_OUT, None, ALU.add).then_inc(pool_chain, 1)
                    pool.wait_ge(pool_chain, at(i, 2, 6 + LNS * B + r + 1))
                    g.tensor_tensor(TB["brstd"][r][:], TB["bvar"][r][:], pow_c[:], ALU.pow).then_inc(n_rstd[r], 1)

        @block.tensor
        def _(pe):
            mm = pe.matmul
            pe.wait_ge(w_in, 16 * N_W)
            pe.wait_ge(pool_const, 2)
            for h in range(2):
                mm(ps[:, h, :], smallw[:, 0:128], up[:, 512 * h:512 * h + 512], start=True, stop=True)
                mm(ps[0:96, 2 + h, :], smallw[:, 128:224], kup[:, 512 * h:512 * h + 512], start=True, stop=True)
                mm(ps[0:96, 4 + h, :], smallw[:, 224:320], vup[:, 512 * h:512 * h + 512], start=True, stop=True)
            for j in range(PAIRS):
                last = mm(ps[:, 6 + j // 4, 128 * (j % 4):128 * (j % 4) + 128], odT[:, 128 * j:128 * j + 128],
                          smallw[:, 320:448], start=True, stop=True)
            last.then_inc(fold_psum, 1)
            pe.wait_ge(fold_done, 4)
            for j in range(PAIRS):
                mm(ps[:, 0, 32 * j:32 * j + 32], wki[:, 128 * j:128 * j + 128], ctx_ipa, start=True, stop=True)
            for j in range(PAIRS):
                mm(ps[:, 0, 256 + 32 * j:256 + 32 * j + 32], wvi[:, 128 * j:128 * j + 128], ctx_ipa, start=True, stop=True)
            for j in range(PAIRS):
                last = pe.transpose(ps[:, 1 + j // 4, 128 * (j % 4):128 * (j % 4) + 128], wq[:, 128 * j:128 * j + 128], ident[:])
            last.then_inc(fold_psum, 1)
            pe.wait_ge(fold_done, 10)
            pe.wait_ge(dve_const, 1)
            for j in range(PAIRS):
                mm(ps[:, 3, 64 * j:64 * j + 64], wqT[:, j, :], kblk[:, j, :, :], start=True, stop=True)
            for j in range(PAIRS):
                last = mm(ps[0:64, 4 + j // 4, 128 * (j % 4):128 * (j % 4) + 128], vblk[:, j, :, :], wo[:, j, :],
                          start=True, stop=True)
            last.then_inc(fold_psum, 1)
            mm(ps[:, 6, 0:128], tmp128[:], xw[:, 3, :], start=True, stop=True).then_inc(fold_psum, 1)
            pe.wait_ge(fold_done, 16)
            pe.wait_ge(w_moe_in, 32)

            def transpose_xn(i, l, bank):
                pe.wait_ge(xn_ready, at(i, LNS, l + 1))
                for t in range(TT):
                    last = pe.transpose(ps[:, bank, 128 * t:128 * t + 128], xn[:, t, :], ident[:])
                last.then_inc(xnT_psum, 1)
                pe.wait_ge(xnT_ready, at(i, 3, l + 1))

            def l0(i):
                pe.wait_ge(x3T_done, at(i, 1, 1))
                transpose_xn(i, 0, 6)
                for t in range(TT):
                    last = mm(ps[:, 7, 64 * t:64 * t + 64], xnT[:, 128 * t:128 * t + 128],
                              g_ipa[:, bass.ds(i, 1), :], start=True, stop=True)
                last.then_inc(ipa_scores, 1)
                pe.wait_ge(ctx_in, at(i, 64, 64))
                for n in range(20):
                    bank = 2 + n % 4
                    if n >= 4:
                        if n - 4 < 12:
                            pe.wait_ge(lo_done, at(i, 12, n - 3))
                        else:
                            pe.wait_ge(hi_done, at(i, 20, n - 3))
                    if n < 4:
                        for h in range(2):
                            j = 2 * n + h
                            last = mm(ps[:, bank, N * h:N * h + N], wq[:, 128 * j:128 * j + 128], xnT[:], start=True, stop=True)
                    elif n < 12:
                        j = n - 4
                        last = mm(ps[:, bank, :], wk[:, 128 * j:128 * j + 128], ctx0[:], start=True, stop=True)
                    else:
                        k, h = divmod(n - 12, 2)
                        last = mm(ps[:, bank, :], ctx0[:, 128 * k:128 * k + 128], wv[:, 512 * h:512 * h + 512], start=True, stop=True)
                    last.then_inc(fill_full, 1)

                def row_max(h):
                    p0 = 64 * (h % 2)
                    if h >= 1:
                        pe.wait_ge(max_done, at(i, H0, h))
                    if h % GH == 0 and h:
                        pe.wait_ge(nmT_ready, at(i, H0 // GH, h // GH))
                    for t in range(TT):
                        last = mm(ps[:, t, 0:SM], q12[p0:p0 + 64, 0, h // 2, 128 * t:128 * t + 128],
                                  k12[p0:p0 + 64, 0, h // 2, 0:SM], start=True, stop=True)
                    last.then_inc(max_full, 1)

                def maxima_T(gr):
                    pe.wait_ge(nm_parts, at(i, H0 // GH, gr + 1))
                    for t in range(TT):
                        last = pe.transpose(ps[:, 0, 128 * t:128 * t + 128], mxs[:, t, :].bitcast(F32), ident[:])
                    last.then_inc(nmT_psum, 1)

                def scores(h):
                    p0 = 64 * (h % 2)
                    if h % GH == 0:
                        pe.wait_ge(nmT_ready, at(i, H0 // GH, h // GH + 1))
                    if h >= 2:
                        pe.wait_ge(probs_ready, at(i, H0, h - 1))
                    elif h == 0:
                        pe.wait_ge(hi_done, at(i, 20, 20))
                    for k in range(KT):
                        o = ps[:, 2 + 2 * (h % 2) + k // 2, N * (k % 2):N * (k % 2) + N]
                        for n, (a, b) in enumerate(((0, 0), (0, 1), (1, 0))):
                            mm(o, k12[p0:p0 + 64, a, h // 2, 128 * k:128 * k + 128], q12[p0:p0 + 64, b, h // 2, :],
                               start=(n == 0), stop=False)
                        last = mm(o, sel4[p0:p0 + 64, h % GH, :], nmT[p0:p0 + 64, :], start=False, stop=True)
                    last.then_inc(score_full, 1)

                def values(h):
                    p0 = 64 * (h % 2)
                    bank = 6 + (h // 2) % 2
                    if h % 2 == 0 and h >= 4:
                        pe.wait_ge(pair_out, at(i, PAIRS, h // 2 - 1))
                    pe.wait_ge(probs_ready, at(i, H0, h + 1))
                    if h == 0:
                        pe.wait_ge(xnT_ready, at(i, 3, 1))
                    if h == 2:
                        pe.wait_ge(ipa_shifted, at(i, 1, 1))
                    for k in range(KT):
                        kr = min(128, SM - 128 * k)
                        pr = probs[0:kr, h % 2, N * k:N * k + N]
                        mm(ps[p0:p0 + 64, bank, 0:N], v0[0:kr, k, 64 * h:64 * h + 64], pr,
                           start=(k == 0), stop=(k == KT - 1), skip_group_check=True)
                        last = mm(ps[p0:p0 + 64, bank, N:2 * N], ones[0:kr, 0:64], pr,
                                  start=False, stop=(k == KT - 1), skip_group_check=True)
                    last.then_inc(pv_head, 1)

                for h in range(GH):
                    row_max(h)
                maxima_T(0)
                for h in range(H0):
                    if h + GH < H0:
                        row_max(h + GH)
                    scores(h)
                    if h >= 1:
                        values(h - 1)
                    if h % GH == GH - 1 and h // GH + 1 < H0 // GH:
                        maxima_T(h // GH + 1)
                values(H0 - 1)
                wait_apart(pe, apart_tally, ipa_probs, at(i, 1, 1))
                for t in range(TT):
                    last = pe.transpose(ps[0:64, 0, 128 * t:128 * t + 128], pi[:, t, :], ident[:])
                last.then_inc(ipa_T, 1)
                pe.wait_ge(ipa_ready, at(i, 1, 1))
                pe.wait_ge(pair_out, at(i, PAIRS, PAIRS))
                for t in range(TT):
                    for j in range(PAIRS):
                        mm(ps[:, 1, 128 * t:128 * t + 128], outT[:, j, 128 * t:128 * t + 128], wo[:, j, :],
                           start=(j == 0), stop=False)
                    last = mm(ps[:, 1, 128 * t:128 * t + 128], piT[:, 128 * t:128 * t + 128], vw[:], start=False, stop=True)
                last.then_inc(y_full, 1)

            def moe(i):
                transpose_xn(i, 1, 6)
                for t in range(TT):
                    last = mm(ps[:, 7, 8 * t:8 * t + 8], xnT[:, 128 * t:128 * t + 128], cst[:, C_WR:C_WR + 8], start=True, stop=True)
                last.then_inc(logits_full, 1)

                def hidden(n):
                    if n >= 4:
                        pe.wait_ge(hs_ready, at(i, 16, n - 3))
                    for h in range(2):
                        c = 2 * n + h
                        last = mm(ps[:, n % 4, N * h:N * h + N], w1T[:, 128 * c:128 * c + 128], xnT[:], start=True, stop=True)
                    last.then_inc(h_full, 1)

                def project(n):
                    pe.wait_ge(hs_ready, at(i, 16, n + 1))
                    if n == 8:
                        pe.wait_ge(gap_ready, at(i, 1, 1))
                    for h in range(2):
                        c = 2 * n + h
                        e = c // 4
                        for t in range(TT):
                            last = mm(ps[:, 4 + 2 * (e // 4) + t, 128 * (e % 4):128 * (e % 4) + 128],
                                      hs[:, n % 3, h, 128 * t:128 * t + 128], w2T[:, c, :],
                                      start=(c % 4 == 0), stop=(c % 4 == 3))
                    last.then_inc(w2_done, 1)
                    if n % 8 == 7:
                        pass

                hidden(0)
                hidden(1)
                for n in range(16):
                    if n + 2 < 16:
                        hidden(n + 2)
                    project(n)

            def cross(i):
                transpose_xn(i, 2, 6)
                pe.wait_ge(ctx_in, at(i, 64, 64))
                mm(ps[:, 0, 0:N], xw[:, 0, :], xnT[:], start=True, stop=True)
                mm(ps[:, 1, :], xw[0:96, 1, :], ctxT[:], start=True, stop=True).then_inc(x_proj, 1)
                for k in range(KT):
                    last = mm(ps[:, 2, 128 * k:128 * k + 128], ctxT[:, 128 * k:128 * k + 128], xw[0:96, 2, :], start=True, stop=True)
                last.then_inc(ctx_used, 1)
                mm(ps[:, 3, 0:128], ident[:], ident[:], start=True, stop=True).then_inc(x_proj, 1)
                pe.wait_ge(x_stacks_in, at(i, 128, 128))
                for h in range(H1):
                    if h >= 1:
                        pe.wait_ge(x_max_done, at(i, H1, h))
                    else:
                        pe.wait_ge(x_lo, at(i, 2, 2))
                    for t in range(TT):
                        last = mm(ps[:, t, :], qst[:, h, 128 * t:128 * t + 128], kst[:, h, :], start=True, stop=True)
                    last.then_inc(x_max_full, 1)
                pe.wait_ge(x_nm_parts, at(i, 1, 1))
                for t in range(TT):
                    last = pe.transpose(ps[:, 0, 128 * t:128 * t + 128], mxs[:, t, :].bitcast(F32), ident[:])
                last.then_inc(x_nmT_psum, 1)
                pe.wait_ge(x_nmT_ready, at(i, 1, 1))

                def scores(n):
                    h = ORDER8[n]
                    if n >= 2:
                        pe.wait_ge(x_probs_ready, at(i, H1, n - 1))
                    elif n == 0:
                        pe.wait_ge(x_v, at(i, 1, 1))
                    for k in range(KT):
                        o = ps[:, 2 + 2 * (n % 2) + k // 2, N * (k % 2):N * (k % 2) + N]
                        mm(o, kst[:, h, 128 * k:128 * k + 128], qst[:, h, :], start=True, stop=False)
                        last = mm(o, sel8[:, h, :], nmT[0:64, :], start=False, stop=True)
                    last.then_inc(x_score_full, 1)

                def values(n):
                    h = ORDER8[n]
                    c0 = 32 * (h // 2)
                    pe.wait_ge(x_probs_ready, at(i, H1, n + 1))
                    for k in range(KT):
                        pr = probs[:, n % 2, N * k:N * k + N]
                        mm(ps[c0:c0 + 32, 6, 0:N], vpx[:, k, h, :], pr, start=(n < 4 and k == 0),
                           stop=(n >= 4 and k == KT - 1), skip_group_check=True, tile_position=(0, c0))
                        last = mm(ps[c0:c0 + 32, 6, N:2 * N], sumsel[:, h % 2, :], pr, start=False,
                                  stop=(n >= 4 and k == KT - 1), skip_group_check=True, tile_position=(0, c0))
                    last.then_inc(x_pv, 1)

                for n in range(H1):
                    scores(n)
                    if n >= 1:
                        values(n - 1)
                values(H1 - 1)
                pe.wait_ge(x_ctxo, at(i, 1, 1))
                for t in range(TT):
                    last = mm(ps[:, 7, 128 * t:128 * t + 128], outT[:, 0, 128 * t:128 * t + 128], xw[:, 3, :], start=True, stop=True)
                last.then_inc(x_y, 1)
                pe.wait_ge(xn_ready, at(i, LNS, LNS))
                for t in range(TT):
                    last = pe.transpose(ps[:, 6, 128 * t:128 * t + 128], xn[:, t, :], ident[:])
                last.then_inc(x3T_psum, 1)

            with pe.Fori(0, B) as i:
                l0(i)
                moe(i)
                cross(i)
            pe.wait_ge(x3T_done, B + 1)
            mm(ps[:, 5, 0:128], ident[:], ident[:], start=True, stop=True).then_inc(loop_a_done, 1)

            raw, fw, fb = TB["raw"], TB["fw"], TB["fb"]
            pe.wait_ge(w_b_in, 16 * N_B)
            for c in range(NODES):
                if c >= 4:
                    pe.wait_ge(fb_done, c - 3)
                b = c % 4
                for n in range(3):
                    mm(ps[:, b, 128 * n:128 * n + 128], raw[:, c, n, :], raw[:, c, 4 + n, :], start=True, stop=True)
                for n in range(3):
                    last = mm(ps[:, b, 384 + n:385 + n], raw[:, c, 4 + n, :], cst[:, C_BE + EDGES[c][0][n]:C_BE + EDGES[c][0][n] + 1],
                              start=True, stop=True)
                last.then_inc(fb_psum, 1)
            pe.wait_ge(fb_done, NODES)
            for c in range(NODES):
                last = mm(ps[:, 5, c:c + 1], raw[:, c, 7, :], fb[:, c, 2:3], start=True, stop=True)
            last.then_inc(fb_psum, 1)
            pe.wait_ge(fb_done, NODES + 1)
            pe.wait_ge(pool_const, 3)

            def proj(i, r, c):
                nq, nk, nv = EDGES[c][1]
                nodes = TB["nodes"][r]
                bank = 6 + r
                if c == 0:
                    pe.wait_ge(b_node0, at(i, 2, r + 1))
                else:
                    pe.wait_ge(n_node[r], at(i, NODES, c))
                mm(ps[:, bank, 0:N], fw[:, c, 0, :], nodes[:, nq, :], start=True, stop=True)
                mm(ps[:, bank, N:2 * N], fw[:, c, 1, :], nodes[:, nk, :], start=True, stop=True).then_inc(n_proj[r], 1)
                pe.wait_ge(n_lo[r], at(i, NODES, c + 1))
                for k in range(TT):
                    mm(ps[:, bank, 128 * k:128 * k + 128], nodes[:, nv, 128 * k:128 * k + 128], fw[:, c, 2, :], start=True, stop=True)
                mm(ps[:, bank, N:2 * N], fw[:, c, 3, :], nodes[:, nq, :], start=True, stop=True).then_inc(n_v_full[r], 1)

            last_max = [None]

            def maxes(i, r, c):
                pe.wait_ge(n_stacks_in[r], at(i, 128 * NODES, 128 * (c + 1)))
                q, k = TB["bqst"][r], TB["bkst"][r]
                for h in range(H1):
                    if h >= 2:
                        pe.wait_ge(n_max_done[r], at(i, NODES * H1, c * H1 + h - 1))
                    elif last_max[0] is not None:
                        lr, lc = last_max[0]
                        pe.wait_ge(n_nmT_ready[lr], at(i, NODES, lc + 1))
                    for t in range(TT):
                        last = mm(ps[:, h % 2, N * t:N * t + N], q[:, h, 128 * t:128 * t + 128], k[:, h, :], start=True, stop=True)
                    last.then_inc(n_max_full[r], 1)
                wait_apart(pe, apart_tally, n_nm_parts[r], at(i, NODES, c + 1))
                for t in range(TT):
                    last = pe.transpose(ps[0:64, 0, 128 * t:128 * t + 128], TB["bmxs"][r][:, t, :].bitcast(F32), ident[:])
                last.then_inc(n_nmT_psum[r], 1)
                last_max[0] = (r, c)

            last_att = [None]

            def attend(i, r, c):
                q, k, pr = TB["bqst"][r], TB["bkst"][r], TB["bprobs"][r]
                bank = 6 + r
                pe.wait_ge(n_nmT_ready[r], at(i, NODES, c + 1))

                def values(half):
                    pe.wait_ge(n_probs[r], at(i, NODES * H1, c * H1 + 4 * half + 4))
                    if half == 0:
                        pe.wait_ge(n_v[r], at(i, NODES, c + 1))
                    for s in range(2):
                        for kt in range(TT):
                            for j in range(4):
                                h = 2 * j + half
                                o = ps[32 * j:32 * j + 32, bank, N * s:N * s + N]
                                w = TB["vpad"][r][:, kt, h, :] if s == 0 else sumsel[:, half, :]
                                last = mm(o, w, pr[:, h, N * kt:N * kt + N], start=(half == 0 and s == 0 and kt == 0),
                                          stop=(half == 1 and kt == TT - 1), skip_group_check=True, tile_position=(0, 32 * j))
                    last.then_inc(n_pv[r], 1)

                for n, h in enumerate(ORDER8):
                    if n >= 4:
                        pe.wait_ge(n_probs[r], at(i, NODES * H1, c * H1 + n - 3))
                    elif last_att[0] is not None:
                        lr, lc = last_att[0]
                        pe.wait_ge(n_probs[lr], at(i, NODES * H1, lc * H1 + 5 + n))
                    for kt in range(TT):
                        o = ps[:, 2 + n % 4, N * kt:N * kt + N]
                        mm(o, k[:, h, 128 * kt:128 * kt + 128], q[:, h, :], start=True, stop=False)
                        last = mm(o, sel8[:, h, :], TB["bnmT"][r][:], start=False, stop=True)
                    last.then_inc(n_score_full[r], 1)
                    if n == 5:
                        values(0)
                values(1)
                last_att[0] = (r, c)

            def node(i, r, c):
                pe.wait_ge(n_ctxo[r], at(i, NODES, c + 1))
                mm(ps[:, 6 + r, 0:N], fw[:, c, 4, :], TB["bctx"][r][:], start=True, stop=True).then_inc(n_wo[r], 1)
                if c == NODES - 1:
                    pe.wait_ge(n_node[r], at(i, NODES, NODES))
                    for t in range(TT):
                        last = pe.transpose(ps[:, 6 + r, N + 128 * t:N + 128 * t + 128], TB["nodes"][r][:, NODES, 128 * t:128 * t + 128], ident[:])
                    last.then_inc(n_last_T[r], 1)

            with pe.Fori(0, B // 2) as i:
                last_max[0] = last_att[0] = None
                for stage, r, c in node_schedule():
                    {"proj": proj, "max": maxes, "attend": attend, "node": node}[stage](i, r, c)

        @block.scalar
        def _(act):
            a = nc.scalar
            act.wait_ge(w_in, 16 * N_W)
            a.activation(tanh_g[:], cst[:, C_GX:C_GX + 4], ACT.Tanh).then_inc(gates_tanh, 1)
            act.sem_inc(x3T_done, 1)

            def l0(i):
                act.wait_ge(xnT_psum, at(i, 3, 1))
                a.copy(xnT[:], ps[:, 6, 0:N]).then_inc(xnT_ready, 1)
                for n in range(20):
                    act.wait_ge(fill_full, at(i, 20, n + 1))
                    src = ps[:, 2 + n % 4, :]
                    if n < 4:
                        dst = q12[:, 0, 2 * n:2 * n + 2, :].rearrange("p a b -> p (a b)")
                    elif n < 12:
                        dst = k12[:, 0, n - 4, :]
                    else:
                        k, h = divmod(n - 12, 2)
                        dst = v0[:, k, 512 * h:512 * h + 512]
                    a.copy(dst, src).then_inc(hi_done, 1)
                    if n == 5:
                        act.wait_ge(ipa_shifted, at(i, 1, 1))
                        a.activation(pi[:, :, :], pi[:, :, :], ACT.Exp, scale=SCALE0).then_inc(ipa_exp, 1)

                def maxima(gr):
                    act.wait_ge(nmT_psum, at(i, H0 // GH, gr + 1))
                    if gr:
                        act.wait_ge(score_full, at(i, H0, GH * gr))
                    a.copy(nmT[:], ps[:, 0, 0:N]).then_inc(nmT_ready, 1)

                maxima(0)
                for h in range(H0):
                    act.wait_ge(score_full, at(i, H0, h + 1))
                    if h >= 2:
                        act.wait_ge(pv_head, at(i, H0, h - 1))
                    b = 2 + 2 * (h % 2)
                    a.activation(probs[:, h % 2, 0:3 * N], ps[:, b:b + 2, :].rearrange("p a b -> p (a b)")[:, 0:3 * N],
                                 ACT.Exp, scale=SCALE0)
                    a.activation(probs[0:SM - 384, h % 2, 3 * N:4 * N], ps[0:SM - 384, b + 1, N:2 * N],
                                 ACT.Exp, scale=SCALE0).then_inc(probs_ready, 1)
                    if h % GH == GH - 1 and h // GH + 1 < H0 // GH:
                        maxima(h // GH + 1)
                act.wait_ge(ipa_T, at(i, 1, 1))
                a.copy(piT[:], ps[0:64, 0, 0:N]).then_inc(ipa_ready, 1)

            def moe(i):
                act.wait_ge(xnT_psum, at(i, 3, 2))
                a.copy(xnT[:], ps[:, 6, 0:N]).then_inc(xnT_ready, 1)
                act.wait_ge(gap_ready, at(i, 1, 1))
                a.activation(gw[:, 1, :], gw[:, 0, :], ACT.Exp).then_inc(gap_exp, 1)
                for n in range(16):
                    act.wait_ge(h_full, at(i, 16, n + 1))
                    if n >= 2:
                        act.wait_ge(hs_ready, at(i, 16, n - 1))
                    a.activation(th[:, n % 2, :], ps[:, n % 4, :], ACT.Tanh, scale=0.5).then_inc(tanh_done, 1)

            def cross(i):
                act.wait_ge(xnT_psum, at(i, 3, 3))
                a.copy(xnT[:], ps[:, 6, 0:N]).then_inc(xnT_ready, 1)
                act.wait_ge(x_proj, at(i, 2, 1))
                a.activation(qx12[:, 0, :], ps[:, 0, 0:N], ACT.Identity, bias=cst[:, C_BQ:C_BQ + 1]).then_inc(x_hi, 1)
                a.activation(kx12[:, 0, :], ps[:, 1, :], ACT.Identity, bias=cst[:, C_BK:C_BK + 1]).then_inc(x_hi, 1)
                act.wait_ge(x_proj, at(i, 2, 2))
                for o in range(2):
                    for k in range(KT):
                        last = a.copy(vpx[:, k, :, :].rearrange("p (j e) c -> p j e c", e=2)[:, :, o, 16 * o:16 * o + 16],
                                      ps[:, 2, 128 * k:128 * k + 128].rearrange("p (j e c) -> p j e c", e=2, c=16)[:, :, o, :])
                last.then_inc(x_v, 1)
                act.wait_ge(x_nmT_psum, at(i, 1, 1))
                a.copy(nmT[:], ps[:, 0, 0:N]).then_inc(x_nmT_ready, 1)
                for n in range(H1):
                    act.wait_ge(x_score_full, at(i, H1, n + 1))
                    if n >= 2:
                        act.wait_ge(x_pv, at(i, H1, n - 1))
                    b = 2 + 2 * (n % 2)
                    a.activation(probs[:, n % 2, :], ps[:, b:b + 2, :].rearrange("p a b -> p (a b)"),
                                 ACT.Exp, scale=SCALE1).then_inc(x_probs_ready, 1)
                act.wait_ge(x3T_psum, at(i, 1, 1))
                a.copy(x3T_all[:, bass.ds(i, 1), :], ps[:, 6, 0:N]).then_inc(x3T_done, 1)

            with act.Fori(0, B) as i:
                l0(i)
                moe(i)
                cross(i)
            act.wait_ge(x3T_done, B + 1)
            a.copy(tanh_g[:, 0:1], tanh_g[:, 0:1]).then_inc(loop_a_done, 1)
            act.wait_ge(fb_done, NODES + 1)
            act.wait_ge(pool_const, 3)
            fb = TB["fb"]

            def proj(i, r, c):
                act.wait_ge(n_proj[r], at(i, NODES, c + 1))
                if c:
                    act.wait_ge(n_parts_out[r], at(i, 16 * NODES, 16 * c))
                qk = TB["qk12"][r]
                a.activation(qk[:, 0, 0, :], ps[:, 6 + r, 0:N], ACT.Identity, bias=fb[:, c, 0:1])
                a.activation(qk[:, 0, 1, :], ps[:, 6 + r, N:2 * N], ACT.Identity, bias=fb[:, c, 1:2]).then_inc(n_hi[r], 1)
                act.wait_ge(n_v_full[r], at(i, NODES, c + 1))
                for o in range(2):
                    for k in range(TT):
                        a.copy(TB["vpad"][r][:, k, :, :].rearrange("p (j e) c -> p j e c", e=2)[:, :, o, 16 * o:16 * o + 16],
                               ps[:, 6 + r, 128 * k:128 * k + 128].rearrange("p (j e c) -> p j e c", e=2, c=16)[:, :, o, :])
                a.activation(TB["qn"][r][:], ps[:, 6 + r, N:2 * N], ACT.Identity, bias=fb[:, c, 3:4]).then_inc(n_v[r], 1)

            def maxes(i, r, c):
                act.wait_ge(n_nmT_psum[r], at(i, NODES, c + 1))
                a.copy(TB["bnmT"][r][:], ps[0:64, 0, 0:N]).then_inc(n_nmT_ready[r], 1)

            def attend(i, r, c):
                for n, h in enumerate(ORDER8):
                    act.wait_ge(n_score_full[r], at(i, NODES * H1, c * H1 + n + 1))
                    a.activation(TB["bprobs"][r][:, h, :], ps[:, 2 + n % 4, :], ACT.Exp, scale=SCALE1).then_inc(n_probs[r], 1)

            with act.Fori(0, B // 2) as i:
                for r in range(2):
                    a.copy(TB["nodes"][r][:, 0, :], x3T_all[:, bass.ds(2 * i + r, 1), :]).then_inc(b_node0, 1)
                for stage, r, c in node_schedule():
                    if stage != "node":
                        {"proj": proj, "max": maxes, "attend": attend}[stage](i, r, c)

        @block.vector
        def _(dve):
            v = nc.vector
            chain = [0]

            def link(turn, per_turn, base, ins):
                chain[0] += 1
                ins.then_inc(dve_chain, 1)
                dve.wait_ge(dve_chain, at(turn, per_turn, base + chain[0]))

            def plink(ins):
                link(None, 0, 0, ins)

            v.memset(kblk, 0.0)
            v.memset(vblk, 0.0)
            dve.wait_ge(w_in, 16 * N_W)
            plink(v.tensor_scalar(cst[:, C_QA:C_OA + 1], cst[:, C_QA:C_OA + 1], 1.0 / RANK, None, ALU.mult))
            dve.wait_ge(gates_tanh, 1)
            dve.wait_ge(pool_const, 2)
            v.tensor_scalar(boT[:], cst[:, C_BO0:C_BO0 + D], tanh_g[:, 0:1], None, ALU.mult)
            v.tensor_scalar(gb[:, 0, :], cst[:, C_LG:C_LG + D], tanh_g[:, 3:4], None, ALU.mult)
            v.tensor_scalar(gb[:, 1, :], cst[:, C_LB:C_LB + D], tanh_g[:, 3:4], None, ALU.mult)
            v.tensor_scalar(xw[:, 3, :], xw[:, 3, :], tanh_g[:, 1:2], None, ALU.mult)
            v.tensor_scalar(xrow[:], cst[:, C_BO1:C_BO1 + D], tanh_g[:, 1:2], None, ALU.mult)
            v.tensor_scalar(tmp128[:], ones[:], cst[:, C_BV:C_BV + 1], None, ALU.mult).then_inc(dve_const, 1)
            dve.wait_ge(fold_psum, 1)
            v.scalar_tensor_tensor(wq[:], ps[:, 0:2, :].rearrange("p a b -> p (a b)"), cst[:, C_QA:C_QA + 1], wq[:],
                                   ALU.mult, ALU.add).then_inc(fold_done, 1)
            v.scalar_tensor_tensor(wk[:], ps[0:96, 2:4, :].rearrange("p a b -> p (a b)"), cst[0:96, C_KA:C_KA + 1], wk[:],
                                   ALU.mult, ALU.add).then_inc(fold_done, 1)
            v.scalar_tensor_tensor(wv[:], ps[0:96, 4:6, :].rearrange("p a b -> p (a b)"), cst[0:96, C_VA:C_VA + 1], wv[:],
                                   ALU.mult, ALU.add).then_inc(fold_done, 1)
            wo_f = wo[:, :, :].rearrange("p a b -> p (a b)")
            plink(v.scalar_tensor_tensor(wo_f, ps[:, 6:8, :].rearrange("p a b -> p (a b)"), cst[:, C_OA:C_OA + 1], wo_f,
                                         ALU.mult, ALU.add))
            v.tensor_scalar(wo_f, wo_f, tanh_g[:, 0:1], None, ALU.mult).then_inc(fold_done, 1)
            dve.wait_ge(fold_psum, 2)
            for s in range(2):
                rows = slice(64 * s, 64 * s + 64)
                v.tensor_copy(kblk[rows, :, s, :], ps[rows, 0, 0:256].rearrange("p (j c) -> p j c", c=32)).then_inc(fold_done, 1)
                v.tensor_copy(vblk[rows, :, s, :], ps[rows, 0, 256:512].rearrange("p (j c) -> p j c", c=32)).then_inc(fold_done, 1)
            for h in range(2):
                v.tensor_copy(wqT[:, 4 * h:4 * h + 4, :], ps[:, 1 + h, :].rearrange("p (j c) -> p j c", j=4)).then_inc(fold_done, 1)
            dve.wait_ge(fold_psum, 3)
            v.tensor_copy(g_ipa[:, :, :].rearrange("p b (t h) -> p h b t", t=IPA),
                          ps[:, 3, :].rearrange("p (h b t) -> p h b t", b=B, t=IPA)).then_inc(fold_done, 1)
            for h in range(2):
                v.tensor_copy(vwsb[:, 4 * h:4 * h + 4, :], ps[0:64, 4 + h, :].rearrange("p (j c) -> p j c", j=4)).then_inc(fold_done, 2)
            dve.wait_ge(fold_psum, 4)
            v.tensor_tensor(xrow[:], ps[:, 6, 0:128], xrow[:], ALU.add).then_inc(fold_done, 1)
            pro = chain[0]
            CH = CH_DVE_A

            def lnk(i, ins, apart=False):
                chain[0] += 1
                ins.then_inc(dve_chain, 1)
                if apart:
                    wait_apart(dve, apart_tally, dve_chain, at(i, CH, chain[0]))
                else:
                    dve.wait_ge(dve_chain, at(i, CH, chain[0]))

            def layernorm(i, l, src):
                for t in range(TT):
                    ins = v.bn_stats(st6[:, t, :], src(t))
                lnk(i, ins, apart=True)
                for t in range(TT):
                    ins = v.bn_aggr(mv[:, t, :], st6[:, t, :])
                ins.then_inc(ln_var, 1)
                dve.wait_ge(ln_rstd, at(i, LNS, l + 1))
                for t in range(TT):
                    ins = v.tensor_scalar(xn[:, t, :], src(t), mv[:, t, 0:1], rstd[:, t:t + 1], ALU.subtract, ALU.mult)
                ins.then_inc(xn_ready, 1)

            def l0(i):
                x_b = x_all[:, bass.ds(TT * i, TT), :]
                lnk(i, v.tensor_copy(xs[:, :, :], x_b))
                layernorm(i, 0, lambda t: xs[:, t, :])
                dve.wait_ge(ipa_scores, at(i, 1, 1))
                s4 = ps[:, 7, 0:TT * 64].rearrange("p (a t h) -> p a h t", t=IPA, a=TT)
                pi4 = pi[:, :, :].rearrange("p a (t h) -> p a h t", t=IPA)
                over_t = lambda x: x.rearrange("p (a h) -> p a h", a=TT).unsqueeze(3).broadcast_to((128, TT, H0, IPA))
                lnk(i, v.tensor_reduce(pis[:, 0, :], s4, AX.X, ALU.max))
                v.tensor_tensor(pi4, s4, over_t(pis[:, 0, :]), ALU.subtract).then_inc(ipa_shifted, 1)
                for n in range(12):
                    if n == 8:
                        dve.wait_ge(ipa_exp, at(i, 1, 1))
                        lnk(i, v.tensor_reduce(pis[:, 0, :], pi4, AX.X, ALU.add))
                        lnk(i, v.reciprocal(pis[:, 1, :], pis[:, 0, :]))
                        v.tensor_tensor(pi4, pi4, over_t(pis[:, 1, :]), ALU.mult).then_inc(ipa_probs, 1)
                    dve.wait_ge(hi_done, at(i, 20, n + 1))
                    src = ps[:, 2 + n % 4, :]
                    if n < 4:
                        hi, lo = (q12[:, p, 2 * n:2 * n + 2, :].rearrange("p a b -> p (a b)") for p in range(2))
                    else:
                        hi, lo = (k12[:, p, n - 4, :] for p in range(2))
                    v.tensor_tensor(lo, src, hi.bitcast(F32), ALU.subtract).then_inc(lo_done, 1)

                def row_max(h):
                    dve.wait_ge(max_full, at(i, H0, h + 1))
                    ins = v.tensor_reduce(nm[:, :, h:h + 1], ps[:, 0:2, 0:SM], AX.X, ALU.max, negate=True)
                    ins.then_inc(max_done, 1)
                    if h % GH == GH - 1:
                        gr = h // GH
                        dve.wait_ge(max_done, at(i, H0, h + 1))
                        if gr:
                            dve.wait_ge(nmT_psum, at(i, H0 // GH, gr))
                        src = nm[:, :, GH * gr:GH * gr + GH]
                        hi = mxs[:, :, :].rearrange("p t (a b) -> p t a b", a=2)[:, :, :, 0:GH]
                        lo = mxs[:, :, :].rearrange("p t (a b) -> p t a b", a=2)[:, :, :, 32:32 + GH]
                        srcb = src.unsqueeze(2).broadcast_to((128, TT, 2, GH))
                        lnk(i, v.tensor_copy(hi, srcb))
                        v.tensor_tensor(lo, srcb, hi.bitcast(F32), ALU.subtract).then_inc(nm_parts, 1)

                def pair(j):
                    dve.wait_ge(pv_head, at(i, H0, 2 * j + 2))
                    b = 6 + j % 2
                    if j:
                        dve.wait_ge(pair_out, at(i, PAIRS, j))
                    lnk(i, v.reciprocal(rsum[:], ps[:, b, N:2 * N]))
                    v.tensor_tensor(outT[:, j, :], ps[:, b, 0:N], rsum[:], ALU.mult).then_inc(pair_out, 1)

                for h in range(GH):
                    row_max(h)
                for h in range(H0):
                    if h + GH < H0:
                        row_max(h + GH)
                    if h >= 3 and h % 2 == 1:
                        pair(h // 2 - 1)
                pair(PAIRS - 1)
                dve.wait_ge(y_full, at(i, 1, 1))
                y = ps[:, 1, 0:TT * D].rearrange("p (t d) -> p t d", t=TT)
                lnk(i, v.tensor_tensor(xs[:, :, :], y, xs[:, :, :], ALU.add))
                lnk(i, v.tensor_tensor(xs[:, :, :], xs[:, :, :], boT[:].unsqueeze(1).broadcast_to((128, TT, D)), ALU.add))

            def moe(i):
                layernorm(i, 1, lambda t: xs[:, t, :])
                dve.wait_ge(logits_full, at(i, 1, 1))
                lnk(i, v.tensor_copy(lg[:, :, :], ps[:, 7, 0:TT * E].rearrange("p (t e) -> p t e", t=TT)), apart=True)
                for t in range(TT):
                    ins = v.max(top[:, t, :], lg[:, t, :])
                lnk(i, ins)
                v.tensor_tensor(gw[:, 0, :], top[:, :, 1], top[:, :, 0], ALU.subtract).then_inc(gap_ready, 1)
                for t in range(TT):
                    ins = v.max_index(topi[:, t, :], top[:, t, :], lg[:, t, :])
                lnk(i, ins)
                lnk(i, v.tensor_copy(topf[:, :, :], topi[:, :, :]))
                for t in range(TT):
                    v.tensor_scalar(gate[:, t, :], iota8[:], topf[:, t, 0:1], None, ALU.is_equal)
                    ins = v.tensor_scalar(gate2[:, t, :], iota8[:], topf[:, t, 1:2], None, ALU.is_equal)
                dve.wait_ge(gap_exp, at(i, 1, 1))
                lnk(i, v.tensor_scalar(gw[:, 2, :], gw[:, 1, :], 1.0, None, ALU.add))
                lnk(i, v.reciprocal(gw[:, 3, :], gw[:, 2, :]))
                lnk(i, v.tensor_scalar(gw[:, 4, :], gw[:, 3, :], tanh_g[:, 2:3], 0.5, ALU.mult, ALU.mult))
                lnk(i, v.tensor_tensor(gw[:, 5, :], gw[:, 4, :], gw[:, 1, :], ALU.mult))
                for t in range(TT):
                    ins = v.tensor_scalar(gate[:, t, :], gate[:, t, :], gw[:, 4, t:t + 1], None, ALU.mult)
                lnk(i, ins)
                for t in range(TT):
                    ins = v.scalar_tensor_tensor(gate[:, t, :], gate2[:, t, :], gw[:, 5, t:t + 1], gate[:, t, :], ALU.mult, ALU.add)
                lnk(i, ins)

                def experts(g):
                    dve.wait_ge(w2_done, at(i, 16, 8 * g + 8))
                    for e in range(4 * g, 4 * g + 4):
                        for t in range(TT):
                            y = ps[:, 4 + 2 * g + t, 128 * (e % 4):128 * (e % 4) + 128]
                            ins = v.scalar_tensor_tensor(xs[:, t, :], y, gate[:, t, e:e + 1], xs[:, t, :], ALU.mult, ALU.add)
                        lnk(i, ins)

                for n in range(16):
                    dve.wait_ge(tanh_done, at(i, 16, n + 1))
                    if n >= 3:
                        dve.wait_ge(w2_done, at(i, 16, n - 2))
                    v.scalar_tensor_tensor(hs[:, n % 3, :, :].rearrange("p a b -> p (a b)"), th[:, n % 2, :], 1.0,
                                           ps[:, n % 4, :], ALU.add, ALU.mult).then_inc(hs_ready, 1)
                    if n == 10:
                        experts(0)
                experts(1)

            def cross(i):
                layernorm(i, 2, lambda t: xs[:, t, :])
                dve.wait_ge(x_hi, at(i, 2, 1))
                v.scalar_tensor_tensor(qx12[:, 1, :], ps[:, 0, 0:N], cst[:, C_BQ:C_BQ + 1], qx12[:, 0, :].bitcast(F32),
                                       ALU.add, ALU.subtract).then_inc(x_lo, 1)
                dve.wait_ge(x_hi, at(i, 2, 2))
                v.scalar_tensor_tensor(kx12[:, 1, :], ps[:, 1, :], cst[:, C_BK:C_BK + 1], kx12[:, 0, :].bitcast(F32),
                                       ALU.add, ALU.subtract).then_inc(x_lo, 1)
                for h in range(H1):
                    dve.wait_ge(x_max_full, at(i, H1, h + 1))
                    ins = v.tensor_reduce(nm[:, :, h:h + 1], ps[:, 0:2, :], AX.X, ALU.max, negate=True).then_inc(x_max_done, 1)
                dve.wait_ge(x_max_done, at(i, H1, H1))
                lnk(i, v.tensor_copy(mxs[:, :, 0:H1], nm[:, :, 0:H1]))
                v.tensor_tensor(mxs[:, :, 32:32 + H1], nm[:, :, 0:H1], mxs[:, :, 0:H1].bitcast(F32), ALU.subtract).then_inc(x_nm_parts, 1)
                dve.wait_ge(x_pv, at(i, H1, H1))
                lnk(i, v.reciprocal(rsum[:], ps[:, 6, N:2 * N]))
                v.tensor_tensor(outT[:, 0, :], ps[:, 6, 0:N], rsum[:], ALU.mult).then_inc(x_ctxo, 1)
                dve.wait_ge(x_nmT_psum, at(i, 1, 1))
                v.memset(mxs[:, :, 0:64].bitcast(F32), 0.0)
                dve.wait_ge(x_y, at(i, 1, 1))
                y = ps[:, 7, 0:TT * D].rearrange("p (t d) -> p t d", t=TT)
                lnk(i, v.tensor_tensor(xs[:, :, :], y, xs[:, :, :], ALU.add))
                lnk(i, v.tensor_tensor(xs[:, :, :], xs[:, :, :], xrow[:].unsqueeze(1).broadcast_to((128, TT, D)), ALU.add))
                v.tensor_tensor(x_all[:, bass.ds(TT * i, TT), :], xs[:, :, :],
                                gb[:, 1, :].unsqueeze(1).broadcast_to((128, TT, D)), ALU.add).then_inc(x3_ready, 1)
                layernorm(i, 3, lambda t: xs[:, t, :])
                dve.wait_ge(xn_ready, at(i, LNS, LNS))
                dve.wait_ge(x3T_psum, at(i, 1, 1))

            with dve.Fori(0, B) as i:
                l0(i)
                moe(i)
                cross(i)
                assert chain[0] - pro == CH_DVE_A, f"CH_DVE_A = {chain[0] - pro}"
            chain[0] = pro + CH_DVE_A * B
            dve.wait_ge(x3_ready, B)
            v.memset(nm[:, 0, 0:1], 0.0).then_inc(loop_a_done, 1)

            raw, fw, fb = TB["raw"], TB["fw"], TB["fb"]
            dve.wait_ge(w_b_in, 16 * N_B)
            for c in range(NODES):
                ew = lambda n: cst[:, C_EW + 3 * c + n:C_EW + 3 * c + n + 1]
                aw = cst[:, C_AW + c:C_AW + c + 1]
                dve.wait_ge(fb_psum, c + 1)
                for n in range(3):
                    v.tensor_scalar(fw[:, c, n, :], ps[:, c % 4, 128 * n:128 * n + 128], ew(n), None, ALU.mult)
                    v.tensor_scalar(fb[:, c, n:n + 1], ps[:, c % 4, 384 + n:385 + n], ew(n), None, ALU.mult)
                v.tensor_scalar(fw[:, c, 3, :], raw[:, c, 3, :], ew(0), None, ALU.mult)
                v.tensor_scalar(fb[:, c, 3:4], cst[:, C_BE + EDGES[c][0][0]:C_BE + EDGES[c][0][0] + 1], ew(0), None, ALU.mult)
                v.tensor_scalar(fw[:, c, 4, :], raw[:, c, 7, :], aw, None, ALU.mult).then_inc(fb_done, 1)
            dve.wait_ge(fb_psum, NODES + 1)
            for c in range(NODES):
                ins = v.tensor_scalar(fb[:, c, 4:5], ps[:, 5, c:c + 1], cst[:, C_AW + c:C_AW + c + 1], None, ALU.mult)
            ins.then_inc(fb_done, 1)
            dve.wait_ge(fb_done, NODES + 1)
            dve.wait_ge(pool_const, 3)
            base_b = chain[0]
            CHB = 2 * (2 * NODES + 3)

            def lnb(i, ins, apart=False):
                chain[0] += 1
                ins.then_inc(dve_chain, 1)
                if apart:
                    wait_apart(dve, apart_tally, dve_chain, at(i, CHB, chain[0]))
                else:
                    dve.wait_ge(dve_chain, at(i, CHB, chain[0]))

            def proj(i, r, c):
                dve.wait_ge(n_hi[r], at(i, NODES, c + 1))
                qk = TB["qk12"][r]
                for n in range(2):
                    ins = v.scalar_tensor_tensor(qk[:, 1, n, :], ps[:, 6 + r, N * n:N * n + N], fb[:, c, n:n + 1],
                                                 qk[:, 0, n, :].bitcast(F32), ALU.add, ALU.subtract)
                ins.then_inc(n_lo[r], 1)

            def maxes(i, r, c):
                bnm, bmx = TB["bnm"][r], TB["bmxs"][r]
                for h in range(H1):
                    dve.wait_ge(n_max_full[r], at(i, NODES * H1, c * H1 + h + 1))
                    v.tensor_reduce(bnm[:, :, h:h + 1], ps[:, h % 2, :].rearrange("p (t k) -> p t k", t=TT), AX.X, ALU.max,
                                    negate=True).then_inc(n_max_done[r], 1)
                dve.wait_ge(n_max_done[r], at(i, NODES * H1, c * H1 + H1))
                lnb(i, v.tensor_copy(bmx[:, :, 0:H1], bnm[:, :, :]))
                v.tensor_tensor(bmx[:, :, 32:32 + H1], bnm[:, :, :], bmx[:, :, 0:H1].bitcast(F32), ALU.subtract).then_inc(n_nm_parts[r], 1)

            def attend(i, r, c):
                pass

            def node(i, r, c):
                dve.wait_ge(n_pv[r], at(i, NODES * 2, c * 2 + 2))
                rs = TB["brs"][r]
                lnb(i, v.reciprocal(rs[:], ps[:, 6 + r, N:2 * N]))
                v.tensor_tensor(TB["bctx"][r][:], ps[:, 6 + r, 0:N], rs[:], ALU.mult).then_inc(n_ctxo[r], 1)
                dve.wait_ge(n_wo[r], at(i, NODES, c + 1))
                dve.wait_ge(n_v[r], at(i, NODES, c + 1))
                v.scalar_tensor_tensor(TB["nodes"][r][:, c + 1, :], ps[:, 6 + r, 0:N], fb[:, c, 4:5], TB["qn"][r][:],
                                       ALU.add, ALU.add).then_inc(n_node[r], 1)
                if c == NODES - 1:
                    dve.wait_ge(n_last_T[r], at(i, 1, 1))
                    o, bmv = TB["o"][r], TB["bmv"][r]
                    for t in range(TT):
                        src = ps[:, 6 + r, N + 128 * t:N + 128 * t + 128]
                        ins = v.bn_stats(TB["bst"][r][:, t, :], src)
                    lnb(i, ins, apart=True)
                    for t in range(TT):
                        ins = v.bn_aggr(bmv[:, t, :], TB["bst"][r][:, t, :])
                    ins.then_inc(n_var[r], 1)
                    dve.wait_ge(n_rstd[r], at(i, 1, 1))
                    for t in range(TT):
                        src = ps[:, 6 + r, N + 128 * t:N + 128 * t + 128]
                        ins = v.tensor_scalar(o[:, t, :], src, bmv[:, t, 0:1], TB["brstd"][r][:, t:t + 1], ALU.subtract, ALU.mult)
                    lnb(i, ins)
                    lnb(i, v.tensor_tensor(o[:, :, :], o[:, :, :], gb[:, 0, :].unsqueeze(1).broadcast_to((128, TT, D)), ALU.mult))
                    v.tensor_tensor(o[:, :, :], o[:, :, :], x_all[:, bass.ds(TT * (2 * i + r), TT), :], ALU.add).then_inc(n_out[r], 1)

            with dve.Fori(0, B // 2) as i:
                for stage, r, c in node_schedule():
                    {"proj": proj, "max": maxes, "attend": attend, "node": node}[stage](i, r, c)
                assert chain[0] - base_b == CHB, f"CHB = {chain[0] - base_b}"


_SHAPES = {}


def kernel(**inputs):
    import concourse.bacc as bacc
    from concourse.bass_utils import run_bass_kernel_spmd

    I = {k: np.asarray(v) for k, v in inputs.items()}
    tr = lambda a: np.ascontiguousarray(np.swapaxes(a, -1, -2))
    row = lambda a: np.broadcast_to(a.reshape(1, -1), (128, a.size))
    col = lambda a: a.reshape(128, -1)
    cst = np.zeros((128, C_ALL), np.float32)
    for c0, a in (
        (C_GX, row(I["g_xattn"])), (C_GF, row(I["g_ffn"])), (C_QA, row(I["L0_xattn_q_alpha"])),
        (C_KA, row(I["L0_xattn_k_alpha"])), (C_VA, row(I["L0_xattn_v_alpha"])), (C_OA, row(I["L0_xattn_o_alpha"])),
        (C_EW, row(I["L1_ffn_ew"])), (C_AW, row(I["L1_ffn_act_w"])),
        (C_BQ, col(I["L1_xattn_bq"])), (C_BK, col(I["L1_xattn_bk"])), (C_BV, col(I["L1_xattn_bv"])),
        (C_BE, tr(I["L1_ffn_be"])), (C_WR, tr(I["L0_ffn_Wr"])),
        (C_BO0, row(I["L0_xattn_bo"])), (C_BO1, row(I["L1_xattn_bo"])),
        (C_LG, row(I["L1_ffn_ln_g"])), (C_LB, row(I["L1_ffn_ln_b"])),
    ):
        cst[:, c0:c0 + a.shape[1]] = a
    ctx = I["ctx_768"]
    arrays = {
        "cst": cst, "x": I["x"], "ctxT": tr(ctx),
        "ctx_ipaT": np.ascontiguousarray(ctx[:, SM:, :].reshape(B * IPA, CD).T),
        "q_downT": tr(I["L0_xattn_q_down"]), "k_downT": tr(I["L0_xattn_k_down"]), "v_downT": tr(I["L0_xattn_v_down"]),
        "o_downT": tr(I["L0_xattn_o_down"]), "q_up": I["L0_xattn_q_up"], "k_up": I["L0_xattn_k_up"],
        "v_up": I["L0_xattn_v_up"], "o_up": I["L0_xattn_o_up"],
        "Wq": I["L0_xattn_Wq"], "Wk": I["L0_xattn_Wk"], "Wv": I["L0_xattn_Wv"], "Wo": I["L0_xattn_Wo"],
        "Wk_ipa": I["L0_xattn_Wk_ipa"], "Wv_ipa": I["L0_xattn_Wv_ipa"],
        "W1T": np.ascontiguousarray(I["L0_ffn_W1"].transpose(2, 0, 1).reshape(D, E * DFF)),
        "W2T": np.ascontiguousarray(I["L0_ffn_W2"].transpose(0, 2, 1).reshape(E * DFF, D)),
        "xWq": I["L1_xattn_Wq"], "xWk": I["L1_xattn_Wk"], "xWv": I["L1_xattn_Wv"], "xWo": I["L1_xattn_Wo"],
        "We": I["L1_ffn_We"], "WeT": tr(I["L1_ffn_We"]), "bWq": I["L1_ffn_Wq"], "bWk": I["L1_ffn_Wk"],
        "bWv": I["L1_ffn_Wv"], "bWo": I["L1_ffn_Wo"], "ident": np.eye(128, dtype=np.float32),
    }
    nc = bacc.Bacc("TRN2", target_bir_lowering=False, num_devices=1)
    feed, T = {}, {}
    for name, a in arrays.items():
        a = np.ascontiguousarray(a)
        feed[f"in_{name}"] = a
        T[name] = nc.dram_tensor(f"in_{name}", a.shape, mybir.dt.from_np(a.dtype), kind="ExternalInput").ap()
    out = nc.dram_tensor("out_0", (B, N, D), F32, kind="ExternalOutput").ap()
    build(nc, T, out)
    r = run_bass_kernel_spmd(nc, [feed], core_ids=[0])
    return r.results[0]["out_0"]
```

```python
from contextlib import ExitStack

import numpy as np
import concourse.bass as bass
from concourse import mybir

ALU = mybir.AluOpType
ACT = mybir.ActivationFunctionType
AX = mybir.AxisListType
F32 = mybir.dt.float32
F32R = mybir.dt.float32r
U32 = mybir.dt.uint32

B, N, D, S, CD = 8, 256, 128, 512, 96
TT = N // 128
IPA = 4
SM = S - IPA
H0, DH0 = 16, 64
ID0 = H0 * DH0
PAIRS = H0 // 2
H1, DH1 = 8, 16
KT = S // 128
SCALE0, SCALE1 = DH0 ** -0.5, DH1 ** -0.5
RANK = 32
E, DFF = 8, 512
NODES, MAX_PREV = 6, 5
GH = 4
LNS = 4
EPS_LN, EPS_OUT = 1e-5, 1e-6

C_GX, C_GF, C_QA, C_KA, C_VA, C_OA = 0, 2, 4, 5, 6, 7
C_EW, C_AW = 8, 26
C_BQ, C_BK, C_BV = 32, 33, 34
C_BE = 35
C_WR = 56
C_BO0, C_BO1, C_LG, C_LB = 64, 192, 320, 448
C_ALL = 576


def edges():
    out, lind = [], 0
    for c in range(NODES):
        nsrc = min(c + 1, MAX_PREV)
        s = c - nsrc
        out.append(((lind + nsrc - 1, lind, lind + nsrc // 2), (c, s + 1, s + nsrc // 2 + 1)))
        lind += nsrc
    return out


def at(turn, per_turn, k):
    return k if turn is None else turn * per_turn + k


def wait_apart(eng, tally, sem, value):
    eng.wait_ge(sem, value)
    eng.sem_inc(tally, 1)


ROWS = 4
STEPS = ROWS * NODES
TURNS_B = B // ROWS
ORDER8 = (0, 2, 4, 6, 1, 3, 5, 7)


def build(nc, T, out):
    EDGES = edges()
    ctx = ExitStack()
    with ctx:
        def sb(name, shape, dt=F32, stack=ctx):
            return stack.enter_context(nc.sbuf_tensor(name, shape, dt))

        def sem(name):
            return ctx.enter_context(nc.semaphore(name))

        def dram(name, shape):
            return nc.dram_tensor(name, shape, F32, kind="Internal").ap()

        ps = ctx.enter_context(nc.psum_tensor("ps", [128, 8, 512], F32))

        vw_dram = dram("vw_dram", (B, H0 * IPA, D))
        qx_dram = dram("qx_dram", (128, 2, N))
        kx_dram = dram("kx_dram", (128, 2, S))
        qk_dram = [dram(f"qk_dram{r}", (128, 2, 2, N)) for r in range(ROWS)]

        cst = sb("cst", [128, C_ALL])
        ident = sb("ident", [128, 128])
        x_all = sb("x_all", [128, B * TT, D])
        x3T_all = sb("x3T_all", [128, B, N])
        tanh_g = sb("tanh_g", [128, 4])
        sel8 = sb("sel8", [64, H1, 128], F32R)
        sumsel = sb("sumsel", [128, 2, 32])
        sel8f = sb("sel8f", [128, H1, 128])
        ones = sb("ones", [128, 128])
        pow_c = sb("pow_c", [128, 2])
        gb = sb("gb", [128, 2, D])
        mv = sb("mv", [128, TT, 2])
        st6 = sb("st6", [128, TT, 6])
        rstd = sb("rstd", [128, TT])
        var_e = sb("var_e", [128, TT])

        w_in = sem("w_in")
        apart_tally = sem("apart_tally")
        w_moe_in = sem("w_moe_in")
        w_b_in = sem("w_b_in")
        pool_const = sem("pool_const")
        dve_const = sem("dve_const")
        dve_chain = sem("dve_chain")
        act_chain = sem("act_chain")
        pool_chain = sem("pool_chain")
        gates_tanh = sem("gates_tanh")
        fold_psum = sem("fold_psum")
        fold_done = sem("fold_done")
        vw_out = sem("vw_out")
        ctx_in = sem("ctx_in")
        ctx_used = sem("ctx_used")
        ln_var = sem("ln_var")
        ln_rstd = sem("ln_rstd")
        xn_ready = sem("xn_ready")
        xnT_psum = sem("xnT_psum")
        xnT_ready = sem("xnT_ready")
        fill_full = sem("fill_full")
        hi_done = sem("hi_done")
        lo_done = sem("lo_done")
        max_full = sem("max_full")
        max_done = sem("max_done")
        nm_parts = sem("nm_parts")
        nmT_psum = sem("nmT_psum")
        nmT_ready = sem("nmT_ready")
        score_full = sem("score_full")
        probs_ready = sem("probs_ready")
        pv_head = sem("pv_head")
        pair_out = sem("pair_out")
        ipa_scores = sem("ipa_scores")
        ipa_shifted = sem("ipa_shifted")
        ipa_exp = sem("ipa_exp")
        ipa_probs = sem("ipa_probs")
        ipa_T = sem("ipa_T")
        ipa_ready = sem("ipa_ready")
        y_full = sem("y_full")
        logits_full = sem("logits_full")
        gap_ready = sem("gap_ready")
        gap_exp = sem("gap_exp")
        h_full = sem("h_full")
        tanh_done = sem("tanh_done")
        hs_ready = sem("hs_ready")
        w2_done = sem("w2_done")
        ye_full = sem("ye_full")
        x_proj = sem("x_proj")
        x_hi = sem("x_hi")
        x_lo = sem("x_lo")
        x_v = sem("x_v")
        x_parts_out = sem("x_parts_out")
        x_stacks_in = sem("x_stacks_in")
        x_max_full = sem("x_max_full")
        x_max_done = sem("x_max_done")
        x_nm_parts = sem("x_nm_parts")
        x_nmT_psum = sem("x_nmT_psum")
        x_nmT_ready = sem("x_nmT_ready")
        x_score_full = sem("x_score_full")
        x_probs_ready = sem("x_probs_ready")
        x_pv = sem("x_pv")
        x_ctxo = sem("x_ctxo")
        x_y = sem("x_y")
        x3_ready = sem("x3_ready")
        x3T_psum = sem("x3T_psum")
        x3T_done = sem("x3T_done")
        loop_a_done = sem("loop_a_done")
        fb_psum = sem("fb_psum")
        fb_done = sem("fb_done")
        b_node0 = sem("b_node0")
        rows_in = sem("rows_in")
        n_proj, n_hi, n_lo, n_v_full, n_v = (sem(n) for n in ("n_proj", "n_hi", "n_lo", "n_v_full", "n_v"))
        n_parts_out = [sem(f"n_parts_out{r}") for r in range(ROWS)]
        n_stacks_in = [sem(f"n_stacks_in{r}") for r in range(ROWS)]
        n_zero, n_max_full, n_max_done = sem("n_zero"), sem("n_max_full"), sem("n_max_done")
        n_nm_parts, n_nmT_psum, n_nmT = sem("n_nm_parts"), sem("n_nmT_psum"), sem("n_nmT")
        n_score, n_probs, n_pv = sem("n_score"), sem("n_probs"), sem("n_pv")
        n_ctxo, n_wo, n_node = sem("n_ctxo"), sem("n_wo"), sem("n_node")
        last_T, last_var, last_rstd, last_out = sem("last_T"), sem("last_var"), sem("last_rstd"), sem("last_out")
        stored = [sem(f"stored{r}") for r in range(ROWS)]

        sa = ExitStack()
        wq = sb("wq", [128, ID0], stack=sa)
        wk = sb("wk", [96, ID0], stack=sa)
        wv = sb("wv", [96, ID0], stack=sa)
        wo = sb("wo", [128, PAIRS, D], stack=sa)
        w1T = sb("w1T", [128, E * DFF], stack=sa)
        w2T = sb("w2T", [128, E * DFF // 128, D], stack=sa)
        xw = sb("xw", [128, 4, D], stack=sa)
        q12 = sb("q12", [128, 2, PAIRS, N], F32R, stack=sa)
        k12 = sb("k12", [128, 2, PAIRS, S], F32R, stack=sa)
        v0 = sb("v0", [128, KT, ID0], stack=sa)
        probs = sb("probs", [128, 2, KT * N], stack=sa)
        outT = sb("outT", [128, PAIRS, N], stack=sa)
        g_ipa = sb("g_ipa", [128, B, H0 * IPA], stack=sa)
        vw = sb("vw", [64, D], stack=sa)
        ctxT = sb("ctxT", [96, S], stack=sa)
        ctx0 = sb("ctx0", [96, S], stack=sa)
        xn = sb("xn", [128, TT, D], stack=sa)
        xnT = sb("xnT", [128, N], stack=sa)
        nm = sb("nm", [128, TT, H0], stack=sa)
        mxs = sb("mxs", [128, TT, 128], F32R, stack=sa)
        nmT = sb("nmT", [128, N], F32R, stack=sa)
        sel4f = sb("sel4f", [128, GH, 128], stack=sa)
        sel4 = sb("sel4", [128, GH, 128], F32R, stack=sa)
        rsum = sb("rsum", [128, N], stack=sa)
        pi = sb("pi", [128, TT, H0 * IPA], stack=sa)
        pis = sb("pis", [128, 2, TT * H0], stack=sa)
        piT = sb("piT", [64, N], stack=sa)
        xs = sb("xs", [128, TT, D], stack=sa)
        lg = sb("lg", [128, TT, E], stack=sa)
        top = sb("top", [128, TT, 8], stack=sa)
        topi = sb("topi", [128, TT, 8], U32, stack=sa)
        topf = sb("topf", [128, TT, 8], stack=sa)
        iota8 = sb("iota8", [128, E], stack=sa)
        gw = sb("gw", [128, 6, TT], stack=sa)
        gate = sb("gate", [128, TT, E], stack=sa)
        gate2 = sb("gate2", [128, TT, E], stack=sa)
        th = sb("th", [128, 2, 2 * N], stack=sa)
        hs = sb("hs", [128, 3, 2, N], stack=sa)
        vpx = sb("vpx", [128, KT, H1, 32], stack=sa)
        qx12 = sb("qx12", [128, 2, N], F32R, stack=sa)
        kx12 = sb("kx12", [128, 2, S], F32R, stack=sa)
        xrow = sb("xrow", [128, D], stack=sa)
        boT = sb("boT", [128, D], stack=sa)
        tmp128 = sb("tmp128", [128, D], stack=sa)
        wki = v0[0:96, 0, :]
        wvi = v0[0:96, 1, :]
        up = v0[0:32, 2, :]
        kup = v0[0:32, 3, :]
        vup = probs[0:32, 0, :]
        odT = probs[0:32, 1, :]
        smallw = outT[0:32, 0:3, :].rearrange("p a b -> p (a b)")
        kblk = x3T_all[:, 0:2, :].rearrange("p a b -> p (a b)").rearrange("p (j s c) -> p j s c", s=2, j=PAIRS)
        vblk = x3T_all[:, 2:4, :].rearrange("p a b -> p (a b)").rearrange("p (j s c) -> p j s c", s=2, j=PAIRS)
        wqT = x3T_all[:, 4:8, :].rearrange("p a b -> p (a b)").rearrange("p (j c) -> p j c", j=PAIRS)
        ctx_ipa = xnT[0:96, 0:32]
        vwsb = hs[0:64, 0:2, :, :].rearrange("p a b c -> p (a b c)").rearrange("p (j d) -> p j d", j=PAIRS)
        qst = q12[0:64, 1, :, :]
        kst = k12[0:64, 1, :, :]

        def place_b():
            sa.close()
            sb_ = ExitStack()
            ctx.enter_context(sb_)
            t = {}

            def per_row(name, shape, dt=F32):
                t[name] = [sb(f"{name}{r}", shape, dt, stack=sb_) for r in range(ROWS)]

            t["fw"] = sb("fw", [128, NODES, 5, D], stack=sb_)
            t["fb"] = sb("fb", [128, NODES, 5], stack=sb_)
            with ExitStack() as under:
                t["raw"] = sb("raw_b", [128, NODES, 8, D], stack=under)
            t["probs"] = sb("bprobs", [128, H1, TT * N], stack=sb_)
            t["rs"] = sb("brs", [128, N], stack=sb_)
            per_row("nodes", [128, NODES + 1, N])
            per_row("qk12", [128, 2, 2, N], F32R)
            per_row("bqst", [128, H1, N], F32R)
            per_row("bkst", [128, H1, N], F32R)
            per_row("vpad", [128, TT, H1, 32])
            per_row("qn", [128, N])
            per_row("bnm", [128, TT, H1])
            per_row("bmxs", [128, TT, 128], F32R)
            per_row("bctx", [128, N])
            per_row("o", [128, TT, D])
            per_row("bmv", [128, TT, 2])
            per_row("bst", [128, TT, 6])
            per_row("brstd", [128, TT])
            per_row("bvar", [128, TT])
            return t

        TB = place_b()
        assert TB is not None

        CH_DVE_A = 44
        block = ctx.enter_context(nc.Block())

        N_W, N_MOE, N_B = 22, 2, 8 * NODES

        @block.sync
        def _(sp):
            for dst, src in (
                (cst[:], T["cst"]), (x_all[:, :, :], T["x"].rearrange("b (t p) d -> p (b t) d", p=128)),
                (smallw[:, 0:128], T["q_downT"]), (up, T["q_up"]), (wq[:], T["Wq"]),
                (smallw[:, 128:224], T["k_downT"]), (kup, T["k_up"]), (wk[:], T["Wk"]),
                (smallw[:, 224:320], T["v_downT"]), (vup, T["v_up"]), (wv[:], T["Wv"]),
                (smallw[:, 320:448], T["o_up"]), (odT, T["o_downT"]),
                (wo[:, :, :], T["Wo"].rearrange("(j p) d -> p j d", p=128)),
                (wki, T["Wk_ipa"]), (wvi, T["Wv_ipa"]), (ctx_ipa, T["ctx_ipaT"]),
                (xw[:, 0, :], T["xWq"]), (xw[0:96, 1, :], T["xWk"]), (xw[0:96, 2, :], T["xWv"]),
                (xw[:, 3, :], T["xWo"]), (ident[:], T["ident"]),
            ):
                sp.dma_start(dst, src).then_inc(w_in, 16)

            def load_ctx(b):
                src = T["ctxT"][bass.ds(b, 1)].rearrange("a c s -> (a c) s")
                sp.dma_start(ctxT[:], src).then_inc(ctx_in, 16)
                sp.dma_start(ctx0[:, 0:SM], src[:, 0:SM]).then_inc(ctx_in, 16)
                sp.dma_start(ctx0[:, SM:S], src[:, SM - IPA:SM]).then_inc(ctx_in, 16)
                sp.dma_start(vw[:], vw_dram[bass.ds(b, 1)].rearrange("a c s -> (a c) s")).then_inc(ctx_in, 16)

            sp.dma_start(w1T[:], T["W1T"]).then_inc(w_moe_in, 16)
            sp.dma_start(w2T[:, :, :], T["W2T"].rearrange("(c p) d -> p c d", p=128)).then_inc(w_moe_in, 16)
            sp.wait_ge(fold_done, 15)
            for s in range(2):
                sp.dma_start(vw_dram.rearrange("b (t j s) d -> s (b t) j d", s=2, t=IPA)[s],
                             vwsb[32 * s:32 * s + 32, :, :]).then_inc(vw_out, 16)
            sp.wait_ge(vw_out, 32)
            load_ctx(0)

            def bounce(i, last):
                sp.wait_ge(x_lo, at(i, 2, 2))
                sp.dma_start(qx_dram, qx12[:, :, :].bitcast(F32)).then_inc(x_parts_out, 16)
                sp.dma_start(kx_dram, kx12[:, :, :].bitcast(F32)).then_inc(x_parts_out, 16)
                sp.wait_ge(x_parts_out, at(i, 32, 32))
                for s in range(2):
                    for r in range(2):
                        sp.dma_start(qst[32 * s + 16 * r:32 * s + 16 * r + 16].bitcast(F32),
                                     qx_dram[:, s].rearrange("(h d) q -> d h q", h=H1)).then_inc(x_stacks_in, 16)
                        sp.dma_start(kst[32 * r + 16 * s:32 * r + 16 * s + 16].bitcast(F32),
                                     kx_dram[:, s].rearrange("(h d) q -> d h q", h=H1)).then_inc(x_stacks_in, 16)

            with sp.Fori(0, B - 1) as i:
                bounce(i, False)
                sp.wait_ge(ctx_used, at(i, 1, 1))
                load_ctx(i + 1)
            bounce(B - 1, True)

            sp.wait_ge(loop_a_done, 3)
            raw = TB["raw"]
            for c, ((eq, ek, ev), _src) in enumerate(EDGES):
                for n, src in enumerate((T["WeT"][eq], T["WeT"][ek], T["WeT"][ev], T["We"][eq],
                                         T["bWq"][c], T["bWk"][c], T["bWv"][c], T["bWo"][c])):
                    sp.dma_start(raw[:, c, n, :], src).then_inc(w_b_in, 16)

            for r in range(ROWS):
                sp.sem_inc(stored[r], 16)
            with sp.Fori(0, TURNS_B) as i:
                for s in range(STEPS):
                    c, r = divmod(s, ROWS)
                    sp.wait_ge(n_lo, at(i, STEPS, s + 1))
                    sp.dma_start(qk_dram[r], TB["qk12"][r][:, :, :, :].bitcast(F32)).then_inc(n_parts_out[r], 16)
                    sp.wait_ge(n_parts_out[r], at(i, 16 * NODES, 16 * (c + 1)))
                    for p in range(2):
                        for k in range(2):
                            sp.dma_start(TB["bqst"][r][32 * p + 16 * k:32 * p + 16 * k + 16].bitcast(F32),
                                         qk_dram[r][:, p, 0].rearrange("(h d) q -> d h q", h=H1)).then_inc(n_stacks_in[r], 16)
                            sp.dma_start(TB["bkst"][r][32 * k + 16 * p:32 * k + 16 * p + 16].bitcast(F32),
                                         qk_dram[r][:, p, 1].rearrange("(h d) q -> d h q", h=H1)).then_inc(n_stacks_in[r], 16)
                for r in range(ROWS):
                    sp.wait_ge(last_out, at(i, ROWS, ROWS + r + 1))
                    sp.dma_start(out[bass.ds(ROWS * i + r, 1)].rearrange("a (t p) d -> p (a t) d", p=128),
                                 TB["o"][r][:, :, :]).then_inc(stored[r], 16)
            for r in range(ROWS):
                sp.wait_ge(stored[r], 16 * (TURNS_B + 1))

        @block.gpsimd
        def _(pool):
            g = nc.gpsimd
            g.memset(mxs[:, :, :].bitcast(F32), 0.0)
            g.memset(vpx[:, :, :, :], 0.0)
            g.memset(ones[:], 1.0)
            g.memset(sumsel[:, :, :], 0.0)
            g.memset(pow_c[:], -0.5)
            g.memset(sel4f[:, :, :], 0.0)
            g.memset(sel8f[:, :, :], 0.0)
            g.iota(topi[:, 0, :], [[1, E]], base=0, channel_multiplier=0).then_inc(pool_const, 1)
            pool.wait_ge(pool_const, 1)
            g.tensor_copy(iota8[:], topi[:, 0, :])
            g.memset(sumsel[:, 0, 0:16], 1.0)
            g.memset(sumsel[:, 1, 16:32], 1.0)
            for base in (0, 32, 64, 96):
                last = g.affine_select(out=sel4f[:, :, :], in_=sel4f[:, :, :], compare_op=ALU.not_equal, fill=1.0,
                                       base=-base, pattern=[[-1, GH], [0, 128]], channel_multiplier=1)
                last.then_inc(pool_chain, 1)
                pool.wait_ge(pool_chain, base // 32 + 1)
            for n, base in enumerate((0, 32, 64, 96)):
                last = g.affine_select(out=sel8f[:, :, :], in_=sel8f[:, :, :], compare_op=ALU.not_equal, fill=1.0,
                                       base=-base, pattern=[[-1, H1], [0, 128]], channel_multiplier=1)
                last.then_inc(pool_chain, 1)
                pool.wait_ge(pool_chain, 5 + n)
            g.tensor_copy(sel8[:, :, :], sel8f[0:64, :, :])
            g.tensor_copy(sel4[:, :, :], sel4f[:, :, :]).then_inc(pool_const, 1)

            with pool.Fori(0, B) as i:
                for l in range(LNS):
                    wait_apart(pool, apart_tally, ln_var, at(i, LNS, l + 1))
                    g.tensor_scalar(var_e[:], mv[:, :, 1], EPS_LN, None, ALU.add).then_inc(pool_chain, 1)
                    pool.wait_ge(pool_chain, at(i, LNS, 8 + l + 1))
                    g.tensor_tensor(rstd[:], var_e[:], pow_c[:], ALU.pow).then_inc(ln_rstd, 1)
            pool.wait_ge(loop_a_done, 3)
            pool.wait_ge(fb_done, NODES + 1)
            for r in range(ROWS):
                g.memset(TB["bmxs"][r][:, :, :].bitcast(F32), 0.0)
                last = g.memset(TB["vpad"][r][:, :, :, :], 0.0)
            last.then_inc(pool_const, 1)
            with pool.Fori(0, TURNS_B) as i:
                for s in range(STEPS):
                    if s < ROWS:
                        wait_apart(pool, apart_tally, rows_in, at(i, ROWS, ROWS))
                    else:
                        wait_apart(pool, apart_tally, n_score, at(i, STEPS * H1, (s - ROWS + 1) * H1))
                    g.memset(TB["bqst"][s % ROWS][64:128, :, :].bitcast(F32), 0.0).then_inc(n_zero, 1)
                for r in range(ROWS):
                    wait_apart(pool, apart_tally, last_var, at(i, ROWS, r + 1))
                    g.tensor_scalar(TB["bvar"][r][:], TB["bmv"][r][:, :, 1], EPS_OUT, None, ALU.add).then_inc(pool_chain, 1)
                    pool.wait_ge(pool_chain, at(i, ROWS, 8 + LNS * B + r + 1))
                    g.tensor_tensor(TB["brstd"][r][:], TB["bvar"][r][:], pow_c[:], ALU.pow).then_inc(last_rstd, 1)

        @block.tensor
        def _(pe):
            mm = pe.matmul
            pe.wait_ge(w_in, 16 * N_W)
            pe.wait_ge(pool_const, 2)
            for h in range(2):
                mm(ps[:, h, :], smallw[:, 0:128], up[:, 512 * h:512 * h + 512], start=True, stop=True)
                mm(ps[0:96, 2 + h, :], smallw[:, 128:224], kup[:, 512 * h:512 * h + 512], start=True, stop=True)
                mm(ps[0:96, 4 + h, :], smallw[:, 224:320], vup[:, 512 * h:512 * h + 512], start=True, stop=True)
            for j in range(PAIRS):
                last = mm(ps[:, 6 + j // 4, 128 * (j % 4):128 * (j % 4) + 128], odT[:, 128 * j:128 * j + 128],
                          smallw[:, 320:448], start=True, stop=True)
            last.then_inc(fold_psum, 1)
            pe.wait_ge(fold_done, 4)
            for j in range(PAIRS):
                mm(ps[:, 0, 32 * j:32 * j + 32], wki[:, 128 * j:128 * j + 128], ctx_ipa, start=True, stop=True)
            for j in range(PAIRS):
                mm(ps[:, 0, 256 + 32 * j:256 + 32 * j + 32], wvi[:, 128 * j:128 * j + 128], ctx_ipa, start=True, stop=True)
            for j in range(PAIRS):
                last = pe.transpose(ps[:, 1 + j // 4, 128 * (j % 4):128 * (j % 4) + 128], wq[:, 128 * j:128 * j + 128], ident[:])
            last.then_inc(fold_psum, 1)
            pe.wait_ge(fold_done, 10)
            pe.wait_ge(dve_const, 1)
            for j in range(PAIRS):
                mm(ps[:, 3, 64 * j:64 * j + 64], wqT[:, j, :], kblk[:, j, :, :], start=True, stop=True)
            for j in range(PAIRS):
                last = mm(ps[0:64, 4 + j // 4, 128 * (j % 4):128 * (j % 4) + 128], vblk[:, j, :, :], wo[:, j, :],
                          start=True, stop=True)
            last.then_inc(fold_psum, 1)
            mm(ps[:, 6, 0:128], tmp128[:], xw[:, 3, :], start=True, stop=True).then_inc(fold_psum, 1)
            pe.wait_ge(fold_done, 16)
            pe.wait_ge(w_moe_in, 32)

            def transpose_xn(i, l, bank):
                pe.wait_ge(xn_ready, at(i, LNS, l + 1))
                for t in range(TT):
                    last = pe.transpose(ps[:, bank, 128 * t:128 * t + 128], xn[:, t, :], ident[:])
                last.then_inc(xnT_psum, 1)
                pe.wait_ge(xnT_ready, at(i, 3, l + 1))

            def l0(i):
                pe.wait_ge(x3T_done, at(i, 1, 1))
                transpose_xn(i, 0, 6)
                for t in range(TT):
                    last = mm(ps[:, 7, 64 * t:64 * t + 64], xnT[:, 128 * t:128 * t + 128],
                              g_ipa[:, bass.ds(i, 1), :], start=True, stop=True)
                last.then_inc(ipa_scores, 1)
                pe.wait_ge(ctx_in, at(i, 64, 64))
                for n in range(20):
                    bank = 2 + n % 4
                    if n >= 4:
                        if n - 4 < 12:
                            pe.wait_ge(lo_done, at(i, 12, n - 3))
                        else:
                            pe.wait_ge(hi_done, at(i, 20, n - 3))
                    if n < 4:
                        for h in range(2):
                            j = 2 * n + h
                            last = mm(ps[:, bank, N * h:N * h + N], wq[:, 128 * j:128 * j + 128], xnT[:], start=True, stop=True)
                    elif n < 12:
                        j = n - 4
                        last = mm(ps[:, bank, :], wk[:, 128 * j:128 * j + 128], ctx0[:], start=True, stop=True)
                    else:
                        k, h = divmod(n - 12, 2)
                        last = mm(ps[:, bank, :], ctx0[:, 128 * k:128 * k + 128], wv[:, 512 * h:512 * h + 512], start=True, stop=True)
                    last.then_inc(fill_full, 1)

                def row_max(h):
                    p0 = 64 * (h % 2)
                    if h >= 1:
                        pe.wait_ge(max_done, at(i, H0, h))
                    if h % GH == 0 and h:
                        pe.wait_ge(nmT_ready, at(i, H0 // GH, h // GH))
                    for t in range(TT):
                        last = mm(ps[:, t, 0:SM], q12[p0:p0 + 64, 0, h // 2, 128 * t:128 * t + 128],
                                  k12[p0:p0 + 64, 0, h // 2, 0:SM], start=True, stop=True)
                    last.then_inc(max_full, 1)

                def maxima_T(gr):
                    pe.wait_ge(nm_parts, at(i, H0 // GH, gr + 1))
                    for t in range(TT):
                        last = pe.transpose(ps[:, 0, 128 * t:128 * t + 128], mxs[:, t, :].bitcast(F32), ident[:])
                    last.then_inc(nmT_psum, 1)

                def scores(h):
                    p0 = 64 * (h % 2)
                    if h % GH == 0:
                        pe.wait_ge(nmT_ready, at(i, H0 // GH, h // GH + 1))
                    if h >= 2:
                        pe.wait_ge(probs_ready, at(i, H0, h - 1))
                    elif h == 0:
                        pe.wait_ge(hi_done, at(i, 20, 20))
                    for k in range(KT):
                        o = ps[:, 2 + 2 * (h % 2) + k // 2, N * (k % 2):N * (k % 2) + N]
                        for n, (a, b) in enumerate(((0, 0), (0, 1), (1, 0))):
                            mm(o, k12[p0:p0 + 64, a, h // 2, 128 * k:128 * k + 128], q12[p0:p0 + 64, b, h // 2, :],
                               start=(n == 0), stop=False)
                        last = mm(o, sel4[p0:p0 + 64, h % GH, :], nmT[p0:p0 + 64, :], start=False, stop=True)
                    last.then_inc(score_full, 1)

                def values(h):
                    p0 = 64 * (h % 2)
                    bank = 6 + (h // 2) % 2
                    if h % 2 == 0 and h >= 4:
                        pe.wait_ge(pair_out, at(i, PAIRS, h // 2 - 1))
                    pe.wait_ge(probs_ready, at(i, H0, h + 1))
                    if h == 0:
                        pe.wait_ge(xnT_ready, at(i, 3, 1))
                    if h == 2:
                        pe.wait_ge(ipa_shifted, at(i, 1, 1))
                    for k in range(KT):
                        kr = min(128, SM - 128 * k)
                        pr = probs[0:kr, h % 2, N * k:N * k + N]
                        mm(ps[p0:p0 + 64, bank, 0:N], v0[0:kr, k, 64 * h:64 * h + 64], pr,
                           start=(k == 0), stop=(k == KT - 1), skip_group_check=True)
                        last = mm(ps[p0:p0 + 64, bank, N:2 * N], ones[0:kr, 0:64], pr,
                                  start=False, stop=(k == KT - 1), skip_group_check=True)
                    last.then_inc(pv_head, 1)

                for h in range(GH):
                    row_max(h)
                maxima_T(0)
                for h in range(H0):
                    if h + GH < H0:
                        row_max(h + GH)
                    scores(h)
                    if h >= 1:
                        values(h - 1)
                    if h % GH == GH - 1 and h // GH + 1 < H0 // GH:
                        maxima_T(h // GH + 1)
                values(H0 - 1)
                wait_apart(pe, apart_tally, ipa_probs, at(i, 1, 1))
                for t in range(TT):
                    last = pe.transpose(ps[0:64, 0, 128 * t:128 * t + 128], pi[:, t, :], ident[:])
                last.then_inc(ipa_T, 1)
                pe.wait_ge(ipa_ready, at(i, 1, 1))
                pe.wait_ge(pair_out, at(i, PAIRS, PAIRS))
                for t in range(TT):
                    for j in range(PAIRS):
                        mm(ps[:, 1, 128 * t:128 * t + 128], outT[:, j, 128 * t:128 * t + 128], wo[:, j, :],
                           start=(j == 0), stop=False)
                    last = mm(ps[:, 1, 128 * t:128 * t + 128], piT[:, 128 * t:128 * t + 128], vw[:], start=False, stop=True)
                last.then_inc(y_full, 1)

            def moe(i):
                transpose_xn(i, 1, 6)
                for t in range(TT):
                    last = mm(ps[:, 7, 8 * t:8 * t + 8], xnT[:, 128 * t:128 * t + 128], cst[:, C_WR:C_WR + 8], start=True, stop=True)
                last.then_inc(logits_full, 1)

                def hidden(n):
                    if n >= 4:
                        pe.wait_ge(hs_ready, at(i, 16, n - 3))
                    for h in range(2):
                        c = 2 * n + h
                        last = mm(ps[:, n % 4, N * h:N * h + N], w1T[:, 128 * c:128 * c + 128], xnT[:], start=True, stop=True)
                    last.then_inc(h_full, 1)

                def project(n):
                    pe.wait_ge(hs_ready, at(i, 16, n + 1))
                    if n == 8:
                        pe.wait_ge(gap_ready, at(i, 1, 1))
                    for h in range(2):
                        c = 2 * n + h
                        e = c // 4
                        for t in range(TT):
                            last = mm(ps[:, 4 + 2 * (e // 4) + t, 128 * (e % 4):128 * (e % 4) + 128],
                                      hs[:, n % 3, h, 128 * t:128 * t + 128], w2T[:, c, :],
                                      start=(c % 4 == 0), stop=(c % 4 == 3))
                    last.then_inc(w2_done, 1)
                    if n % 8 == 7:
                        pass

                hidden(0)
                hidden(1)
                for n in range(16):
                    if n + 2 < 16:
                        hidden(n + 2)
                    project(n)

            def cross(i):
                transpose_xn(i, 2, 6)
                pe.wait_ge(ctx_in, at(i, 64, 64))
                mm(ps[:, 0, 0:N], xw[:, 0, :], xnT[:], start=True, stop=True)
                mm(ps[:, 1, :], xw[0:96, 1, :], ctxT[:], start=True, stop=True).then_inc(x_proj, 1)
                for k in range(KT):
                    last = mm(ps[:, 2, 128 * k:128 * k + 128], ctxT[:, 128 * k:128 * k + 128], xw[0:96, 2, :], start=True, stop=True)
                last.then_inc(ctx_used, 1)
                mm(ps[:, 3, 0:128], ident[:], ident[:], start=True, stop=True).then_inc(x_proj, 1)
                pe.wait_ge(x_stacks_in, at(i, 128, 128))
                for h in range(H1):
                    if h >= 1:
                        pe.wait_ge(x_max_done, at(i, H1, h))
                    else:
                        pe.wait_ge(x_lo, at(i, 2, 2))
                    for t in range(TT):
                        last = mm(ps[:, t, :], qst[:, h, 128 * t:128 * t + 128], kst[:, h, :], start=True, stop=True)
                    last.then_inc(x_max_full, 1)
                pe.wait_ge(x_nm_parts, at(i, 1, 1))
                for t in range(TT):
                    last = pe.transpose(ps[:, 0, 128 * t:128 * t + 128], mxs[:, t, :].bitcast(F32), ident[:])
                last.then_inc(x_nmT_psum, 1)
                pe.wait_ge(x_nmT_ready, at(i, 1, 1))

                def scores(n):
                    h = ORDER8[n]
                    if n >= 2:
                        pe.wait_ge(x_probs_ready, at(i, H1, n - 1))
                    elif n == 0:
                        pe.wait_ge(x_v, at(i, 1, 1))
                    for k in range(KT):
                        o = ps[:, 2 + 2 * (n % 2) + k // 2, N * (k % 2):N * (k % 2) + N]
                        mm(o, kst[:, h, 128 * k:128 * k + 128], qst[:, h, :], start=True, stop=False)
                        last = mm(o, sel8[:, h, :], nmT[0:64, :], start=False, stop=True)
                    last.then_inc(x_score_full, 1)

                def values(n):
                    h = ORDER8[n]
                    c0 = 32 * (h // 2)
                    pe.wait_ge(x_probs_ready, at(i, H1, n + 1))
                    for k in range(KT):
                        pr = probs[:, n % 2, N * k:N * k + N]
                        mm(ps[c0:c0 + 32, 6, 0:N], vpx[:, k, h, :], pr, start=(n < 4 and k == 0),
                           stop=(n >= 4 and k == KT - 1), skip_group_check=True, tile_position=(0, c0))
                        last = mm(ps[c0:c0 + 32, 6, N:2 * N], sumsel[:, h % 2, :], pr, start=False,
                                  stop=(n >= 4 and k == KT - 1), skip_group_check=True, tile_position=(0, c0))
                    last.then_inc(x_pv, 1)

                for n in range(H1):
                    scores(n)
                    if n >= 1:
                        values(n - 1)
                values(H1 - 1)
                pe.wait_ge(x_ctxo, at(i, 1, 1))
                for t in range(TT):
                    last = mm(ps[:, 7, 128 * t:128 * t + 128], outT[:, 0, 128 * t:128 * t + 128], xw[:, 3, :], start=True, stop=True)
                last.then_inc(x_y, 1)
                pe.wait_ge(xn_ready, at(i, LNS, LNS))
                for t in range(TT):
                    last = pe.transpose(ps[:, 6, 128 * t:128 * t + 128], xn[:, t, :], ident[:])
                last.then_inc(x3T_psum, 1)

            with pe.Fori(0, B) as i:
                l0(i)
                moe(i)
                cross(i)
            pe.wait_ge(x3T_done, B + 1)
            mm(ps[:, 5, 0:128], ident[:], ident[:], start=True, stop=True).then_inc(loop_a_done, 1)

            raw, fw, fb = TB["raw"], TB["fw"], TB["fb"]
            pe.wait_ge(w_b_in, 16 * N_B)
            for c in range(NODES):
                if c >= 4:
                    pe.wait_ge(fb_done, c - 3)
                b = c % 4
                for n in range(3):
                    mm(ps[:, b, 128 * n:128 * n + 128], raw[:, c, n, :], raw[:, c, 4 + n, :], start=True, stop=True)
                for n in range(3):
                    last = mm(ps[:, b, 384 + n:385 + n], raw[:, c, 4 + n, :], cst[:, C_BE + EDGES[c][0][n]:C_BE + EDGES[c][0][n] + 1],
                              start=True, stop=True)
                last.then_inc(fb_psum, 1)
            pe.wait_ge(fb_done, NODES)
            for c in range(NODES):
                last = mm(ps[:, 5, c:c + 1], raw[:, c, 7, :], fb[:, c, 2:3], start=True, stop=True)
            last.then_inc(fb_psum, 1)
            pe.wait_ge(fb_done, NODES + 1)
            pe.wait_ge(pool_const, 3)

            def proj_qk(i, s):
                c, r = divmod(s, ROWS)
                nq, nk, nv = EDGES[c][1]
                if c == 0:
                    pe.wait_ge(rows_in, at(i, ROWS, r + 1))
                else:
                    pe.wait_ge(n_node, at(i, STEPS, s - ROWS + 1))
                nodes = TB["nodes"][r]
                mm(ps[:, 4 + r, 0:N], fw[:, c, 0, :], nodes[:, nq, :], start=True, stop=True)
                mm(ps[:, 4 + r, N:2 * N], fw[:, c, 1, :], nodes[:, nk, :], start=True, stop=True).then_inc(n_proj, 1)

            def proj_v(i, s):
                c, r = divmod(s, ROWS)
                nq, nk, nv = EDGES[c][1]
                nodes = TB["nodes"][r]
                pe.wait_ge(n_lo, at(i, STEPS, s + 1))
                for k in range(TT):
                    mm(ps[:, 4 + r, 128 * k:128 * k + 128], nodes[:, nv, 128 * k:128 * k + 128], fw[:, c, 2, :], start=True, stop=True)
                mm(ps[:, 4 + r, N:2 * N], fw[:, c, 3, :], nodes[:, nq, :], start=True, stop=True).then_inc(n_v_full, 1)

            def row_max(i, s, n):
                c, r = divmod(s, ROWS)
                q, k = TB["bqst"][r], TB["bkst"][r]
                if n == 0:
                    pe.wait_ge(n_stacks_in[r], at(i, 128 * NODES, 128 * (c + 1)))
                    pe.wait_ge(n_zero, at(i, STEPS, s + 1))
                    if s:
                        pe.wait_ge(n_nmT, at(i, 2 * STEPS, 2 * s))
                if H1 * s + n >= 2:
                    pe.wait_ge(n_max_done, at(i, STEPS * H1, H1 * s + n - 1))
                for t in range(TT):
                    last = mm(ps[:, n % 2, N * t:N * t + N], q[:, n, 128 * t:128 * t + 128], k[:, n, :], start=True, stop=True)
                last.then_inc(n_max_full, 1)

            def maxima_T(i, s):
                pe.wait_ge(n_nm_parts, at(i, STEPS, s + 1))
                for t in range(TT):
                    last = pe.transpose(ps[:, 0, 128 * t:128 * t + 128], TB["bmxs"][s % ROWS][:, t, :].bitcast(F32), ident[:])
                last.then_inc(n_nmT_psum, 1)

            def scores(i, s, n):
                h = ORDER8[n]
                q, k = TB["bqst"][s % ROWS], TB["bkst"][s % ROWS]
                if n % 4 == 0:
                    pe.wait_ge(n_nmT, at(i, 2 * STEPS, 2 * s + n // 4 + 1))
                if H1 * s + n >= 2:
                    pe.wait_ge(n_probs, at(i, STEPS * H1, H1 * s + n - 1))
                for kt in range(TT):
                    last = mm(ps[:, 2 + n % 2, N * kt:N * kt + N], k[:, h, 128 * kt:128 * kt + 128], q[:, h, :], start=True, stop=True)
                last.then_inc(n_score, 1)

            def values(i, s, half):
                r = s % ROWS
                pe.wait_ge(n_probs, at(i, STEPS * H1, H1 * s + 4 * half + 4))
                if half == 0:
                    pe.wait_ge(n_v, at(i, STEPS, s + 1))
                for u in range(2):
                    for kt in range(TT):
                        for j in range(4):
                            h = 2 * j + half
                            o = ps[32 * j:32 * j + 32, 4 + r, N * u:N * u + N]
                            w = TB["vpad"][r][:, kt, h, :] if u == 0 else sumsel[:, half, :]
                            last = mm(o, w, TB["probs"][:, h, N * kt:N * kt + N], start=(half == 0 and u == 0 and kt == 0),
                                      stop=(half == 1 and kt == TT - 1), skip_group_check=True, tile_position=(0, 32 * j))
                last.then_inc(n_pv, 1)

            def through_wo(i, s):
                c, r = divmod(s, ROWS)
                pe.wait_ge(n_ctxo, at(i, STEPS, s + 1))
                mm(ps[:, 4 + r, 0:N], fw[:, c, 4, :], TB["bctx"][r][:], start=True, stop=True).then_inc(n_wo, 1)

            with pe.Fori(0, TURNS_B) as i:
                for s in range(ROWS):
                    proj_qk(i, s)
                for s in range(ROWS):
                    proj_v(i, s)
                for n in range(H1):
                    row_max(i, 0, n)
                maxima_T(i, 0)
                for s in range(STEPS):
                    def both(n):
                        scores(i, s, n)
                        if s + 1 < STEPS:
                            row_max(i, s + 1, n)
                    both(0)
                    both(1)
                    if s >= 2 and s + 2 < STEPS:
                        proj_v(i, s + 2)
                    if s:
                        values(i, s - 1, 1)
                    both(2)
                    both(3)
                    values(i, s, 0)
                    both(4)
                    both(5)
                    if s:
                        through_wo(i, s - 1)
                    both(6)
                    both(7)
                    if s and s + 3 < STEPS:
                        proj_qk(i, s + 3)
                    if s + 1 < STEPS:
                        maxima_T(i, s + 1)
                values(i, STEPS - 1, 1)
                through_wo(i, STEPS - 1)
                for r in range(ROWS):
                    pe.wait_ge(n_node, at(i, STEPS, STEPS - ROWS + r + 1))
                    for t in range(TT):
                        last = pe.transpose(ps[:, 4 + r, N + 128 * t:N + 128 * t + 128], TB["nodes"][r][:, NODES, 128 * t:128 * t + 128], ident[:])
                    last.then_inc(last_T, 1)

        @block.scalar
        def _(act):
            a = nc.scalar
            act.wait_ge(w_in, 16 * N_W)
            a.activation(tanh_g[:], cst[:, C_GX:C_GX + 4], ACT.Tanh).then_inc(gates_tanh, 1)
            act.sem_inc(x3T_done, 1)

            def l0(i):
                act.wait_ge(xnT_psum, at(i, 3, 1))
                a.copy(xnT[:], ps[:, 6, 0:N]).then_inc(xnT_ready, 1)
                for n in range(20):
                    act.wait_ge(fill_full, at(i, 20, n + 1))
                    src = ps[:, 2 + n % 4, :]
                    if n < 4:
                        dst = q12[:, 0, 2 * n:2 * n + 2, :].rearrange("p a b -> p (a b)")
                    elif n < 12:
                        dst = k12[:, 0, n - 4, :]
                    else:
                        k, h = divmod(n - 12, 2)
                        dst = v0[:, k, 512 * h:512 * h + 512]
                    a.copy(dst, src).then_inc(hi_done, 1)
                    if n == 5:
                        act.wait_ge(ipa_shifted, at(i, 1, 1))
                        a.activation(pi[:, :, :], pi[:, :, :], ACT.Exp, scale=SCALE0).then_inc(ipa_exp, 1)

                def maxima(gr):
                    act.wait_ge(nmT_psum, at(i, H0 // GH, gr + 1))
                    if gr:
                        act.wait_ge(score_full, at(i, H0, GH * gr))
                    a.copy(nmT[:], ps[:, 0, 0:N]).then_inc(nmT_ready, 1)

                maxima(0)
                for h in range(H0):
                    act.wait_ge(score_full, at(i, H0, h + 1))
                    if h >= 2:
                        act.wait_ge(pv_head, at(i, H0, h - 1))
                    b = 2 + 2 * (h % 2)
                    a.activation(probs[:, h % 2, 0:3 * N], ps[:, b:b + 2, :].rearrange("p a b -> p (a b)")[:, 0:3 * N],
                                 ACT.Exp, scale=SCALE0)
                    a.activation(probs[0:SM - 384, h % 2, 3 * N:4 * N], ps[0:SM - 384, b + 1, N:2 * N],
                                 ACT.Exp, scale=SCALE0).then_inc(probs_ready, 1)
                    if h % GH == GH - 1 and h // GH + 1 < H0 // GH:
                        maxima(h // GH + 1)
                act.wait_ge(ipa_T, at(i, 1, 1))
                a.copy(piT[:], ps[0:64, 0, 0:N]).then_inc(ipa_ready, 1)

            def moe(i):
                act.wait_ge(xnT_psum, at(i, 3, 2))
                a.copy(xnT[:], ps[:, 6, 0:N]).then_inc(xnT_ready, 1)
                act.wait_ge(gap_ready, at(i, 1, 1))
                a.activation(gw[:, 1, :], gw[:, 0, :], ACT.Exp).then_inc(gap_exp, 1)
                for n in range(16):
                    act.wait_ge(h_full, at(i, 16, n + 1))
                    if n >= 2:
                        act.wait_ge(hs_ready, at(i, 16, n - 1))
                    a.activation(th[:, n % 2, :], ps[:, n % 4, :], ACT.Tanh, scale=0.5).then_inc(tanh_done, 1)

            def cross(i):
                act.wait_ge(xnT_psum, at(i, 3, 3))
                a.copy(xnT[:], ps[:, 6, 0:N]).then_inc(xnT_ready, 1)
                act.wait_ge(x_proj, at(i, 2, 1))
                a.activation(qx12[:, 0, :], ps[:, 0, 0:N], ACT.Identity, bias=cst[:, C_BQ:C_BQ + 1]).then_inc(x_hi, 1)
                a.activation(kx12[:, 0, :], ps[:, 1, :], ACT.Identity, bias=cst[:, C_BK:C_BK + 1]).then_inc(x_hi, 1)
                act.wait_ge(x_proj, at(i, 2, 2))
                for o in range(2):
                    for k in range(KT):
                        last = a.copy(vpx[:, k, :, :].rearrange("p (j e) c -> p j e c", e=2)[:, :, o, 16 * o:16 * o + 16],
                                      ps[:, 2, 128 * k:128 * k + 128].rearrange("p (j e c) -> p j e c", e=2, c=16)[:, :, o, :])
                last.then_inc(x_v, 1)
                act.wait_ge(x_nmT_psum, at(i, 1, 1))
                a.copy(nmT[:], ps[:, 0, 0:N]).then_inc(x_nmT_ready, 1)
                for n in range(H1):
                    act.wait_ge(x_score_full, at(i, H1, n + 1))
                    if n >= 2:
                        act.wait_ge(x_pv, at(i, H1, n - 1))
                    b = 2 + 2 * (n % 2)
                    a.activation(probs[:, n % 2, :], ps[:, b:b + 2, :].rearrange("p a b -> p (a b)"),
                                 ACT.Exp, scale=SCALE1).then_inc(x_probs_ready, 1)
                act.wait_ge(x3T_psum, at(i, 1, 1))
                a.copy(x3T_all[:, bass.ds(i, 1), :], ps[:, 6, 0:N]).then_inc(x3T_done, 1)

            with act.Fori(0, B) as i:
                l0(i)
                moe(i)
                cross(i)
            act.wait_ge(x3T_done, B + 1)
            a.copy(tanh_g[:, 0:1], tanh_g[:, 0:1]).then_inc(loop_a_done, 1)
            act.wait_ge(fb_done, NODES + 1)
            act.wait_ge(pool_const, 3)
            fb = TB["fb"]
            for r in range(ROWS):
                for u in range(2):
                    a.copy(TB["bkst"][r][64:128, :, 128 * u:128 * u + 128], sel8f[64:128, :, :])
            act.sem_inc(last_out, ROWS)

            def hi_parts(i, s):
                c, r = divmod(s, ROWS)
                act.wait_ge(n_proj, at(i, STEPS, s + 1))
                if c:
                    act.wait_ge(n_parts_out[r], at(i, 16 * NODES, 16 * c))
                for n in range(2):
                    last = a.activation(TB["qk12"][r][:, 0, n, :], ps[:, 4 + r, N * n:N * n + N], ACT.Identity, bias=fb[:, c, n:n + 1])
                last.then_inc(n_hi, 1)

            def v_and_q(i, s):
                c, r = divmod(s, ROWS)
                act.wait_ge(n_v_full, at(i, STEPS, s + 1))
                for o in range(2):
                    a.copy(TB["vpad"][r][:, :, :, :].rearrange("p k (j e) c -> p k j e c", e=2)[:, :, :, o, 16 * o:16 * o + 16],
                           ps[:, 4 + r, 0:TT * D].rearrange("p (k j e c) -> p k j e c", k=TT, e=2, c=16)[:, :, :, o, :])
                a.activation(TB["qn"][r][:], ps[:, 4 + r, N:2 * N], ACT.Identity, bias=fb[:, c, 3:4]).then_inc(n_v, 1)

            def maxima(i, s):
                act.wait_ge(n_nmT_psum, at(i, STEPS, s + 1))
                for half in range(2):
                    dst = TB["bqst"][s % ROWS][64:128, :, :].rearrange("p (j e) q -> p j e q", e=2)[:, :, half, :]
                    src = ps[64:128, 0, 0:N].unsqueeze(1).broadcast_to((64, 4, N))
                    a.copy(dst, src).then_inc(n_nmT, 1)

            def exps(i, s, n):
                act.wait_ge(n_score, at(i, STEPS * H1, H1 * s + n + 1))
                if s and n % 4 == 0:
                    act.wait_ge(n_pv, at(i, 2 * STEPS, 2 * s - 1 + n // 4))
                a.activation(TB["probs"][:, ORDER8[n], :], ps[:, 2 + n % 2, :], ACT.Exp, scale=SCALE1).then_inc(n_probs, 1)

            with act.Fori(0, TURNS_B) as i:
                act.wait_ge(last_out, at(i, ROWS, ROWS))
                for r in range(ROWS):
                    a.copy(TB["nodes"][r][:, 0, :], x3T_all[:, bass.ds(ROWS * i + r, 1), :]).then_inc(rows_in, 1)
                for s in range(ROWS):
                    hi_parts(i, s)
                for s in range(ROWS):
                    v_and_q(i, s)
                maxima(i, 0)
                for s in range(STEPS):
                    exps(i, s, 0)
                    exps(i, s, 1)
                    if s >= 2 and s + 2 < STEPS:
                        v_and_q(i, s + 2)
                    for n in range(2, H1):
                        exps(i, s, n)
                    if s and s + 3 < STEPS:
                        hi_parts(i, s + 3)
                    if s + 1 < STEPS:
                        maxima(i, s + 1)

        @block.vector
        def _(dve):
            v = nc.vector
            chain = [0]

            def link(turn, per_turn, base, ins):
                chain[0] += 1
                ins.then_inc(dve_chain, 1)
                dve.wait_ge(dve_chain, at(turn, per_turn, base + chain[0]))

            def plink(ins):
                link(None, 0, 0, ins)

            v.memset(kblk, 0.0)
            v.memset(vblk, 0.0)
            dve.wait_ge(w_in, 16 * N_W)
            plink(v.tensor_scalar(cst[:, C_QA:C_OA + 1], cst[:, C_QA:C_OA + 1], 1.0 / RANK, None, ALU.mult))
            dve.wait_ge(gates_tanh, 1)
            dve.wait_ge(pool_const, 2)
            v.tensor_scalar(boT[:], cst[:, C_BO0:C_BO0 + D], tanh_g[:, 0:1], None, ALU.mult)
            v.tensor_scalar(gb[:, 0, :], cst[:, C_LG:C_LG + D], tanh_g[:, 3:4], None, ALU.mult)
            v.tensor_scalar(gb[:, 1, :], cst[:, C_LB:C_LB + D], tanh_g[:, 3:4], None, ALU.mult)
            v.tensor_scalar(xw[:, 3, :], xw[:, 3, :], tanh_g[:, 1:2], None, ALU.mult)
            v.tensor_scalar(xrow[:], cst[:, C_BO1:C_BO1 + D], tanh_g[:, 1:2], None, ALU.mult)
            v.tensor_scalar(tmp128[:], ones[:], cst[:, C_BV:C_BV + 1], None, ALU.mult).then_inc(dve_const, 1)
            dve.wait_ge(fold_psum, 1)
            v.scalar_tensor_tensor(wq[:], ps[:, 0:2, :].rearrange("p a b -> p (a b)"), cst[:, C_QA:C_QA + 1], wq[:],
                                   ALU.mult, ALU.add).then_inc(fold_done, 1)
            v.scalar_tensor_tensor(wk[:], ps[0:96, 2:4, :].rearrange("p a b -> p (a b)"), cst[0:96, C_KA:C_KA + 1], wk[:],
                                   ALU.mult, ALU.add).then_inc(fold_done, 1)
            v.scalar_tensor_tensor(wv[:], ps[0:96, 4:6, :].rearrange("p a b -> p (a b)"), cst[0:96, C_VA:C_VA + 1], wv[:],
                                   ALU.mult, ALU.add).then_inc(fold_done, 1)
            wo_f = wo[:, :, :].rearrange("p a b -> p (a b)")
            plink(v.scalar_tensor_tensor(wo_f, ps[:, 6:8, :].rearrange("p a b -> p (a b)"), cst[:, C_OA:C_OA + 1], wo_f,
                                         ALU.mult, ALU.add))
            v.tensor_scalar(wo_f, wo_f, tanh_g[:, 0:1], None, ALU.mult).then_inc(fold_done, 1)
            dve.wait_ge(fold_psum, 2)
            for s in range(2):
                rows = slice(64 * s, 64 * s + 64)
                v.tensor_copy(kblk[rows, :, s, :], ps[rows, 0, 0:256].rearrange("p (j c) -> p j c", c=32)).then_inc(fold_done, 1)
                v.tensor_copy(vblk[rows, :, s, :], ps[rows, 0, 256:512].rearrange("p (j c) -> p j c", c=32)).then_inc(fold_done, 1)
            for h in range(2):
                v.tensor_copy(wqT[:, 4 * h:4 * h + 4, :], ps[:, 1 + h, :].rearrange("p (j c) -> p j c", j=4)).then_inc(fold_done, 1)
            dve.wait_ge(fold_psum, 3)
            v.tensor_copy(g_ipa[:, :, :].rearrange("p b (t h) -> p h b t", t=IPA),
                          ps[:, 3, :].rearrange("p (h b t) -> p h b t", b=B, t=IPA)).then_inc(fold_done, 1)
            for h in range(2):
                v.tensor_copy(vwsb[:, 4 * h:4 * h + 4, :], ps[0:64, 4 + h, :].rearrange("p (j c) -> p j c", j=4)).then_inc(fold_done, 2)
            dve.wait_ge(fold_psum, 4)
            v.tensor_tensor(xrow[:], ps[:, 6, 0:128], xrow[:], ALU.add).then_inc(fold_done, 1)
            pro = chain[0]
            CH = CH_DVE_A

            def lnk(i, ins, apart=False):
                chain[0] += 1
                ins.then_inc(dve_chain, 1)
                if apart:
                    wait_apart(dve, apart_tally, dve_chain, at(i, CH, chain[0]))
                else:
                    dve.wait_ge(dve_chain, at(i, CH, chain[0]))

            def layernorm(i, l, src):
                for t in range(TT):
                    ins = v.bn_stats(st6[:, t, :], src(t))
                lnk(i, ins, apart=True)
                for t in range(TT):
                    ins = v.bn_aggr(mv[:, t, :], st6[:, t, :])
                ins.then_inc(ln_var, 1)
                dve.wait_ge(ln_rstd, at(i, LNS, l + 1))
                for t in range(TT):
                    ins = v.tensor_scalar(xn[:, t, :], src(t), mv[:, t, 0:1], rstd[:, t:t + 1], ALU.subtract, ALU.mult)
                ins.then_inc(xn_ready, 1)

            def l0(i):
                x_b = x_all[:, bass.ds(TT * i, TT), :]
                lnk(i, v.tensor_copy(xs[:, :, :], x_b))
                layernorm(i, 0, lambda t: xs[:, t, :])
                dve.wait_ge(ipa_scores, at(i, 1, 1))
                s4 = ps[:, 7, 0:TT * 64].rearrange("p (a t h) -> p a h t", t=IPA, a=TT)
                pi4 = pi[:, :, :].rearrange("p a (t h) -> p a h t", t=IPA)
                over_t = lambda x: x.rearrange("p (a h) -> p a h", a=TT).unsqueeze(3).broadcast_to((128, TT, H0, IPA))
                lnk(i, v.tensor_reduce(pis[:, 0, :], s4, AX.X, ALU.max))
                v.tensor_tensor(pi4, s4, over_t(pis[:, 0, :]), ALU.subtract).then_inc(ipa_shifted, 1)
                for n in range(12):
                    if n == 8:
                        dve.wait_ge(ipa_exp, at(i, 1, 1))
                        lnk(i, v.tensor_reduce(pis[:, 0, :], pi4, AX.X, ALU.add))
                        lnk(i, v.reciprocal(pis[:, 1, :], pis[:, 0, :]))
                        v.tensor_tensor(pi4, pi4, over_t(pis[:, 1, :]), ALU.mult).then_inc(ipa_probs, 1)
                    dve.wait_ge(hi_done, at(i, 20, n + 1))
                    src = ps[:, 2 + n % 4, :]
                    if n < 4:
                        hi, lo = (q12[:, p, 2 * n:2 * n + 2, :].rearrange("p a b -> p (a b)") for p in range(2))
                    else:
                        hi, lo = (k12[:, p, n - 4, :] for p in range(2))
                    v.tensor_tensor(lo, src, hi.bitcast(F32), ALU.subtract).then_inc(lo_done, 1)

                def row_max(h):
                    dve.wait_ge(max_full, at(i, H0, h + 1))
                    ins = v.tensor_reduce(nm[:, :, h:h + 1], ps[:, 0:2, 0:SM], AX.X, ALU.max, negate=True)
                    ins.then_inc(max_done, 1)
                    if h % GH == GH - 1:
                        gr = h // GH
                        dve.wait_ge(max_done, at(i, H0, h + 1))
                        if gr:
                            dve.wait_ge(nmT_psum, at(i, H0 // GH, gr))
                        src = nm[:, :, GH * gr:GH * gr + GH]
                        hi = mxs[:, :, :].rearrange("p t (a b) -> p t a b", a=2)[:, :, :, 0:GH]
                        lo = mxs[:, :, :].rearrange("p t (a b) -> p t a b", a=2)[:, :, :, 32:32 + GH]
                        srcb = src.unsqueeze(2).broadcast_to((128, TT, 2, GH))
                        lnk(i, v.tensor_copy(hi, srcb))
                        v.tensor_tensor(lo, srcb, hi.bitcast(F32), ALU.subtract).then_inc(nm_parts, 1)

                def pair(j):
                    dve.wait_ge(pv_head, at(i, H0, 2 * j + 2))
                    b = 6 + j % 2
                    if j:
                        dve.wait_ge(pair_out, at(i, PAIRS, j))
                    lnk(i, v.reciprocal(rsum[:], ps[:, b, N:2 * N]))
                    v.tensor_tensor(outT[:, j, :], ps[:, b, 0:N], rsum[:], ALU.mult).then_inc(pair_out, 1)

                for h in range(GH):
                    row_max(h)
                for h in range(H0):
                    if h + GH < H0:
                        row_max(h + GH)
                    if h >= 3 and h % 2 == 1:
                        pair(h // 2 - 1)
                pair(PAIRS - 1)
                dve.wait_ge(y_full, at(i, 1, 1))
                y = ps[:, 1, 0:TT * D].rearrange("p (t d) -> p t d", t=TT)
                lnk(i, v.tensor_tensor(xs[:, :, :], y, xs[:, :, :], ALU.add))
                lnk(i, v.tensor_tensor(xs[:, :, :], xs[:, :, :], boT[:].unsqueeze(1).broadcast_to((128, TT, D)), ALU.add))

            def moe(i):
                layernorm(i, 1, lambda t: xs[:, t, :])
                dve.wait_ge(logits_full, at(i, 1, 1))
                lnk(i, v.tensor_copy(lg[:, :, :], ps[:, 7, 0:TT * E].rearrange("p (t e) -> p t e", t=TT)), apart=True)
                for t in range(TT):
                    ins = v.max(top[:, t, :], lg[:, t, :])
                lnk(i, ins)
                v.tensor_tensor(gw[:, 0, :], top[:, :, 1], top[:, :, 0], ALU.subtract).then_inc(gap_ready, 1)
                for t in range(TT):
                    ins = v.max_index(topi[:, t, :], top[:, t, :], lg[:, t, :])
                lnk(i, ins)
                lnk(i, v.tensor_copy(topf[:, :, :], topi[:, :, :]))
                for t in range(TT):
                    v.tensor_scalar(gate[:, t, :], iota8[:], topf[:, t, 0:1], None, ALU.is_equal)
                    ins = v.tensor_scalar(gate2[:, t, :], iota8[:], topf[:, t, 1:2], None, ALU.is_equal)
                dve.wait_ge(gap_exp, at(i, 1, 1))
                lnk(i, v.tensor_scalar(gw[:, 2, :], gw[:, 1, :], 1.0, None, ALU.add))
                lnk(i, v.reciprocal(gw[:, 3, :], gw[:, 2, :]))
                lnk(i, v.tensor_scalar(gw[:, 4, :], gw[:, 3, :], tanh_g[:, 2:3], 0.5, ALU.mult, ALU.mult))
                lnk(i, v.tensor_tensor(gw[:, 5, :], gw[:, 4, :], gw[:, 1, :], ALU.mult))
                for t in range(TT):
                    ins = v.tensor_scalar(gate[:, t, :], gate[:, t, :], gw[:, 4, t:t + 1], None, ALU.mult)
                lnk(i, ins)
                for t in range(TT):
                    ins = v.scalar_tensor_tensor(gate[:, t, :], gate2[:, t, :], gw[:, 5, t:t + 1], gate[:, t, :], ALU.mult, ALU.add)
                lnk(i, ins)

                def experts(g):
                    dve.wait_ge(w2_done, at(i, 16, 8 * g + 8))
                    for e in range(4 * g, 4 * g + 4):
                        for t in range(TT):
                            y = ps[:, 4 + 2 * g + t, 128 * (e % 4):128 * (e % 4) + 128]
                            ins = v.scalar_tensor_tensor(xs[:, t, :], y, gate[:, t, e:e + 1], xs[:, t, :], ALU.mult, ALU.add)
                        lnk(i, ins)

                for n in range(16):
                    dve.wait_ge(tanh_done, at(i, 16, n + 1))
                    if n >= 3:
                        dve.wait_ge(w2_done, at(i, 16, n - 2))
                    v.scalar_tensor_tensor(hs[:, n % 3, :, :].rearrange("p a b -> p (a b)"), th[:, n % 2, :], 1.0,
                                           ps[:, n % 4, :], ALU.add, ALU.mult).then_inc(hs_ready, 1)
                    if n == 10:
                        experts(0)
                experts(1)

            def cross(i):
                layernorm(i, 2, lambda t: xs[:, t, :])
                dve.wait_ge(x_hi, at(i, 2, 1))
                v.scalar_tensor_tensor(qx12[:, 1, :], ps[:, 0, 0:N], cst[:, C_BQ:C_BQ + 1], qx12[:, 0, :].bitcast(F32),
                                       ALU.add, ALU.subtract).then_inc(x_lo, 1)
                dve.wait_ge(x_hi, at(i, 2, 2))
                v.scalar_tensor_tensor(kx12[:, 1, :], ps[:, 1, :], cst[:, C_BK:C_BK + 1], kx12[:, 0, :].bitcast(F32),
                                       ALU.add, ALU.subtract).then_inc(x_lo, 1)
                for h in range(H1):
                    dve.wait_ge(x_max_full, at(i, H1, h + 1))
                    ins = v.tensor_reduce(nm[:, :, h:h + 1], ps[:, 0:2, :], AX.X, ALU.max, negate=True).then_inc(x_max_done, 1)
                dve.wait_ge(x_max_done, at(i, H1, H1))
                lnk(i, v.tensor_copy(mxs[:, :, 0:H1], nm[:, :, 0:H1]))
                v.tensor_tensor(mxs[:, :, 32:32 + H1], nm[:, :, 0:H1], mxs[:, :, 0:H1].bitcast(F32), ALU.subtract).then_inc(x_nm_parts, 1)
                dve.wait_ge(x_pv, at(i, H1, H1))
                lnk(i, v.reciprocal(rsum[:], ps[:, 6, N:2 * N]))
                v.tensor_tensor(outT[:, 0, :], ps[:, 6, 0:N], rsum[:], ALU.mult).then_inc(x_ctxo, 1)
                dve.wait_ge(x_nmT_psum, at(i, 1, 1))
                v.memset(mxs[:, :, 0:64].bitcast(F32), 0.0)
                dve.wait_ge(x_y, at(i, 1, 1))
                y = ps[:, 7, 0:TT * D].rearrange("p (t d) -> p t d", t=TT)
                lnk(i, v.tensor_tensor(xs[:, :, :], y, xs[:, :, :], ALU.add))
                lnk(i, v.tensor_tensor(xs[:, :, :], xs[:, :, :], xrow[:].unsqueeze(1).broadcast_to((128, TT, D)), ALU.add))
                v.tensor_tensor(x_all[:, bass.ds(TT * i, TT), :], xs[:, :, :],
                                gb[:, 1, :].unsqueeze(1).broadcast_to((128, TT, D)), ALU.add).then_inc(x3_ready, 1)
                layernorm(i, 3, lambda t: xs[:, t, :])
                dve.wait_ge(xn_ready, at(i, LNS, LNS))
                dve.wait_ge(x3T_psum, at(i, 1, 1))

            with dve.Fori(0, B) as i:
                l0(i)
                moe(i)
                cross(i)
                assert chain[0] - pro == CH_DVE_A, f"CH_DVE_A = {chain[0] - pro}"
            chain[0] = pro + CH_DVE_A * B
            dve.wait_ge(x3_ready, B)
            v.memset(nm[:, 0, 0:1], 0.0).then_inc(loop_a_done, 1)

            raw, fw, fb = TB["raw"], TB["fw"], TB["fb"]
            dve.wait_ge(w_b_in, 16 * N_B)
            for c in range(NODES):
                ew = lambda n: cst[:, C_EW + 3 * c + n:C_EW + 3 * c + n + 1]
                aw = cst[:, C_AW + c:C_AW + c + 1]
                dve.wait_ge(fb_psum, c + 1)
                for n in range(3):
                    v.tensor_scalar(fw[:, c, n, :], ps[:, c % 4, 128 * n:128 * n + 128], ew(n), None, ALU.mult)
                    v.tensor_scalar(fb[:, c, n:n + 1], ps[:, c % 4, 384 + n:385 + n], ew(n), None, ALU.mult)
                v.tensor_scalar(fw[:, c, 3, :], raw[:, c, 3, :], ew(0), None, ALU.mult)
                v.tensor_scalar(fb[:, c, 3:4], cst[:, C_BE + EDGES[c][0][0]:C_BE + EDGES[c][0][0] + 1], ew(0), None, ALU.mult)
                v.tensor_scalar(fw[:, c, 4, :], raw[:, c, 7, :], aw, None, ALU.mult).then_inc(fb_done, 1)
            dve.wait_ge(fb_psum, NODES + 1)
            for c in range(NODES):
                ins = v.tensor_scalar(fb[:, c, 4:5], ps[:, 5, c:c + 1], cst[:, C_AW + c:C_AW + c + 1], None, ALU.mult)
            ins.then_inc(fb_done, 1)
            dve.wait_ge(fb_done, NODES + 1)
            dve.wait_ge(pool_const, 3)
            base_b = chain[0]
            CHB = 2 * STEPS + 3 * ROWS

            def lnb(i, ins, apart=False):
                chain[0] += 1
                ins.then_inc(dve_chain, 1)
                if apart:
                    wait_apart(dve, apart_tally, dve_chain, at(i, CHB, chain[0]))
                else:
                    dve.wait_ge(dve_chain, at(i, CHB, chain[0]))

            def lo_parts(i, s):
                c, r = divmod(s, ROWS)
                dve.wait_ge(n_hi, at(i, STEPS, s + 1))
                for n in range(2):
                    ins = v.scalar_tensor_tensor(TB["qk12"][r][:, 1, n, :], ps[:, 4 + r, N * n:N * n + N], fb[:, c, n:n + 1],
                                                 TB["qk12"][r][:, 0, n, :].bitcast(F32), ALU.add, ALU.subtract)
                ins.then_inc(n_lo, 1)

            def row_max(i, s, n):
                dve.wait_ge(n_max_full, at(i, STEPS * H1, H1 * s + n + 1))
                v.tensor_reduce(TB["bnm"][s % ROWS][:, :, n:n + 1], ps[:, n % 2, :].rearrange("p (t k) -> p t k", t=TT), AX.X, ALU.max,
                                negate=True).then_inc(n_max_done, 1)

            def nm_split(i, s):
                bnm, bmx = TB["bnm"][s % ROWS], TB["bmxs"][s % ROWS]
                dve.wait_ge(n_max_done, at(i, STEPS * H1, H1 * s + H1))
                lnb(i, v.tensor_copy(bmx[:, :, 64:64 + H1], bnm[:, :, :]))
                v.tensor_tensor(bmx[:, :, 96:96 + H1], bnm[:, :, :], bmx[:, :, 64:64 + H1].bitcast(F32), ALU.subtract).then_inc(n_nm_parts, 1)

            def normalize(i, s):
                r = s % ROWS
                dve.wait_ge(n_pv, at(i, 2 * STEPS, 2 * s + 2))
                if s:
                    dve.wait_ge(n_ctxo, at(i, STEPS, s))
                lnb(i, v.reciprocal(TB["rs"][:], ps[:, 4 + r, N:2 * N]))
                v.tensor_tensor(TB["bctx"][r][:], ps[:, 4 + r, 0:N], TB["rs"][:], ALU.mult).then_inc(n_ctxo, 1)

            def node(i, s):
                c, r = divmod(s, ROWS)
                dve.wait_ge(n_wo, at(i, STEPS, s + 1))
                v.scalar_tensor_tensor(TB["nodes"][r][:, c + 1, :], ps[:, 4 + r, 0:N], fb[:, c, 4:5], TB["qn"][r][:],
                                       ALU.add, ALU.add).then_inc(n_node, 1)

            def last_ln(i, r):
                dve.wait_ge(last_T, at(i, ROWS, r + 1))
                dve.wait_ge(stored[r], at(i, 16, 16))
                o, bmv = TB["o"][r], TB["bmv"][r]
                src = [ps[:, 4 + r, N + 128 * t:N + 128 * t + 128] for t in range(TT)]
                for t in range(TT):
                    ins = v.bn_stats(TB["bst"][r][:, t, :], src[t])
                lnb(i, ins, apart=True)
                for t in range(TT):
                    ins = v.bn_aggr(bmv[:, t, :], TB["bst"][r][:, t, :])
                ins.then_inc(last_var, 1)
                dve.wait_ge(last_rstd, at(i, ROWS, r + 1))
                for t in range(TT):
                    ins = v.tensor_scalar(o[:, t, :], src[t], bmv[:, t, 0:1], TB["brstd"][r][:, t:t + 1], ALU.subtract, ALU.mult)
                lnb(i, ins)
                lnb(i, v.tensor_tensor(o[:, :, :], o[:, :, :], gb[:, 0, :].unsqueeze(1).broadcast_to((128, TT, D)), ALU.mult))
                v.tensor_tensor(o[:, :, :], o[:, :, :], x_all[:, bass.ds(TT * (ROWS * i + r), TT), :], ALU.add).then_inc(last_out, 1)

            with dve.Fori(0, TURNS_B) as i:
                for s in range(ROWS):
                    lo_parts(i, s)
                for n in range(H1):
                    row_max(i, 0, n)
                nm_split(i, 0)
                for s in range(STEPS):
                    more = s + 1 < STEPS
                    for n in range(4 * more):
                        row_max(i, s + 1, n)
                    if s:
                        normalize(i, s - 1)
                    for n in range(4, 4 + 2 * more):
                        row_max(i, s + 1, n)
                    if s:
                        node(i, s - 1)
                    for n in range(6, 6 + 2 * more):
                        row_max(i, s + 1, n)
                    if more:
                        nm_split(i, s + 1)
                    if s and s + 3 < STEPS:
                        lo_parts(i, s + 3)
                normalize(i, STEPS - 1)
                node(i, STEPS - 1)
                for r in range(ROWS):
                    last_ln(i, r)
                assert chain[0] - base_b == CHB, f"CHB = {chain[0] - base_b}"


def kernel(**inputs):
    import concourse.bacc as bacc
    from concourse.bass_utils import run_bass_kernel_spmd

    I = {k: np.asarray(v) for k, v in inputs.items()}
    tr = lambda a: np.ascontiguousarray(np.swapaxes(a, -1, -2))
    row = lambda a: np.broadcast_to(a.reshape(1, -1), (128, a.size))
    col = lambda a: a.reshape(128, -1)
    cst = np.zeros((128, C_ALL), np.float32)
    for c0, a in (
        (C_GX, row(I["g_xattn"])), (C_GF, row(I["g_ffn"])), (C_QA, row(I["L0_xattn_q_alpha"])),
        (C_KA, row(I["L0_xattn_k_alpha"])), (C_VA, row(I["L0_xattn_v_alpha"])), (C_OA, row(I["L0_xattn_o_alpha"])),
        (C_EW, row(I["L1_ffn_ew"])), (C_AW, row(I["L1_ffn_act_w"])),
        (C_BQ, col(I["L1_xattn_bq"])), (C_BK, col(I["L1_xattn_bk"])), (C_BV, col(I["L1_xattn_bv"])),
        (C_BE, tr(I["L1_ffn_be"])), (C_WR, tr(I["L0_ffn_Wr"])),
        (C_BO0, row(I["L0_xattn_bo"])), (C_BO1, row(I["L1_xattn_bo"])),
        (C_LG, row(I["L1_ffn_ln_g"])), (C_LB, row(I["L1_ffn_ln_b"])),
    ):
        cst[:, c0:c0 + a.shape[1]] = a
    ctx = I["ctx_768"]
    arrays = {
        "cst": cst, "x": I["x"], "ctxT": tr(ctx),
        "ctx_ipaT": np.ascontiguousarray(ctx[:, SM:, :].reshape(B * IPA, CD).T),
        "q_downT": tr(I["L0_xattn_q_down"]), "k_downT": tr(I["L0_xattn_k_down"]), "v_downT": tr(I["L0_xattn_v_down"]),
        "o_downT": tr(I["L0_xattn_o_down"]), "q_up": I["L0_xattn_q_up"], "k_up": I["L0_xattn_k_up"],
        "v_up": I["L0_xattn_v_up"], "o_up": I["L0_xattn_o_up"],
        "Wq": I["L0_xattn_Wq"], "Wk": I["L0_xattn_Wk"], "Wv": I["L0_xattn_Wv"], "Wo": I["L0_xattn_Wo"],
        "Wk_ipa": I["L0_xattn_Wk_ipa"], "Wv_ipa": I["L0_xattn_Wv_ipa"],
        "W1T": np.ascontiguousarray(I["L0_ffn_W1"].transpose(2, 0, 1).reshape(D, E * DFF)),
        "W2T": np.ascontiguousarray(I["L0_ffn_W2"].transpose(0, 2, 1).reshape(E * DFF, D)),
        "xWq": I["L1_xattn_Wq"], "xWk": I["L1_xattn_Wk"], "xWv": I["L1_xattn_Wv"], "xWo": I["L1_xattn_Wo"],
        "We": I["L1_ffn_We"], "WeT": tr(I["L1_ffn_We"]), "bWq": I["L1_ffn_Wq"], "bWk": I["L1_ffn_Wk"],
        "bWv": I["L1_ffn_Wv"], "bWo": I["L1_ffn_Wo"], "ident": np.eye(128, dtype=np.float32),
    }
    nc = bacc.Bacc("TRN2", target_bir_lowering=False, num_devices=1)
    feed, T = {}, {}
    for name, a in arrays.items():
        a = np.ascontiguousarray(a)
        feed[f"in_{name}"] = a
        T[name] = nc.dram_tensor(f"in_{name}", a.shape, mybir.dt.from_np(a.dtype), kind="ExternalInput").ap()
    out = nc.dram_tensor("out_0", (B, N, D), F32, kind="ExternalOutput").ap()
    build(nc, T, out)
    r = run_bass_kernel_spmd(nc, [feed], core_ids=[0])
    return r.results[0]["out_0"]
```

```python
from contextlib import ExitStack

import numpy as np
import concourse.bass as bass
from concourse import mybir

ALU = mybir.AluOpType
ACT = mybir.ActivationFunctionType
AX = mybir.AxisListType
F32 = mybir.dt.float32
F32R = mybir.dt.float32r
U32 = mybir.dt.uint32

B, N, D, S, CD = 8, 256, 128, 512, 96
TT = N // 128
IPA = 4
SM = S - IPA
H0, DH0 = 16, 64
ID0 = H0 * DH0
PAIRS = H0 // 2
H1, DH1 = 8, 16
KT = S // 128
SCALE0, SCALE1 = DH0 ** -0.5, DH1 ** -0.5
RANK = 32
E, DFF = 8, 512
NODES, MAX_PREV = 6, 5
GH = 4
MAX_AT = (2, 4, 6, 8)
ROUTER_AT = 10
LN0_AT = 9
LNS = 3
EPS_LN, EPS_OUT = 1e-5, 1e-6

C_GX, C_GF, C_QA, C_KA, C_VA, C_OA = 0, 2, 4, 5, 6, 7
C_EW, C_AW = 8, 26
C_BQ, C_BK, C_BV = 32, 33, 34
C_BE = 35
C_WR = 56
C_BO0, C_BO1, C_LG, C_LB = 64, 192, 320, 448
C_ALL = 576


def edges():
    out, lind = [], 0
    for c in range(NODES):
        nsrc = min(c + 1, MAX_PREV)
        s = c - nsrc
        out.append(((lind + nsrc - 1, lind, lind + nsrc // 2), (c, s + 1, s + nsrc // 2 + 1)))
        lind += nsrc
    return out


def at(turn, per_turn, k):
    return k if turn is None else turn * per_turn + k


def step_index(turn, m):
    return m if turn is None else 2 * turn + m


def count(turn, m, per_step, k):
    return at(turn, 2 * per_step, m * per_step + k)


def wait_apart(eng, tally, sem, value):
    eng.wait_ge(sem, value)
    eng.sem_inc(tally, 1)


ROWS = 4
STEPS = ROWS * NODES
TURNS_B = B // ROWS
C_MAX = (2, 2, 1, 1, 1, 1, 0, 1, 1, 1, 2, 1, 1, 1, 0, 0)
TURNS_C = B // 2 - 1
CU = 16
ORDER8 = (0, 2, 4, 6, 1, 3, 5, 7)


def build(nc, T, out):
    EDGES = edges()
    ctx = ExitStack()
    with ctx:
        def sb(name, shape, dt=F32, stack=ctx):
            return stack.enter_context(nc.sbuf_tensor(name, shape, dt))

        def sem(name):
            return ctx.enter_context(nc.semaphore(name))

        def dram(name, shape):
            return nc.dram_tensor(name, shape, F32, kind="Internal").ap()

        ps = ctx.enter_context(nc.psum_tensor("ps", [128, 8, 512], F32))

        vw_dram = dram("vw_dram", (B, H0 * IPA, D))
        qx_dram = dram("qx_dram", (B, 3 * 16, H1, N))
        kx_dram = dram("kx_dram", (B, 3 * 16, H1, S))
        qk_dram = [dram(f"qk_dram{r}", (2, 3 * 16, H1, N)) for r in range(ROWS)]

        cst = sb("cst", [128, C_ALL])
        ident = sb("ident", [128, 128])
        x_all = sb("x_all", [128, B * TT, D])
        x3T_all = sb("x3T_all", [128, B, N])
        tanh_g = sb("tanh_g", [128, 4])
        sumsel = sb("sumsel", [128, 2, 32])
        sel8f = sb("sel8f", [128, H1, 128])
        ones = sb("ones", [128, 128])
        xw = sb("xw", [128, 4, D])
        xrow = sb("xrow", [128, D])
        pow_c = sb("pow_c", [128, 2])
        gb = sb("gb", [128, 2, D])
        mv = sb("mv", [128, TT, 2])
        st6 = sb("st6", [128, TT, 6])
        rstd = sb("rstd", [128, TT])
        var_e = sb("var_e", [128, TT])

        w_in = sem("w_in")
        apart_tally = sem("apart_tally")
        w_moe_in = sem("w_moe_in")
        w_b_in = sem("w_b_in")
        pool_const = sem("pool_const")
        dve_const = sem("dve_const")
        dve_chain = sem("dve_chain")
        pool_chain = sem("pool_chain")
        gates_tanh = sem("gates_tanh")
        fold_psum = sem("fold_psum")
        fold_done = sem("fold_done")
        vw_out = sem("vw_out")
        ctx_in = sem("ctx_in")
        ctx_used = sem("ctx_used")
        ln_var, ln_eps, ln_rstd, xn_ready, xnT_psum, xnT_ready = (
            [sem(f"{n}{l}") for l in range(LNS)] for n in ("ln_var", "ln_eps", "ln_rstd", "xn_ready", "xnT_psum", "xnT_ready"))
        ctx0_in, vw_in = sem("ctx0_in"), sem("vw_in")
        sum_half, sum_ready, sum_done = sem("sum_half"), sem("sum_ready"), sem("sum_done")
        fill_full = sem("fill_full")
        hi_done = sem("hi_done")
        lo_done = sem("lo_done")
        max_full = sem("max_full")
        max_done = sem("max_done")
        nm_parts = sem("nm_parts")
        nmT_psum = sem("nmT_psum")
        nmT_ready = sem("nmT_ready")
        score_full = sem("score_full")
        probs_ready = sem("probs_ready")
        pv_head = sem("pv_head")
        pair_out = sem("pair_out")
        ipa_scores = sem("ipa_scores")
        ipa_shifted = sem("ipa_shifted")
        ipa_exp = sem("ipa_exp")
        ipa_probs = sem("ipa_probs")
        ipa_T = sem("ipa_T")
        ipa_ready = sem("ipa_ready")
        y_full = sem("y_full")
        logits_full = sem("logits_full")
        gap_ready = sem("gap_ready")
        gap_exp = sem("gap_exp")
        h_full = sem("h_full")
        tanh_done = sem("tanh_done")
        hs_ready = sem("hs_ready")
        w2_done = sem("w2_done")
        x_proj = sem("x_proj")
        x_hi = sem("x_hi")
        x_lo = sem("x_lo")
        x_parts_out = sem("x_parts_out")
        c_ctx_in = [sem(f"c_ctx_in{p}") for p in range(2)]
        c_stacks_in = [[sem(f"c_stacks_in{p}_{half}") for half in range(2)] for p in range(2)]
        c_v_full, c_v, c_max_full, c_max_done = (sem(n) for n in ("c_v_full", "c_v", "c_max_full", "c_max_done"))
        c_nm_parts, c_nmT_psum, c_nmT = sem("c_nm_parts"), sem("c_nmT_psum"), sem("c_nmT")
        c_score, c_probs, c_pv = sem("c_score"), sem("c_probs"), sem("c_pv")
        c_ctxo, c_y, c_x3, c_var, c_rstd = (sem(n) for n in ("c_ctxo", "c_y", "c_x3", "c_var", "c_rstd"))
        c_xn, c_x3T_psum, c_x3T = sem("c_xn"), sem("c_x3T_psum"), sem("c_x3T")
        loop_c_done = sem("loop_c_done")
        c_hi = sem("c_hi")
        b_zeroed = sem("b_zeroed")
        c_zeroed, c_sum = sem("c_zeroed"), sem("c_sum")
        loop_a_done = sem("loop_a_done")
        fb_psum = sem("fb_psum")
        fb_done = sem("fb_done")
        rows_in = sem("rows_in")
        n_proj, n_hi, n_lo, n_v_full, n_v = (sem(n) for n in ("n_proj", "n_hi", "n_lo", "n_v_full", "n_v"))
        n_parts_out = [sem(f"n_parts_out{r}") for r in range(ROWS)]
        n_stacks_in = [sem(f"n_stacks_in{r}") for r in range(ROWS)]
        n_zero, n_max_full, n_max_done = sem("n_zero"), sem("n_max_full"), sem("n_max_done")
        n_nm_parts, n_nmT_psum, n_nmT = sem("n_nm_parts"), sem("n_nmT_psum"), sem("n_nmT")
        n_score, n_probs, n_sum, n_pv = sem("n_score"), sem("n_probs"), sem("n_sum"), sem("n_pv")
        n_ctxo, n_wo, n_node = sem("n_ctxo"), sem("n_wo"), sem("n_node")
        last_T, last_var, last_rstd, last_out = sem("last_T"), sem("last_var"), sem("last_rstd"), sem("last_out")
        stored = [sem(f"stored{r}") for r in range(ROWS)]

        sa = ExitStack()
        wq = sb("wq", [128, ID0], stack=sa)
        wk = sb("wk", [96, ID0], stack=sa)
        wv = sb("wv", [96, ID0], stack=sa)
        wo = sb("wo", [128, PAIRS, D], stack=sa)
        w1T = sb("w1T", [128, E * DFF], stack=sa)
        w2T = sb("w2T", [128, E * DFF // 128, D], stack=sa)
        q12 = sb("q12", [128, 2, PAIRS, N], F32R, stack=sa)
        k12 = sb("k12", [128, 2, PAIRS, S], F32R, stack=sa)
        v0 = sb("v0", [128, KT, ID0], stack=sa)
        probs = sb("probs", [128, 2, KT * N], stack=sa)
        outT = sb("outT", [128, PAIRS, N], stack=sa)
        g_ipa = sb("g_ipa", [128, B, H0 * IPA], stack=sa)
        vw = sb("vw", [64, D], stack=sa)
        ctxT = sb("ctxT", [96, S], stack=sa)
        ctx0 = sb("ctx0", [96, S], stack=sa)
        xn0 = sb("xn0", [128, TT, D], stack=sa)
        xn0T = sb("xn0T", [128, N], stack=sa)
        x_next = sb("x_next", [128, TT, D], stack=sa)
        mv0 = sb("mv0", [128, TT, 2], stack=sa)
        st0 = sb("st0", [128, TT, 6], stack=sa)
        rstd0 = sb("rstd0", [128, TT], stack=sa)
        var0 = sb("var0", [128, TT], stack=sa)
        xn = sb("xn", [128, TT, D], stack=sa)
        xnT = sb("xnT", [128, N], stack=sa)
        psm = sb("psm", [128, 2, 2 * N], stack=sa)
        nm = sb("nm", [128, TT, H0], stack=sa)
        mxs = sb("mxs", [128, TT, 128], F32R, stack=sa)
        nmT = sb("nmT", [128, N], F32R, stack=sa)
        sel4f = sb("sel4f", [128, GH, 128], stack=sa)
        sel4 = sb("sel4", [128, GH, 128], F32R, stack=sa)
        rsum = sb("rsum", [128, N], stack=sa)
        pi = sb("pi", [128, TT, H0 * IPA], stack=sa)
        pis = sb("pis", [128, 2, TT * H0], stack=sa)
        piT = sb("piT", [64, N], stack=sa)
        xs = sb("xs", [128, TT, D], stack=sa)
        lg = sb("lg", [128, TT, E], stack=sa)
        top = sb("top", [128, TT, 8], stack=sa)
        topi = sb("topi", [128, TT, 8], U32, stack=sa)
        topf = sb("topf", [128, TT, 8], stack=sa)
        iota8 = sb("iota8", [128, E], stack=sa)
        gw = sb("gw", [128, 6, TT], stack=sa)
        gate = sb("gate", [128, TT, E], stack=sa)
        gate2 = sb("gate2", [128, TT, E], stack=sa)
        th = sb("th", [128, 2, 2 * N], stack=sa)
        hs = sb("hs", [128, 3, 2, N], stack=sa)
        qx12 = sb("qx12", [128, 2, N], F32R, stack=sa)
        kx12 = sb("kx12", [128, 2, S], F32R, stack=sa)
        boT = sb("boT", [128, D], stack=sa)
        tmp128 = sb("tmp128", [128, D], stack=sa)
        wki = v0[0:96, 0, :]
        wvi = v0[0:96, 1, :]
        up = v0[0:32, 2, :]
        kup = v0[0:32, 3, :]
        vup = probs[0:32, 0, :]
        odT = probs[0:32, 1, :]
        smallw = outT[0:32, 0:3, :].rearrange("p a b -> p (a b)")
        kblk = x3T_all[:, 0:2, :].rearrange("p a b -> p (a b)").rearrange("p (j s c) -> p j s c", s=2, j=PAIRS)
        vblk = x3T_all[:, 2:4, :].rearrange("p a b -> p (a b)").rearrange("p (j s c) -> p j s c", s=2, j=PAIRS)
        wqT = x3T_all[:, 4:8, :].rearrange("p a b -> p (a b)").rearrange("p (j c) -> p j c", j=PAIRS)
        ctx_ipa = xnT[0:96, 0:32]
        vwsb = hs[0:64, 0:2, :, :].rearrange("p a b c -> p (a b c)").rearrange("p (j d) -> p j d", j=PAIRS)

        sa.close()
        fw = sb("fw", [128, NODES, 5, D])
        fb = sb("fb", [128, NODES, 5])
        sc = ExitStack()
        raw = sb("raw_b", [128, NODES, 8, D], stack=sc)
        cctxT = [sb(f"cctxT{p}", [96, S], stack=sc) for p in range(2)]
        cq = [sb(f"cq{p}", [128, H1, N], F32R, stack=sc) for p in range(2)]
        ck = [sb(f"ck{p}", [128, H1, S], F32R, stack=sc) for p in range(2)]
        cv = [sb(f"cv{p}", [128, KT, H1, 32], stack=sc) for p in range(2)]
        cprobs = sb("cprobs", [128, H1, KT * N], stack=sc)
        csum = sb("csum", [128, H1, 2 * N], stack=sc)
        cnm = sb("cnm", [128, TT, H1], stack=sc)
        cmxs = sb("cmxs", [128, TT, 128], F32R, stack=sc)
        crs = sb("crs", [128, N], stack=sc)
        cctx = sb("cctx", [128, N], stack=sc)
        cx = sb("cx", [128, TT, D], stack=sc)
        cxn = sb("cxn", [128, TT, D], stack=sc)
        sc.close()

        def place_b():
            sb_ = ExitStack()
            ctx.enter_context(sb_)
            t = {}

            def per_row(name, shape, dt=F32):
                t[name] = [sb(f"{name}{r}", shape, dt, stack=sb_) for r in range(ROWS)]

            t["probs"] = sb("bprobs", [128, H1, TT * N], stack=sb_)
            t["sums"] = sb("bsums", [128, H1, N], stack=sb_)
            t["rs"] = sb("brs", [128, N], stack=sb_)
            per_row("nodes", [128, NODES + 1, N])
            per_row("qk12", [128, 2, 2, N], F32R)
            per_row("bqst", [128, H1, N], F32R)
            per_row("bkst", [128, H1, N], F32R)
            per_row("vpad", [128, TT, H1, 32])
            per_row("qn", [128, N])
            per_row("bnm", [128, TT, H1])
            per_row("bmxs", [128, TT, 128], F32R)
            per_row("bctx", [128, N])
            per_row("o", [128, TT, D])
            per_row("bmv", [128, TT, 2])
            per_row("bst", [128, TT, 6])
            per_row("brstd", [128, TT])
            per_row("bvar", [128, TT])
            return t

        TB = place_b()

        CH_DVE_A = 40
        block = ctx.enter_context(nc.Block())

        N_W, N_B = 22, 8 * NODES

        @block.sync
        def _(sp):
            for dst, src in (
                (cst[:], T["cst"]), (x_all[:, :, :], T["x"].rearrange("b (t p) d -> p (b t) d", p=128)),
                (smallw[:, 0:128], T["q_downT"]), (up, T["q_up"]), (wq[:], T["Wq"]),
                (smallw[:, 128:224], T["k_downT"]), (kup, T["k_up"]), (wk[:], T["Wk"]),
                (smallw[:, 224:320], T["v_downT"]), (vup, T["v_up"]), (wv[:], T["Wv"]),
                (smallw[:, 320:448], T["o_up"]), (odT, T["o_downT"]),
                (wo[:, :, :], T["Wo"].rearrange("(j p) d -> p j d", p=128)),
                (wki, T["Wk_ipa"]), (wvi, T["Wv_ipa"]), (ctx_ipa, T["ctx_ipaT"]),
                (xw[:, 0, :], T["xWq"]), (xw[0:96, 1, :], T["xWk"]), (xw[0:96, 2, :], T["xWv"]),
                (xw[:, 3, :], T["xWo"]), (ident[:], T["ident"]),
            ):
                sp.dma_start(dst, src).then_inc(w_in, 16)

            def ctx0_load(b):
                src = T["ctxT"][bass.ds(b, 1)].rearrange("a c s -> (a c) s")
                sp.dma_start(ctx0[:, 0:SM], src[:, 0:SM]).then_inc(ctx0_in, 16)
                sp.dma_start(ctx0[:, SM:S], src[:, SM - IPA:SM]).then_inc(ctx0_in, 16)

            def vw_load(b):
                sp.dma_start(vw[:], vw_dram[bass.ds(b, 1)].rearrange("a c s -> (a c) s")).then_inc(vw_in, 16)

            def ctx_load(b):
                src = T["ctxT"][bass.ds(b, 1)].rearrange("a c s -> (a c) s")
                sp.dma_start(ctxT[:], src).then_inc(ctx_in, 16)

            ctx0_load(0)
            ctx_load(0)
            sp.dma_start(w1T[:], T["W1T"]).then_inc(w_moe_in, 16)
            sp.dma_start(w2T[:, :, :], T["W2T"].rearrange("(c p) d -> p c d", p=128)).then_inc(w_moe_in, 16)
            sp.wait_ge(fold_done, 15)
            for s in range(2):
                sp.dma_start(vw_dram.rearrange("b (t j s) d -> s (b t) j d", s=2, t=IPA)[s],
                             vwsb[32 * s:32 * s + 32, :, :]).then_inc(vw_out, 16)
            sp.wait_ge(vw_out, 32)
            vw_load(0)

            def parts_out(i):
                row = bass.ds(i, 1) if not isinstance(i, int) else slice(i, i + 1)
                sp.wait_ge(x_lo, at(i, 2, 2))
                for part, q_places, k_places in ((0, (0, 1), (0, 2)), (1, (2,), (1,))):
                    for k in q_places:
                        sp.dma_start(qx_dram[row, 16 * k:16 * k + 16].rearrange("a d h q -> (a h) d q"),
                                     qx12[:, part, :].bitcast(F32)).then_inc(x_parts_out, 16)
                    for k in k_places:
                        sp.dma_start(kx_dram[row, 16 * k:16 * k + 16].rearrange("a d h q -> (a h) d q"),
                                     kx12[:, part, :].bitcast(F32)).then_inc(x_parts_out, 16)

            sp.sem_inc(x_parts_out, 96)
            with sp.Fori(0, B - 1) as i:
                sp.wait_ge(fill_full, at(i, 20, 20))
                ctx0_load(i + 1)
                sp.wait_ge(y_full, at(i, 1, 1))
                vw_load(i + 1)
                sp.wait_ge(ctx_used, at(i, 1, 1))
                ctx_load(i + 1)
                parts_out(i)
            parts_out(B - 1)

            sp.wait_ge(x_parts_out, 96 * (B + 1))
            sp.wait_ge(loop_a_done, 3)
            sp.wait_ge(c_zeroed, 1)

            def stacks_in(i, m):
                b = step_index(i, m)
                row = bass.ds(b, 1) if i is not None else slice(b, b + 1)
                for half in range(2):
                    if m >= 2 or i is not None:
                        sp.wait_ge(c_score, count(i, m - 2, CU, 8 * half + 8))
                    for dst, src in ((cq[m % 2], qx_dram), (ck[m % 2], kx_dram)):
                        of_half = lambda x: x.rearrange("p (j e) q -> p j e q", e=2)[:, :, half, :]
                        sp.dma_start(of_half(dst[0:48]).bitcast(F32),
                                     of_half(src[row].rearrange("a p h q -> (a p) h q"))).then_inc(c_stacks_in[m % 2][half], 16)
                sp.dma_start(cctxT[m % 2][:], T["ctxT"][row].rearrange("a c s -> (a c) s")).then_inc(c_ctx_in[m % 2], 16)

            stacks_in(None, 0)
            stacks_in(None, 1)
            for c, ((eq, ek, ev), _src) in enumerate(EDGES):
                for n, src in enumerate((T["WeT"][eq], T["WeT"][ek], T["WeT"][ev], T["We"][eq],
                                         T["bWq"][c], T["bWk"][c], T["bWv"][c], T["bWo"][c])):
                    sp.dma_start(raw[:, c, n, :], src).then_inc(w_b_in, 16)
            with sp.Fori(0, TURNS_C) as i:
                stacks_in(i, 2)
                stacks_in(i, 3)

            for r in range(ROWS):
                sp.sem_inc(stored[r], 16)
            with sp.Fori(0, TURNS_B) as i:
                for s in range(STEPS):
                    c, r = divmod(s, ROWS)
                    for wait, part, places in ((n_hi, 0, ((0, 1), (0, 2))), (n_lo, 1, ((2,), (1,)))):
                        sp.wait_ge(wait, at(i, STEPS, s + 1))
                        for n in range(2):
                            for k in places[n]:
                                sp.dma_start(qk_dram[r][n, 16 * k:16 * k + 16].rearrange("d h q -> h d q"),
                                             TB["qk12"][r][:, part, n, :].bitcast(F32)).then_inc(n_parts_out[r], 16)
                    sp.wait_ge(n_parts_out[r], at(i, 96 * NODES, 96 * (c + 1)))
                    for n, dst in enumerate((TB["bqst"][r], TB["bkst"][r])):
                        sp.dma_start(dst[0:48].bitcast(F32), qk_dram[r][n]).then_inc(n_stacks_in[r], 16)
                for r in range(ROWS):
                    sp.wait_ge(last_out, at(i, ROWS, ROWS + r + 1))
                    sp.dma_start(out[bass.ds(ROWS * i + r, 1)].rearrange("a (t p) d -> p (a t) d", p=128),
                                 TB["o"][r][:, :, :]).then_inc(stored[r], 16)
            for r in range(ROWS):
                sp.wait_ge(stored[r], 16 * (TURNS_B + 1))

        @block.gpsimd
        def _(pool):
            g = nc.gpsimd
            g.memset(mxs[:, :, :].bitcast(F32), 0.0)
            g.memset(ones[:], 1.0)
            g.memset(sumsel[:, :, :], 0.0)
            g.memset(pow_c[:], -0.5)
            g.memset(sel4f[:, :, :], 0.0)
            g.memset(sel8f[:, :, :], 0.0)
            g.iota(topi[:, 0, :], [[1, E]], base=0, channel_multiplier=0).then_inc(pool_const, 1)
            pool.wait_ge(pool_const, 1)
            g.tensor_copy(iota8[:], topi[:, 0, :])
            g.memset(sumsel[:, 0, 0:16], 1.0)
            g.memset(sumsel[:, 1, 16:32], 1.0)
            for base in (0, 32, 64, 96):
                last = g.affine_select(out=sel4f[:, :, :], in_=sel4f[:, :, :], compare_op=ALU.not_equal, fill=1.0,
                                       base=-base, pattern=[[-1, GH], [0, 128]], channel_multiplier=1)
                last.then_inc(pool_chain, 1)
                pool.wait_ge(pool_chain, base // 32 + 1)
            for n, base in enumerate((0, 32, 64, 96)):
                last = g.affine_select(out=sel8f[:, :, :], in_=sel8f[:, :, :], compare_op=ALU.not_equal, fill=1.0,
                                       base=-base, pattern=[[-1, H1], [0, 128]], channel_multiplier=1)
                last.then_inc(pool_chain, 1)
                pool.wait_ge(pool_chain, 5 + n)
            g.tensor_copy(sel4[:, :, :], sel4f[:, :, :]).then_inc(pool_const, 1)

            def ln_step(i, l, row):
                stats, ve, rs = (mv0, var0, rstd0) if l == 0 else (mv, var_e, rstd)
                wait_apart(pool, apart_tally, ln_var[l], at(i, 1, row + 1))
                g.tensor_scalar(ve[:], stats[:, :, 1], EPS_LN, None, ALU.add).then_inc(ln_eps[l], 1)
                pool.wait_ge(ln_eps[l], at(i, 1, row + 1))
                g.tensor_tensor(rs[:], ve[:], pow_c[:], ALU.pow).then_inc(ln_rstd[l], 1)

            def head_sum(i, row, h):
                pr, t = probs[:, h % 2, :], psm[:, h % 2, :]
                pool.wait_ge(probs_ready, at(i, H0, H0 * row + h + 1))
                if h >= 2:
                    pool.wait_ge(sum_done, at(i, H0, H0 * row + h - 1))
                g.tensor_tensor(t, pr[:, 0:2 * N], pr[:, 2 * N:4 * N], ALU.add).then_inc(sum_half, 1)
                pool.wait_ge(sum_half, at(i, H0, H0 * row + h + 1))
                g.tensor_tensor(t[:, 0:N], t[:, 0:N], t[:, N:2 * N], ALU.add).then_inc(sum_ready, 1)

            def loop_a_turn(i, row, more):
                for h in range(GH, H0):
                    head_sum(i, row, h)
                    if h == LN0_AT and more:
                        ln_step(i, 0, row + 1)
                ln_step(i, 1, row)
                ln_step(i, 2, row)
                if more:
                    for h in range(GH):
                        head_sum(i, row + 1, h)

            ln_step(None, 0, 0)
            for h in range(GH):
                head_sum(None, 0, h)
            with pool.Fori(0, B - 1) as i:
                loop_a_turn(i, 0, True)
            loop_a_turn(None, B - 1, False)
            pool.wait_ge(loop_a_done, 3)
            g.memset(cmxs[:, :, :].bitcast(F32), 0.0)
            for p in range(2):
                last = g.memset(cv[p][:, :, :, :], 0.0)
            last.then_inc(pool_const, 1)

            def c_head_sum(i, m, n):
                h = ORDER8[n]
                pool.wait_ge(c_probs, count(i, m, CU, 2 * n + 2))
                if m:
                    pool.wait_ge(c_pv, count(i, m - 1, 2, n // 4 + 1))
                g.tensor_tensor(csum[:, h, :], cprobs[:, h, 0:2 * N], cprobs[:, h, 2 * N:4 * N], ALU.add).then_inc(c_sum, 1)

            def c_step(i, m):
                for n in range(H1):
                    c_head_sum(i, m, n)
                    if n == 4 and m:
                        c_rstd_step(i, m - 1)

            def c_rstd_step(i, m):
                wait_apart(pool, apart_tally, c_var, count(i, m, 1, 1))
                g.tensor_scalar(var_e[:], mv[:, :, 1], EPS_LN, None, ALU.add).then_inc(pool_chain, 1)
                pool.wait_ge(pool_chain, count(i, m, 1, 8 + 1))
                g.tensor_tensor(rstd[:], var_e[:], pow_c[:], ALU.pow).then_inc(c_rstd, 1)

            c_step(None, 0)
            with pool.Fori(0, TURNS_C) as i:
                c_step(i, 1)
                c_step(i, 2)
            c_step(None, B - 1)
            c_rstd_step(None, B - 1)
            pool.wait_ge(loop_c_done, 3)
            for r in range(ROWS):
                g.memset(TB["bmxs"][r][:, :, :].bitcast(F32), 0.0)
                g.memset(TB["vpad"][r][:, :, :, :], 0.0).then_inc(b_zeroed, 1)
            for n, stack in enumerate((*TB["bqst"], *TB["bkst"])):
                pool.wait_ge(b_zeroed, ROWS + n)
                g.memset(stack[32:64, :, :].bitcast(F32), 0.0).then_inc(b_zeroed, 1)
            pool.wait_ge(b_zeroed, 3 * ROWS)
            g.memset(TB["bvar"][0][:], 0.0).then_inc(pool_const, 1)

            def zero(i, s):
                if s < ROWS:
                    wait_apart(pool, apart_tally, rows_in, at(i, ROWS, ROWS))
                else:
                    wait_apart(pool, apart_tally, n_score, at(i, STEPS * H1, (s - ROWS + 1) * H1))
                if s > 2:
                    wait_apart(pool, apart_tally, n_sum, at(i, STEPS * H1, (s - 2) * H1))
                g.memset(TB["bqst"][s % ROWS][64:128, :, :].bitcast(F32), 0.0).then_inc(n_zero, 1)

            def head_sum(i, s, n):
                h = ORDER8[n]
                pool.wait_ge(n_probs, at(i, STEPS * H1, H1 * s + n + 1))
                if s:
                    pool.wait_ge(n_pv, at(i, 2 * STEPS, 2 * s - 1 + n // 4))
                if n == 0:
                    pool.wait_ge(n_zero, at(i, STEPS, min(s + 3, STEPS)))
                g.tensor_tensor(TB["sums"][:, h, :], TB["probs"][:, h, 0:N], TB["probs"][:, h, N:2 * N], ALU.add).then_inc(n_sum, 1)

            with pool.Fori(0, TURNS_B) as i:
                zero(i, 0)
                zero(i, 1)
                for s in range(STEPS):
                    if s + 2 < STEPS:
                        zero(i, s + 2)
                    for n in range(H1):
                        head_sum(i, s, n)
                for r in range(ROWS):
                    wait_apart(pool, apart_tally, last_var, at(i, ROWS, r + 1))
                    g.tensor_scalar(TB["bvar"][r][:], TB["bmv"][r][:, :, 1], EPS_OUT, None, ALU.add).then_inc(pool_chain, 1)
                    pool.wait_ge(pool_chain, at(i, ROWS, 8 + B + r + 1))
                    g.tensor_tensor(TB["brstd"][r][:], TB["bvar"][r][:], pow_c[:], ALU.pow).then_inc(last_rstd, 1)

        @block.tensor
        def _(pe):
            mm = pe.matmul
            pe.wait_ge(w_in, 16 * N_W)
            pe.wait_ge(pool_const, 2)
            for h in range(2):
                mm(ps[:, h, :], smallw[:, 0:128], up[:, 512 * h:512 * h + 512], start=True, stop=True)
                mm(ps[0:96, 2 + h, :], smallw[:, 128:224], kup[:, 512 * h:512 * h + 512], start=True, stop=True)
                mm(ps[0:96, 4 + h, :], smallw[:, 224:320], vup[:, 512 * h:512 * h + 512], start=True, stop=True)
            for j in range(PAIRS):
                last = mm(ps[:, 6 + j // 4, 128 * (j % 4):128 * (j % 4) + 128], odT[:, 128 * j:128 * j + 128],
                          smallw[:, 320:448], start=True, stop=True)
            last.then_inc(fold_psum, 1)
            pe.wait_ge(fold_done, 4)
            for j in range(PAIRS):
                mm(ps[:, 0, 32 * j:32 * j + 32], wki[:, 128 * j:128 * j + 128], ctx_ipa, start=True, stop=True)
            for j in range(PAIRS):
                mm(ps[:, 0, 256 + 32 * j:256 + 32 * j + 32], wvi[:, 128 * j:128 * j + 128], ctx_ipa, start=True, stop=True)
            for j in range(PAIRS):
                last = pe.transpose(ps[:, 1 + j // 4, 128 * (j % 4):128 * (j % 4) + 128], wq[:, 128 * j:128 * j + 128], ident[:])
            last.then_inc(fold_psum, 1)
            pe.wait_ge(fold_done, 10)
            pe.wait_ge(dve_const, 1)
            for j in range(PAIRS):
                mm(ps[:, 3, 64 * j:64 * j + 64], wqT[:, j, :], kblk[:, j, :, :], start=True, stop=True)
            for j in range(PAIRS):
                last = mm(ps[0:64, 4 + j // 4, 128 * (j % 4):128 * (j % 4) + 128], vblk[:, j, :, :], wo[:, j, :],
                          start=True, stop=True)
            last.then_inc(fold_psum, 1)
            mm(ps[:, 6, 0:128], tmp128[:], xw[:, 3, :], start=True, stop=True).then_inc(fold_psum, 1)
            pe.wait_ge(fold_done, 16)

            def transpose_xn(i, row, l, bank, c0):
                src = xn0 if l == 0 else xn
                pe.wait_ge(xn_ready[l], at(i, 1, row + 1))
                for t in range(TT):
                    last = pe.transpose(ps[:, bank, c0 + 128 * t:c0 + 128 * t + 128], src[:, t, :], ident[:])
                last.then_inc(xnT_psum[l], 1)

            def fill(i, row, n):
                bank = 2 + n % 4
                if n == 0:
                    pe.wait_ge(ctx0_in, at(i, 32, 32 * row + 32))
                if n >= 16:
                    pe.wait_ge(hi_done, at(i, 20, 20 * row + n - 3))
                elif n >= 4:
                    pe.wait_ge(lo_done, at(i, 12, 12 * row + n - 3))
                if n < 8:
                    last = mm(ps[:, bank, :], wk[:, 128 * n:128 * n + 128], ctx0[:], start=True, stop=True)
                elif n < 12:
                    for h in range(2):
                        j = 2 * (n - 8) + h
                        last = mm(ps[:, bank, N * h:N * h + N], wq[:, 128 * j:128 * j + 128], xn0T[:], start=True, stop=True)
                else:
                    k, h = divmod(n - 12, 2)
                    last = mm(ps[:, bank, :], ctx0[:, 128 * k:128 * k + 128], wv[:, 512 * h:512 * h + 512], start=True, stop=True)
                last.then_inc(fill_full, 1)

            def ipa_score(i, row):
                pe.wait_ge(xnT_ready[0], at(i, 1, row + 1))
                for t in range(TT):
                    last = mm(ps[:, 7, 64 * t:64 * t + 64], xn0T[:, 128 * t:128 * t + 128],
                              g_ipa[:, bass.ds(i + row, 1), :] if i is not None else g_ipa[:, row, :], start=True, stop=True)
                last.then_inc(ipa_scores, 1)

            def row_max(i, row, h):
                p0 = 64 * (h % 2)
                if h >= 1:
                    pe.wait_ge(max_done, at(i, H0, H0 * row + h))
                else:
                    pe.wait_ge(hi_done, at(i, 20, 20 * row + 20))
                if h % GH == 0 and h:
                    pe.wait_ge(nmT_ready, at(i, H0 // GH, H0 // GH * row + h // GH))
                for t in range(TT):
                    last = mm(ps[:, t, 0:SM], q12[p0:p0 + 64, 0, h // 2, 128 * t:128 * t + 128],
                              k12[p0:p0 + 64, 0, h // 2, 0:SM], start=True, stop=True)
                last.then_inc(max_full, 1)

            def maxima_T(i, row, gr):
                pe.wait_ge(nm_parts, at(i, H0 // GH, H0 // GH * row + gr + 1))
                for t in range(TT):
                    last = pe.transpose(ps[:, 0, 128 * t:128 * t + 128], mxs[:, t, :].bitcast(F32), ident[:])
                last.then_inc(nmT_psum, 1)

            def scores(i, row, h, after):
                p0 = 64 * (h % 2)
                if h % GH == 0:
                    pe.wait_ge(nmT_ready, at(i, H0 // GH, H0 // GH * row + h // GH + 1))
                if h >= 2:
                    pe.wait_ge(probs_ready, at(i, H0, H0 * row + h - 1))
                elif h == 0:
                    pe.wait_ge(lo_done, at(i, 12, 12 * row + 12))
                elif after:
                    pe.wait_ge(x_lo, at(i, 2, 2 * row - 1))
                for k in range(KT):
                    o = ps[:, 2 + 2 * (h % 2) + k // 2, N * (k % 2):N * (k % 2) + N]
                    for n, (a, b) in enumerate(((0, 0), (0, 1), (1, 0))):
                        mm(o, k12[p0:p0 + 64, a, h // 2, 128 * k:128 * k + 128], q12[p0:p0 + 64, b, h // 2, :],
                           start=(n == 0), stop=False)
                    last = mm(o, sel4[p0:p0 + 64, h % GH, :], nmT[p0:p0 + 64, :], start=False, stop=True)
                last.then_inc(score_full, 1)

            def values(i, row, h, after=False):
                p0 = 64 * (h % 2)
                bank = 6 + (h // 2) % 2
                if h % 2 == 0 and h >= 4:
                    pe.wait_ge(pair_out, at(i, PAIRS, PAIRS * row + h // 2 - 1))
                if h == 2:
                    pe.wait_ge(ipa_shifted, at(i, 1, row + 1))
                    if after:
                        pe.wait_ge(x_lo, at(i, 2, 2 * row))
                pe.wait_ge(probs_ready, at(i, H0, H0 * row + h + 1))
                for k in range(KT):
                    kr = min(128, SM - 128 * k)
                    last = mm(ps[p0:p0 + 64, bank, 0:N], v0[0:kr, k, 64 * h:64 * h + 64], probs[0:kr, h % 2, N * k:N * k + N],
                              start=(k == 0), stop=(k == KT - 1), skip_group_check=True)
                last.then_inc(pv_head, 1)

            def sums(i, row, h):
                p0 = 64 * (h % 2)
                pe.wait_ge(sum_ready, at(i, H0, H0 * row + h + 1))
                mm(ps[p0:p0 + 64, 6 + (h // 2) % 2, N:2 * N], ones[:, 0:64], psm[:, h % 2, 0:N],
                   start=False, stop=True, skip_group_check=True).then_inc(sum_done, 1)

            def first_heads(i, row, after):
                for h in range(GH):
                    if h or not after:
                        row_max(i, row, h + GH)
                    scores(i, row, h, after)
                    if h == 1 and after:
                        transpose_xn(i, row - 1, 2, 7, N)
                    if h == 2 and after:
                        l1_queries(i, row - 1)
                    if h == 3:
                        maxima_T(i, row, 1)
                    if h >= 1:
                        values(i, row, h - 1, after)
                    if h >= 2:
                        sums(i, row, h - 2)

            def l1_queries(i, row):
                pe.wait_ge(xnT_ready[2], at(i, 1, row + 1))
                mm(ps[:, 7, 0:N], xw[:, 0, :], xnT[:], start=True, stop=True).then_inc(x_proj, 1)

            def heads(i, row):
                for h in range(GH, H0):
                    if h + GH < H0:
                        row_max(i, row, h + GH)
                    scores(i, row, h, False)
                    if h % GH == GH - 1 and h // GH + 1 < H0 // GH:
                        maxima_T(i, row, h // GH + 1)
                    values(i, row, h - 1)
                    sums(i, row, h - 2)
                values(i, row, H0 - 1)
                sums(i, row, H0 - 2)
                wait_apart(pe, apart_tally, ipa_probs, at(i, 1, row + 1))
                for t in range(TT):
                    last = pe.transpose(ps[0:64, 0, 128 * t:128 * t + 128], pi[:, t, :], ident[:])
                last.then_inc(ipa_T, 1)

            def attention_out(i, row, more):
                if more:
                    fill(i, row + 1, 0)
                    fill(i, row + 1, 1)
                pe.wait_ge(ipa_ready, at(i, 1, row + 1))
                pe.wait_ge(vw_in, at(i, 16, 16 * row + 16))
                pe.wait_ge(pair_out, at(i, PAIRS, PAIRS * row + PAIRS - 1))
                for t in range(TT):
                    mm(ps[:, 1, 128 * t:128 * t + 128], piT[:, 128 * t:128 * t + 128], vw[:], start=(t == 0), stop=False,
                       skip_group_check=True)
                    for j in range(PAIRS - 1):
                        mm(ps[:, 1, 128 * t:128 * t + 128], outT[:, j, 128 * t:128 * t + 128], wo[:, j, :],
                           start=False, stop=False, skip_group_check=True)
                sums(i, row, H0 - 1)
                if more:
                    transpose_xn(i, row + 1, 0, 6, N)
                    fill(i, row + 1, 2)
                    fill(i, row + 1, 3)
                pe.wait_ge(pair_out, at(i, PAIRS, PAIRS * row + PAIRS))
                for t in range(TT):
                    last = mm(ps[:, 1, 128 * t:128 * t + 128], outT[:, PAIRS - 1, 128 * t:128 * t + 128], wo[:, PAIRS - 1, :],
                              start=False, stop=True, skip_group_check=True)
                last.then_inc(y_full, 1)

            def router(i, row, more):
                transpose_xn(i, row, 1, 6, 0)
                if more:
                    pe.wait_ge(ipa_shifted, at(i, 1, row + 2))
                    fill(i, row + 1, ROUTER_AT)
                pe.wait_ge(xnT_ready[1], at(i, 1, row + 1))
                for t in range(TT):
                    last = mm(ps[:, 7, 256 + 8 * t:256 + 8 * t + 8], xnT[:, 128 * t:128 * t + 128], cst[:, C_WR:C_WR + 8], start=True, stop=True)
                last.then_inc(logits_full, 1)

            def hidden(i, row, n, more=False):
                if n >= 2:
                    pe.wait_ge(hs_ready, at(i, 16, 16 * row + n - 1))
                elif more:
                    pe.wait_ge(hi_done, at(i, 20, 20 * (row + 1) + 17 + n))
                for h in range(2):
                    c = 2 * n + h
                    last = mm(ps[:, 2 + n % 2, N * h:N * h + N], w1T[:, 128 * c:128 * c + 128], xnT[:], start=True, stop=True)
                last.then_inc(h_full, 1)

            def moe(i, row, more):
                def project(n):
                    pe.wait_ge(hs_ready, at(i, 16, 16 * row + n + 1))
                    if n < 8 and n % 4 == 0 and more:
                        pe.wait_ge(hi_done, at(i, 20, 20 * (row + 1) + 19 + n // 4))
                    if n == 8:
                        pe.wait_ge(gap_ready, at(i, 1, row + 1))
                    for h in range(2):
                        c = 2 * n + h
                        e = c // 4
                        for t in range(TT):
                            c0 = 256 * (e % 2) + 128 * t
                            last = mm(ps[:, 4 + e // 2, c0:c0 + 128], hs[:, n % 3, h, 128 * t:128 * t + 128], w2T[:, c, :],
                                      start=(c % 8 == 0 and t == 0), stop=(c % 8 == 7 and t == 1), skip_group_check=True)
                    last.then_inc(w2_done, 1)

                for n in range(16):
                    if n + 2 < 16:
                        hidden(i, row, n + 2)
                    project(n)
                    if more and n in MAX_AT:
                        row_max(i, row + 1, MAX_AT.index(n))
                    if more and n == 11:
                        maxima_T(i, row + 1, 0)
                    if more and n == 14:
                        row_max(i, row + 1, GH)
                    if n == 8:
                        pe.wait_ge(ctx_in, at(i, 16, 16 * row + 16))
                        mm(ps[:, 4, :], xw[0:96, 1, :], ctxT[:], start=True, stop=True).then_inc(ctx_used, 1)

            def loop_a_turn(i, row, more):
                heads(i, row)
                attention_out(i, row, more)
                if more:
                    ipa_score(i, row + 1)
                    for n in range(4, ROUTER_AT):
                        fill(i, row + 1, n)
                router(i, row, more)
                if more:
                    for n in range(ROUTER_AT + 1, 19):
                        fill(i, row + 1, n)
                hidden(i, row, 0, more)
                if more:
                    fill(i, row + 1, 19)
                hidden(i, row, 1, more)
                moe(i, row, more)
                if more:
                    first_heads(i, row + 1, True)
                else:
                    transpose_xn(i, row, 2, 7, N)
                    l1_queries(i, row)
                    pe.wait_ge(x_lo, at(i, 2, 2 * row + 2))

            transpose_xn(None, 0, 0, 6, N)
            ipa_score(None, 0)
            for n in range(20):
                fill(None, 0, n)
            for h in range(GH):
                row_max(None, 0, h)
            maxima_T(None, 0, 0)
            first_heads(None, 0, False)
            pe.wait_ge(w_moe_in, 32)
            with pe.Fori(0, B - 1) as i:
                loop_a_turn(i, 0, True)
            loop_a_turn(None, B - 1, False)
            mm(ps[:, 5, 0:128], ident[:], ident[:], start=True, stop=True).then_inc(loop_a_done, 1)

            def v_fill(i, m):
                if m >= 2 or i is not None:
                    pe.wait_ge(c_ctxo, count(i, m - 2, 1, 1))
                pe.wait_ge(c_ctx_in[m % 2], at(i, 16, 16 * (m // 2 + 1)))
                for k in range(KT):
                    last = mm(ps[:, 4 + m % 2, 128 * k:128 * k + 128], cctxT[m % 2][:, 128 * k:128 * k + 128], xw[0:96, 2, :], start=True, stop=True)
                last.then_inc(c_v_full, 1)

            def c_row_max(i, m, n):
                h, t = ORDER8[n // 2], n % 2
                if n % 8 == 0:
                    pe.wait_ge(c_stacks_in[m % 2][n // 8], at(i, 32, 32 * (m // 2 + 1)))
                if m or n >= 2:
                    pe.wait_ge(c_max_done, count(i, m, CU, n - 1))
                mm(ps[:, t, :], cq[m % 2][0:48, h, 128 * t:128 * t + 128], ck[m % 2][0:48, h, :], start=True, stop=True).then_inc(c_max_full, 1)

            def c_maxima_T(i, m):
                pe.wait_ge(c_v, count(i, m, 1, 1))
                pe.wait_ge(c_nm_parts, count(i, m, 1, 1))
                for t in range(TT):
                    last = pe.transpose(ps[:, 4 + m % 2, 128 * t:128 * t + 128], cmxs[:, t, :].bitcast(F32), ident[:])
                last.then_inc(c_nmT_psum, 1)

            def c_scores(i, m, n):
                h = ORDER8[n // 2]
                if n % 8 == 0:
                    pe.wait_ge(c_nmT, count(i, m, 2, n // 8 + 1))
                if m or n >= 2:
                    pe.wait_ge(c_probs, count(i, m, CU, n - 1))
                for k in range(2):
                    kt = 2 * (n % 2) + k
                    last = mm(ps[:, 2 + n % 2, N * k:N * k + N], ck[m % 2][:, h, 128 * kt:128 * kt + 128], cq[m % 2][:, h, :], start=True, stop=True)
                last.then_inc(c_score, 1)

            def c_value_quad(i, m, half, kt):
                if kt == 0:
                    pe.wait_ge(c_probs, count(i, m, CU, 8 * half + 8))
                for j in range(4):
                    h = 2 * j + half
                    mm(ps[32 * j:32 * j + 32, 4 + m % 2, 0:N], cv[m % 2][:, kt, h, :], cprobs[:, h, N * kt:N * kt + N],
                       start=(half == 0 and kt == 0), stop=(half == 1 and kt == KT - 1), skip_group_check=True,
                       tile_position=(0, 32 * j))

            def c_sum_quad(i, m, half, k):
                if k == 0:
                    pe.wait_ge(c_sum, count(i, m, H1, 4 * half + 4))
                for j in range(4):
                    last = mm(ps[32 * j:32 * j + 32, 4 + m % 2, N:2 * N], sumsel[:, half, :], csum[:, 2 * j + half, N * k:N * k + N],
                              start=False, stop=(half == 1 and k == 1), skip_group_check=True, tile_position=(0, 32 * j))
                if k:
                    last.then_inc(c_pv, 1)

            def c_out(i, m):
                pe.wait_ge(c_ctxo, count(i, m, 1, 1))
                for t in range(TT):
                    last = mm(ps[:, 6 + m % 2, 128 * t:128 * t + 128], cctx[:, 128 * t:128 * t + 128], xw[:, 3, :], start=True, stop=True)
                last.then_inc(c_y, 1)

            def c_x3T_out(i, m):
                pe.wait_ge(c_xn, count(i, m, 1, 1))
                for t in range(TT):
                    last = pe.transpose(ps[:, 6 + m % 2, N + 128 * t:N + 128 * t + 128], cxn[:, t, :], ident[:])
                last.then_inc(c_x3T_psum, 1)

            def c_step(i, m, more):
                maxima = 0
                for n in range(CU):
                    for _ in range(C_MAX[n] if more else 0):
                        c_row_max(i, m + 1, maxima)
                        maxima += 1
                    if n == 14 and more:
                        c_maxima_T(i, m + 1)
                    c_scores(i, m, n)
                    if m and 1 <= n <= 3:
                        for kt in ((0, 1), (2,), (3,))[n - 1]:
                            c_value_quad(i, m - 1, 1, kt)
                    if m and 3 <= n <= 4:
                        c_sum_quad(i, m - 1, 1, n - 3)
                    if n == 8:
                        if m:
                            c_out(i, m - 1)
                        if more:
                            v_fill(i, m + 1)
                    if 9 <= n <= 12:
                        c_value_quad(i, m, 0, n - 9)
                    if n == 15 and m:
                        c_x3T_out(i, m - 1)
                    if n >= 14:
                        c_sum_quad(i, m, 0, n - 14)

            pe.wait_ge(pool_const, 3)
            v_fill(None, 0)
            for n in range(CU):
                c_row_max(None, 0, n)
            c_maxima_T(None, 0)
            c_step(None, 0, True)
            with pe.Fori(0, TURNS_C) as i:
                c_step(i, 1, True)
                c_step(i, 2, True)
            c_step(None, B - 1, False)
            for kt in range(KT):
                c_value_quad(None, B - 1, 1, kt)
            for k in range(2):
                c_sum_quad(None, B - 1, 1, k)
            c_out(None, B - 1)
            c_x3T_out(None, B - 1)
            pe.wait_ge(c_x3T, B)
            mm(ps[:, 5, 0:128], ident[:], ident[:], start=True, stop=True).then_inc(loop_c_done, 1)

            pe.wait_ge(w_b_in, 16 * N_B)
            for c in range(NODES):
                if c >= 4:
                    pe.wait_ge(fb_done, c - 3)
                b = c % 4
                for n in range(3):
                    mm(ps[:, b, 128 * n:128 * n + 128], raw[:, c, n, :], raw[:, c, 4 + n, :], start=True, stop=True)
                for n in range(3):
                    last = mm(ps[:, b, 384 + n:385 + n], raw[:, c, 4 + n, :], cst[:, C_BE + EDGES[c][0][n]:C_BE + EDGES[c][0][n] + 1],
                              start=True, stop=True)
                last.then_inc(fb_psum, 1)
            pe.wait_ge(fb_done, NODES)
            for c in range(NODES):
                last = mm(ps[:, 5, c:c + 1], raw[:, c, 7, :], fb[:, c, 2:3], start=True, stop=True)
            last.then_inc(fb_psum, 1)
            pe.wait_ge(fb_done, NODES + 1)
            pe.wait_ge(pool_const, 4)

            def proj_qk(i, s):
                c, r = divmod(s, ROWS)
                nq, nk, nv = EDGES[c][1]
                if c == 0:
                    pe.wait_ge(rows_in, at(i, ROWS, r + 1))
                else:
                    pe.wait_ge(n_node, at(i, STEPS, s - ROWS + 1))
                nodes = TB["nodes"][r]
                mm(ps[:, 4 + r, 0:N], fw[:, c, 0, :], nodes[:, nq, :], start=True, stop=True)
                mm(ps[:, 4 + r, N:2 * N], fw[:, c, 1, :], nodes[:, nk, :], start=True, stop=True).then_inc(n_proj, 1)

            def proj_v(i, s):
                c, r = divmod(s, ROWS)
                nq, nk, nv = EDGES[c][1]
                nodes = TB["nodes"][r]
                pe.wait_ge(n_lo, at(i, STEPS, s + 1))
                for k in range(TT):
                    mm(ps[:, 4 + r, 128 * k:128 * k + 128], nodes[:, nv, 128 * k:128 * k + 128], fw[:, c, 2, :], start=True, stop=True)
                mm(ps[:, 4 + r, N:2 * N], fw[:, c, 3, :], nodes[:, nq, :], start=True, stop=True).then_inc(n_v_full, 1)

            def row_max(i, s, n):
                c, r = divmod(s, ROWS)
                q, k = TB["bqst"][r], TB["bkst"][r]
                if n == 0:
                    pe.wait_ge(n_stacks_in[r], at(i, 32 * NODES, 32 * (c + 1)))
                    pe.wait_ge(n_zero, at(i, STEPS, s + 1))
                if H1 * s + n >= 2:
                    pe.wait_ge(n_max_done, at(i, STEPS * H1, H1 * s + n - 1))
                for t in range(TT):
                    last = mm(ps[:, n % 2, N * t:N * t + N], q[:, n, 128 * t:128 * t + 128], k[:, n, :], start=True, stop=True)
                last.then_inc(n_max_full, 1)

            def maxima_T(i, s):
                pe.wait_ge(n_v, at(i, STEPS, s + 1))
                pe.wait_ge(n_nm_parts, at(i, STEPS, s + 1))
                for t in range(TT):
                    last = pe.transpose(ps[:, 4 + s % ROWS, 128 * t:128 * t + 128], TB["bmxs"][s % ROWS][:, t, :].bitcast(F32), ident[:])
                last.then_inc(n_nmT_psum, 1)

            def scores(i, s, n):
                h = ORDER8[n]
                q, k = TB["bqst"][s % ROWS], TB["bkst"][s % ROWS]
                if n % 4 == 0:
                    pe.wait_ge(n_nmT, at(i, 2 * STEPS, 2 * s + n // 4 + 1))
                if H1 * s + n >= 2:
                    pe.wait_ge(n_probs, at(i, STEPS * H1, H1 * s + n - 1))
                for kt in range(TT):
                    last = mm(ps[:, 2 + n % 2, N * kt:N * kt + N], k[:, h, 128 * kt:128 * kt + 128], q[:, h, :], start=True, stop=True)
                last.then_inc(n_score, 1)

            def value_quad(i, s, half, kt):
                r = s % ROWS
                if kt == 0:
                    pe.wait_ge(n_probs, at(i, STEPS * H1, H1 * s + 4 * half + 4))
                for j in range(4):
                    h = 2 * j + half
                    mm(ps[32 * j:32 * j + 32, 4 + r, 0:N], TB["vpad"][r][:, kt, h, :], TB["probs"][:, h, N * kt:N * kt + N],
                       start=(half == 0 and kt == 0), stop=(half == 1 and kt == TT - 1), skip_group_check=True,
                       tile_position=(0, 32 * j))

            def sum_quad(i, s, half):
                pe.wait_ge(n_sum, at(i, STEPS * H1, H1 * s + 4 * half + 4))
                for j in range(4):
                    last = mm(ps[32 * j:32 * j + 32, 4 + s % ROWS, N:2 * N], sumsel[:, half, :], TB["sums"][:, 2 * j + half, :],
                              start=False, stop=(half == 1), skip_group_check=True, tile_position=(0, 32 * j))
                last.then_inc(n_pv, 1)

            def through_wo(i, s):
                c, r = divmod(s, ROWS)
                pe.wait_ge(n_ctxo, at(i, STEPS, s + 1))
                mm(ps[:, 4 + r, 0:N], fw[:, c, 4, :], TB["bctx"][r][:], start=True, stop=True).then_inc(n_wo, 1)

            def last_node_T(i, r):
                pe.wait_ge(n_node, at(i, STEPS, STEPS - ROWS + r + 1))
                for t in range(TT):
                    last = pe.transpose(ps[:, 4 + r, N + 128 * t:N + 128 * t + 128], TB["nodes"][r][:, NODES, 128 * t:128 * t + 128], ident[:])
                last.then_inc(last_T, 1)

            with pe.Fori(0, TURNS_B) as i:
                for s in range(ROWS):
                    proj_qk(i, s)
                for s in range(ROWS):
                    proj_v(i, s)
                for n in range(H1):
                    row_max(i, 0, n)
                maxima_T(i, 0)
                for s in range(STEPS):
                    more = s + 1 < STEPS
                    for n in range(H1):
                        if n == 7 and more:
                            maxima_T(i, s + 1)
                        if more and n == 0:
                            row_max(i, s + 1, 0)
                        scores(i, s, n)
                        if more and n < 7:
                            row_max(i, s + 1, n + 1)
                        if n == 1 and s:
                            value_quad(i, s - 1, 1, 0)
                            value_quad(i, s - 1, 1, 1)
                        if n == 2 and s:
                            sum_quad(i, s - 1, 1)
                        if n == 3 and s >= 2 and s + 2 < STEPS:
                            proj_v(i, s + 2)
                        if n == 5:
                            if s:
                                through_wo(i, s - 1)
                            value_quad(i, s, 0, 0)
                        if n == 6:
                            value_quad(i, s, 0, 1)
                            if s and s + 3 < STEPS:
                                proj_qk(i, s + 3)
                        if n == 7:
                            sum_quad(i, s, 0)
                for r in range(ROWS - 1):
                    last_node_T(i, r)
                value_quad(i, STEPS - 1, 1, 0)
                value_quad(i, STEPS - 1, 1, 1)
                sum_quad(i, STEPS - 1, 1)
                through_wo(i, STEPS - 1)
                last_node_T(i, ROWS - 1)

        @block.scalar
        def _(act):
            a = nc.scalar
            act.wait_ge(w_in, 16 * N_W)
            a.activation(tanh_g[:], cst[:, C_GX:C_GX + 4], ACT.Tanh).then_inc(gates_tanh, 1)

            def xT_copy(i, row, l, dst, bank, c0):
                act.wait_ge(xnT_psum[l], at(i, 1, row + 1))
                a.copy(dst[:], ps[:, bank, c0:c0 + N]).then_inc(xnT_ready[l], 1)

            def hi_copy(i, row, n):
                act.wait_ge(fill_full, at(i, 20, 20 * row + n + 1))
                if n < 8:
                    dst = k12[:, 0, n, :]
                elif n < 12:
                    dst = q12[:, 0, 2 * (n - 8):2 * (n - 8) + 2, :].rearrange("p a b -> p (a b)")
                else:
                    k, h = divmod(n - 12, 2)
                    dst = v0[:, k, 512 * h:512 * h + 512]
                a.copy(dst, ps[:, 2 + n % 4, :]).then_inc(hi_done, 1)

            def ipa_exponentials(i, row):
                act.wait_ge(ipa_shifted, at(i, 1, row + 1))
                a.activation(pi[:, :, :], pi[:, :, :], ACT.Exp, scale=SCALE0).then_inc(ipa_exp, 1)

            def maxima(i, row, gr):
                act.wait_ge(nmT_psum, at(i, H0 // GH, H0 // GH * row + gr + 1))
                if gr:
                    act.wait_ge(score_full, at(i, H0, H0 * row + GH * gr))
                a.copy(nmT[:], ps[:, 0, 0:N]).then_inc(nmT_ready, 1)

            def head_exp(i, row, h):
                act.wait_ge(score_full, at(i, H0, H0 * row + h + 1))
                if h >= 2:
                    act.wait_ge(pv_head, at(i, H0, H0 * row + h - 1))
                    act.wait_ge(sum_ready, at(i, H0, H0 * row + h - 1))
                b = 2 + 2 * (h % 2)
                a.activation(probs[:, h % 2, 0:3 * N], ps[:, b:b + 2, :].rearrange("p a b -> p (a b)")[:, 0:3 * N],
                             ACT.Exp, scale=SCALE0)
                a.activation(probs[0:SM - 384, h % 2, 3 * N:4 * N], ps[0:SM - 384, b + 1, N:2 * N],
                             ACT.Exp, scale=SCALE0).then_inc(probs_ready, 1)

            def l1_queries(i, row):
                act.wait_ge(x_proj, at(i, 1, row + 1))
                a.activation(qx12[:, 0, :], ps[:, 7, 0:N], ACT.Identity, bias=cst[:, C_BQ:C_BQ + 1]).then_inc(x_hi, 1)

            def first_heads(i, row, after):
                for h in range(GH):
                    if h == 3 and after:
                        l1_queries(i, row - 1)
                    head_exp(i, row, h)
                    if h == 1 and after:
                        xT_copy(i, row - 1, 2, xnT, 7, N)
                maxima(i, row, 1)

            def heads(i, row):
                for h in range(GH, H0):
                    head_exp(i, row, h)
                    if h % GH == GH - 1 and h // GH + 1 < H0 // GH:
                        maxima(i, row, h // GH + 1)
                act.wait_ge(ipa_T, at(i, 1, row + 1))
                a.copy(piT[:], ps[0:64, 0, 0:N]).then_inc(ipa_ready, 1)

            def loop_a_turn(i, row, more):
                heads(i, row)
                if more:
                    hi_copy(i, row + 1, 0)
                    hi_copy(i, row + 1, 1)
                    xT_copy(i, row + 1, 0, xn0T, 6, N)
                    for n in range(2, ROUTER_AT):
                        hi_copy(i, row + 1, n)
                        if n == 8:
                            ipa_exponentials(i, row + 1)
                xT_copy(i, row, 1, xnT, 6, 0)
                if more:
                    for n in range(ROUTER_AT, 15):
                        hi_copy(i, row + 1, n)
                act.wait_ge(gap_ready, at(i, 1, row + 1))
                a.activation(gw[:, 1, :], gw[:, 0, :], ACT.Exp).then_inc(gap_exp, 1)
                if more:
                    for n in range(15, 19):
                        hi_copy(i, row + 1, n)
                for n in range(16):
                    act.wait_ge(h_full, at(i, 16, 16 * row + n + 1))
                    if n >= 2:
                        act.wait_ge(hs_ready, at(i, 16, 16 * row + n - 1))
                    a.activation(th[:, n % 2, :], ps[:, 2 + n % 2, :], ACT.Tanh, scale=0.5).then_inc(tanh_done, 1)
                    if n == 0 and more:
                        hi_copy(i, row + 1, 19)
                    if n == 11:
                        act.wait_ge(ctx_used, at(i, 1, row + 1))
                        act.wait_ge(x_parts_out, at(i, 96, 96 * row + 96))
                        a.activation(kx12[:, 0, :], ps[:, 4, :], ACT.Identity, bias=cst[:, C_BK:C_BK + 1]).then_inc(x_hi, 1)
                    if n == 12 and more:
                        maxima(i, row + 1, 0)
                if more:
                    first_heads(i, row + 1, True)
                else:
                    xT_copy(i, row, 2, xnT, 7, N)
                    l1_queries(i, row)

            xT_copy(None, 0, 0, xn0T, 6, N)
            for n in range(20):
                hi_copy(None, 0, n)
                if n == 5:
                    ipa_exponentials(None, 0)
            maxima(None, 0, 0)
            first_heads(None, 0, False)
            with act.Fori(0, B - 1) as i:
                loop_a_turn(i, 0, True)
            loop_a_turn(None, B - 1, False)
            act.wait_ge(x_lo, 2 * B)
            a.copy(tanh_g[:, 0:1], tanh_g[:, 0:1]).then_inc(loop_a_done, 1)

            def c_v_copy(i, m):
                act.wait_ge(c_v_full, count(i, m, 1, 1))
                if m >= 2 or i is not None:
                    act.wait_ge(c_pv, count(i, m - 2, 2, 2))
                for o in range(2):
                    last = a.copy(cv[m % 2][:, :, :, :].rearrange("p k (j e) c -> p k j e c", e=2)[:, :, :, o, 16 * o:16 * o + 16],
                                  ps[:, 4 + m % 2, :].rearrange("p (k j e c) -> p k j e c", k=KT, e=2, c=16)[:, :, :, o, :])
                last.then_inc(c_v, 1)

            def c_maxima(i, m, half):
                act.wait_ge(c_nmT_psum, count(i, m, 1, 1))
                a.copy(cq[m % 2][64:128, :, :].rearrange("p (j e) q -> p j e q", e=2)[:, :, half, :],
                       ps[64:128, 4 + m % 2, 0:N].unsqueeze(1).broadcast_to((64, 4, N))).then_inc(c_nmT, 1)

            def c_exp(i, m, n):
                act.wait_ge(c_score, count(i, m, CU, n + 1))
                if m and n % 8 == 0:
                    act.wait_ge(c_pv, count(i, m - 1, 2, n // 8 + 1))
                a.activation(cprobs[:, ORDER8[n // 2], 2 * N * (n % 2):2 * N * (n % 2) + 2 * N], ps[:, 2 + n % 2, :],
                             ACT.Exp, scale=SCALE1).then_inc(c_probs, 1)

            def c_x3T_copy(i, m):
                b = step_index(i, m)
                act.wait_ge(c_x3T_psum, count(i, m, 1, 1))
                dst = x3T_all[:, bass.ds(b, 1), :] if i is not None else x3T_all[:, b, :]
                a.copy(dst, ps[:, 6 + m % 2, N:2 * N]).then_inc(c_x3T, 1)

            def c_step(i, m, more):
                for n in range(CU):
                    c_exp(i, m, n)
                    if n == 9 and more:
                        c_v_copy(i, m + 1)
                    if n >= 14 and more:
                        c_maxima(i, m + 1, n - 14)
                if m:
                    c_x3T_copy(i, m - 1)

            act.wait_ge(loop_a_done, 3)
            for p in range(2):
                for u in range(KT):
                    a.copy(ck[p][64:128, :, 128 * u:128 * u + 128], sel8f[64:128, :, :])
            act.wait_ge(pool_const, 3)
            c_v_copy(None, 0)
            c_maxima(None, 0, 0)
            c_maxima(None, 0, 1)
            c_step(None, 0, True)
            with act.Fori(0, TURNS_C) as i:
                c_step(i, 1, True)
                c_step(i, 2, True)
            c_step(None, B - 1, False)
            c_x3T_copy(None, B - 1)
            act.wait_ge(c_x3T, B)
            a.copy(tanh_g[:, 1:2], tanh_g[:, 1:2]).then_inc(loop_c_done, 1)

            act.wait_ge(loop_c_done, 3)
            for r in range(ROWS):
                for u in range(2):
                    a.copy(TB["bkst"][r][64:128, :, 128 * u:128 * u + 128], sel8f[64:128, :, :])
            act.wait_ge(fb_done, NODES + 1)
            act.wait_ge(pool_const, 4)
            act.sem_inc(last_out, ROWS)

            def hi_parts(i, s):
                c, r = divmod(s, ROWS)
                act.wait_ge(n_proj, at(i, STEPS, s + 1))
                if c:
                    act.wait_ge(n_parts_out[r], at(i, 96 * NODES, 96 * c))
                for n in range(2):
                    last = a.activation(TB["qk12"][r][:, 0, n, :], ps[:, 4 + r, N * n:N * n + N], ACT.Identity, bias=fb[:, c, n:n + 1])
                last.then_inc(n_hi, 1)

            def v_and_q(i, s):
                c, r = divmod(s, ROWS)
                act.wait_ge(n_v_full, at(i, STEPS, s + 1))
                for o in range(2):
                    a.copy(TB["vpad"][r][:, :, :, :].rearrange("p k (j e) c -> p k j e c", e=2)[:, :, :, o, 16 * o:16 * o + 16],
                           ps[:, 4 + r, 0:TT * D].rearrange("p (k j e c) -> p k j e c", k=TT, e=2, c=16)[:, :, :, o, :])
                a.activation(TB["qn"][r][:], ps[:, 4 + r, N:2 * N], ACT.Identity, bias=fb[:, c, 3:4]).then_inc(n_v, 1)

            def maxima(i, s, half):
                act.wait_ge(n_nmT_psum, at(i, STEPS, s + 1))
                dst = TB["bqst"][s % ROWS][64:128, :, :].rearrange("p (j e) q -> p j e q", e=2)[:, :, half, :]
                src = ps[64:128, 4 + s % ROWS, 0:N].unsqueeze(1).broadcast_to((64, 4, N))
                a.copy(dst, src).then_inc(n_nmT, 1)

            def exps(i, s, n):
                act.wait_ge(n_score, at(i, STEPS * H1, H1 * s + n + 1))
                if s and n % 4 == 0:
                    act.wait_ge(n_pv, at(i, 2 * STEPS, 2 * s - 1 + n // 4))
                a.activation(TB["probs"][:, ORDER8[n], :], ps[:, 2 + n % 2, :], ACT.Exp, scale=SCALE1).then_inc(n_probs, 1)

            with act.Fori(0, TURNS_B) as i:
                act.wait_ge(last_out, at(i, ROWS, ROWS))
                for r in range(ROWS):
                    a.copy(TB["nodes"][r][:, 0, :], x3T_all[:, bass.ds(ROWS * i + r, 1), :]).then_inc(rows_in, 1)
                for s in range(ROWS):
                    hi_parts(i, s)
                for s in range(ROWS):
                    v_and_q(i, s)
                maxima(i, 0, 0)
                maxima(i, 0, 1)
                for s in range(STEPS):
                    more = s + 1 < STEPS
                    for n in range(H1):
                        exps(i, s, n)
                        if n == 4 and s >= 2 and s + 2 < STEPS:
                            v_and_q(i, s + 2)
                        if n == 6 and more:
                            maxima(i, s + 1, 0)
                    if more:
                        maxima(i, s + 1, 1)
                    if s and s + 3 < STEPS:
                        hi_parts(i, s + 3)

        @block.vector
        def _(dve):
            v = nc.vector
            chain = [0]

            def link(turn, per_turn, base, ins):
                chain[0] += 1
                ins.then_inc(dve_chain, 1)
                dve.wait_ge(dve_chain, at(turn, per_turn, base + chain[0]))

            def plink(ins):
                link(None, 0, 0, ins)

            v.memset(kblk, 0.0)
            v.memset(vblk, 0.0)
            v.memset(probs[96:128, :, 3 * N:4 * N], 0.0)
            dve.wait_ge(w_in, 16 * N_W)
            plink(v.tensor_scalar(cst[:, C_QA:C_OA + 1], cst[:, C_QA:C_OA + 1], 1.0 / RANK, None, ALU.mult))
            dve.wait_ge(gates_tanh, 1)
            dve.wait_ge(pool_const, 2)
            v.tensor_scalar(boT[:], cst[:, C_BO0:C_BO0 + D], tanh_g[:, 0:1], None, ALU.mult)
            v.tensor_scalar(gb[:, 0, :], cst[:, C_LG:C_LG + D], tanh_g[:, 3:4], None, ALU.mult)
            v.tensor_scalar(gb[:, 1, :], cst[:, C_LB:C_LB + D], tanh_g[:, 3:4], None, ALU.mult)
            v.tensor_scalar(xw[:, 3, :], xw[:, 3, :], tanh_g[:, 1:2], None, ALU.mult)
            v.tensor_scalar(xrow[:], cst[:, C_BO1:C_BO1 + D], tanh_g[:, 1:2], None, ALU.mult)
            v.tensor_scalar(tmp128[:], ones[:], cst[:, C_BV:C_BV + 1], None, ALU.mult).then_inc(dve_const, 1)
            dve.wait_ge(fold_psum, 1)
            v.scalar_tensor_tensor(wq[:], ps[:, 0:2, :].rearrange("p a b -> p (a b)"), cst[:, C_QA:C_QA + 1], wq[:],
                                   ALU.mult, ALU.add).then_inc(fold_done, 1)
            v.scalar_tensor_tensor(wk[:], ps[0:96, 2:4, :].rearrange("p a b -> p (a b)"), cst[0:96, C_KA:C_KA + 1], wk[:],
                                   ALU.mult, ALU.add).then_inc(fold_done, 1)
            v.scalar_tensor_tensor(wv[:], ps[0:96, 4:6, :].rearrange("p a b -> p (a b)"), cst[0:96, C_VA:C_VA + 1], wv[:],
                                   ALU.mult, ALU.add).then_inc(fold_done, 1)
            wo_f = wo[:, :, :].rearrange("p a b -> p (a b)")
            plink(v.scalar_tensor_tensor(wo_f, ps[:, 6:8, :].rearrange("p a b -> p (a b)"), cst[:, C_OA:C_OA + 1], wo_f,
                                         ALU.mult, ALU.add))
            v.tensor_scalar(wo_f, wo_f, tanh_g[:, 0:1], None, ALU.mult).then_inc(fold_done, 1)
            dve.wait_ge(fold_psum, 2)
            for s in range(2):
                rows = slice(64 * s, 64 * s + 64)
                v.tensor_copy(kblk[rows, :, s, :], ps[rows, 0, 0:256].rearrange("p (j c) -> p j c", c=32)).then_inc(fold_done, 1)
                v.tensor_copy(vblk[rows, :, s, :], ps[rows, 0, 256:512].rearrange("p (j c) -> p j c", c=32)).then_inc(fold_done, 1)
            for h in range(2):
                v.tensor_copy(wqT[:, 4 * h:4 * h + 4, :], ps[:, 1 + h, :].rearrange("p (j c) -> p j c", j=4)).then_inc(fold_done, 1)
            dve.wait_ge(fold_psum, 3)
            v.tensor_copy(g_ipa[:, :, :].rearrange("p b (t h) -> p h b t", t=IPA),
                          ps[:, 3, :].rearrange("p (h b t) -> p h b t", b=B, t=IPA)).then_inc(fold_done, 1)
            for h in range(2):
                v.tensor_copy(vwsb[:, 4 * h:4 * h + 4, :], ps[0:64, 4 + h, :].rearrange("p (j c) -> p j c", j=4)).then_inc(fold_done, 2)
            dve.wait_ge(fold_psum, 4)
            v.tensor_tensor(xrow[:], ps[:, 6, 0:128], xrow[:], ALU.add).then_inc(fold_done, 1)
            CH = CH_DVE_A

            def lnk(i, ins, apart=False):
                chain[0] += 1
                ins.then_inc(dve_chain, 1)
                if apart:
                    wait_apart(dve, apart_tally, dve_chain, at(i, CH, chain[0]))
                else:
                    dve.wait_ge(dve_chain, at(i, CH, chain[0]))

            def ln_stats(i, l, src, st, mean_var):
                for t in range(TT):
                    ins = v.bn_stats(st[:, t, :], src(t))
                lnk(i, ins, apart=True)
                for t in range(TT):
                    ins = v.bn_aggr(mean_var[:, t, :], st[:, t, :])
                ins.then_inc(ln_var[l], 1)

            def ln_apply(i, row, l, src, dst, mean_var, rs):
                dve.wait_ge(ln_rstd[l], at(i, 1, row + 1))
                for t in range(TT):
                    ins = v.tensor_scalar(dst[:, t, :], src(t), mean_var[:, t, 0:1], rs[:, t:t + 1], ALU.subtract, ALU.mult)
                ins.then_inc(xn_ready[l], 1)

            x_row = lambda i, row: x_all[:, bass.ds(TT * i + TT * row, TT), :] if i is not None else x_all[:, TT * row:TT * row + TT, :]
            of_next = lambda t: x_next[:, t, :]
            of_xs = lambda t: xs[:, t, :]
            over_t = lambda x: x.rearrange("p (a h) -> p a h", a=TT).unsqueeze(3).broadcast_to((128, TT, H0, IPA))
            pi4 = pi[:, :, :].rearrange("p a (t h) -> p a h t", t=IPA)

            def ipa_shift(i, row):
                dve.wait_ge(ipa_scores, at(i, 1, row + 1))
                s4 = ps[:, 7, 0:TT * 64].rearrange("p (a t h) -> p a h t", t=IPA, a=TT)
                lnk(i, v.tensor_reduce(pis[:, 0, :], s4, AX.X, ALU.max))
                v.tensor_tensor(pi4, s4, over_t(pis[:, 0, :]), ALU.subtract).then_inc(ipa_shifted, 1)

            def ipa_normalize(i, row):
                dve.wait_ge(ipa_exp, at(i, 1, row + 1))
                lnk(i, v.tensor_reduce(pis[:, 0, :], pi4, AX.X, ALU.add))
                lnk(i, v.reciprocal(pis[:, 1, :], pis[:, 0, :]))
                v.tensor_tensor(pi4, pi4, over_t(pis[:, 1, :]), ALU.mult).then_inc(ipa_probs, 1)

            def lo_part(i, row, n):
                dve.wait_ge(hi_done, at(i, 20, 20 * row + n + 1))
                if n < 8:
                    hi, lo = (k12[:, p, n, :] for p in range(2))
                else:
                    hi, lo = (q12[:, p, 2 * (n - 8):2 * (n - 8) + 2, :].rearrange("p a b -> p (a b)") for p in range(2))
                v.tensor_tensor(lo, ps[:, 2 + n % 4, :], hi.bitcast(F32), ALU.subtract).then_inc(lo_done, 1)

            def row_max(i, row, h):
                dve.wait_ge(max_full, at(i, H0, H0 * row + h + 1))
                v.tensor_reduce(nm[:, :, h:h + 1], ps[:, 0:2, 0:SM], AX.X, ALU.max, negate=True).then_inc(max_done, 1)
                if h % GH == GH - 1:
                    gr = h // GH
                    dve.wait_ge(max_done, at(i, H0, H0 * row + h + 1))
                    if gr:
                        dve.wait_ge(nmT_psum, at(i, H0 // GH, H0 // GH * row + gr))
                    src = nm[:, :, GH * gr:GH * gr + GH]
                    hi = mxs[:, :, :].rearrange("p t (a b) -> p t a b", a=2)[:, :, :, 0:GH]
                    lo = mxs[:, :, :].rearrange("p t (a b) -> p t a b", a=2)[:, :, :, 32:32 + GH]
                    srcb = src.unsqueeze(2).broadcast_to((128, TT, 2, GH))
                    lnk(i, v.tensor_copy(hi, srcb))
                    v.tensor_tensor(lo, srcb, hi.bitcast(F32), ALU.subtract).then_inc(nm_parts, 1)

            def pair(i, row, j):
                dve.wait_ge(pv_head, at(i, H0, H0 * row + 2 * j + 2))
                dve.wait_ge(sum_done, at(i, H0, H0 * row + 2 * j + 2))
                b = 6 + j % 2
                if j:
                    dve.wait_ge(pair_out, at(i, PAIRS, PAIRS * row + j))
                lnk(i, v.reciprocal(rsum[:], ps[:, b, N:2 * N]))
                v.tensor_tensor(outT[:, j, :], ps[:, b, 0:N], rsum[:], ALU.mult).then_inc(pair_out, 1)

            def gates(i, row):
                dve.wait_ge(logits_full, at(i, 1, row + 1))
                lnk(i, v.tensor_copy(lg[:, :, :], ps[:, 7, 256:256 + TT * E].rearrange("p (t e) -> p t e", t=TT)), apart=True)
                for t in range(TT):
                    ins = v.max(top[:, t, :], lg[:, t, :])
                lnk(i, ins)
                v.tensor_tensor(gw[:, 0, :], top[:, :, 1], top[:, :, 0], ALU.subtract).then_inc(gap_ready, 1)
                for t in range(TT):
                    ins = v.max_index(topi[:, t, :], top[:, t, :], lg[:, t, :])
                lnk(i, ins)
                lnk(i, v.tensor_copy(topf[:, :, :], topi[:, :, :]))
                for t in range(TT):
                    v.tensor_scalar(gate[:, t, :], iota8[:], topf[:, t, 0:1], None, ALU.is_equal)
                    ins = v.tensor_scalar(gate2[:, t, :], iota8[:], topf[:, t, 1:2], None, ALU.is_equal)
                dve.wait_ge(gap_exp, at(i, 1, row + 1))
                lnk(i, v.tensor_scalar(gw[:, 2, :], gw[:, 1, :], 1.0, None, ALU.add))
                lnk(i, v.reciprocal(gw[:, 3, :], gw[:, 2, :]))
                lnk(i, v.tensor_scalar(gw[:, 4, :], gw[:, 3, :], tanh_g[:, 2:3], 0.5, ALU.mult, ALU.mult))
                lnk(i, v.tensor_tensor(gw[:, 5, :], gw[:, 4, :], gw[:, 1, :], ALU.mult))
                for t in range(TT):
                    ins = v.tensor_scalar(gate[:, t, :], gate[:, t, :], gw[:, 4, t:t + 1], None, ALU.mult)
                lnk(i, ins)
                for t in range(TT):
                    ins = v.scalar_tensor_tensor(gate[:, t, :], gate2[:, t, :], gw[:, 5, t:t + 1], gate[:, t, :], ALU.mult, ALU.add)
                lnk(i, ins)

            def experts(i, row, g):
                dve.wait_ge(w2_done, at(i, 16, 16 * row + 4 * g + 4))
                for e in (2 * g, 2 * g + 1):
                    for t in range(TT):
                        c0 = 256 * (e % 2) + 128 * t
                        y = ps[:, 4 + g, c0:c0 + 128]
                        ins = v.scalar_tensor_tensor(xs[:, t, :], y, gate[:, t, e:e + 1], xs[:, t, :], ALU.mult, ALU.add)
                    lnk(i, ins)

            def first_ln(i, row):
                lnk(i, v.tensor_copy(x_next[:, :, :], x_row(i, row)))
                ln_stats(i, 0, of_next, st0, mv0)

            def l1_lo(i, row, part):
                dve.wait_ge(x_hi, at(i, 2, 2 * row + part + 1))
                bank, n, both, bias = ((4, S, kx12, C_BK), (7, N, qx12, C_BQ))[part]
                v.scalar_tensor_tensor(both[:, 1, :], ps[:, bank, 0:n], cst[:, bias:bias + 1], both[:, 0, :].bitcast(F32),
                                       ALU.add, ALU.subtract).then_inc(x_lo, 1)

            def keep_x2(i, row):
                lnk(i, v.tensor_tensor(x_row(i, row), xs[:, :, :],
                                       xrow[:].unsqueeze(1).broadcast_to((128, TT, D)), ALU.add))

            def loop_a_turn(i, row, more):
                for h in range(GH, H0):
                    if h + GH < H0:
                        row_max(i, row, h + GH)
                    if h == LN0_AT and more:
                        first_ln(i, row + 1)
                    if h == LN0_AT + 2 and more:
                        ln_apply(i, row + 1, 0, of_next, xn0, mv0, rstd0)
                    if h % 2 == 0:
                        pair(i, row, h // 2 - 2)
                pair(i, row, PAIRS - 2)
                if more:
                    lo_part(i, row + 1, 0)
                pair(i, row, PAIRS - 1)
                if more:
                    lo_part(i, row + 1, 1)
                dve.wait_ge(y_full, at(i, 1, row + 1))
                y = ps[:, 1, 0:TT * D].rearrange("p (t d) -> p t d", t=TT)
                lnk(i, v.tensor_tensor(xs[:, :, :], y, x_row(i, row), ALU.add))
                lnk(i, v.tensor_tensor(xs[:, :, :], xs[:, :, :], boT[:].unsqueeze(1).broadcast_to((128, TT, D)), ALU.add))
                ln_stats(i, 1, of_xs, st6, mv)
                if more:
                    lo_part(i, row + 1, 2)
                    lo_part(i, row + 1, 3)
                ln_apply(i, row, 1, of_xs, xn, mv, rstd)
                if more:
                    ipa_shift(i, row + 1)
                    for n in range(4, 12):
                        lo_part(i, row + 1, n)
                gates(i, row)
                if more:
                    ipa_normalize(i, row + 1)
                for n in range(16):
                    dve.wait_ge(tanh_done, at(i, 16, 16 * row + n + 1))
                    if n >= 3:
                        dve.wait_ge(w2_done, at(i, 16, 16 * row + n - 2))
                    v.scalar_tensor_tensor(hs[:, n % 3, :, :].rearrange("p a b -> p (a b)"), th[:, n % 2, :], 1.0,
                                           ps[:, 2 + n % 2, :], ALU.add, ALU.mult).then_inc(hs_ready, 1)
                    if more and n - 1 in MAX_AT:
                        row_max(i, row + 1, MAX_AT.index(n - 1))
                    if n in (6, 10, 14):
                        experts(i, row, (n - 6) // 4)
                    if n == 12:
                        l1_lo(i, row, 0)
                if more:
                    row_max(i, row + 1, GH)
                experts(i, row, 3)
                ln_stats(i, 2, of_xs, st6, mv)
                ln_apply(i, row, 2, of_xs, xn, mv, rstd)
                keep_x2(i, row)
                if more:
                    row_max(i, row + 1, GH + 1)
                    row_max(i, row + 1, GH + 2)
                l1_lo(i, row, 1)
                if more:
                    row_max(i, row + 1, GH + 3)

            first_ln(None, 0)
            ln_apply(None, 0, 0, of_next, xn0, mv0, rstd0)
            ipa_shift(None, 0)
            for n in range(12):
                lo_part(None, 0, n)
            ipa_normalize(None, 0)
            for h in range(2 * GH):
                row_max(None, 0, h)
            pro = chain[0]
            with dve.Fori(0, B - 1) as i:
                loop_a_turn(i, 0, True)
                assert chain[0] - pro == CH_DVE_A, f"CH_DVE_A = {chain[0] - pro}"
            chain[0] = pro + CH_DVE_A * (B - 1)
            loop_a_turn(None, B - 1, False)
            dve.wait_ge(x_lo, 2 * B)
            v.memset(nm[:, 0, 0:1], 0.0).then_inc(loop_a_done, 1)
            dve.wait_ge(loop_a_done, 3)

            for p in range(2):
                for stack in (cq[p], ck[p]):
                    v.memset(stack[32:64, :, :].bitcast(F32), 0.0)
            v.memset(csum[:, 0, 0:1], 0.0).then_inc(c_zeroed, 1)
            base_c = chain[0]
            CHC = 4

            def lnc(i, m, k, ins, apart=False):
                ins.then_inc(dve_chain, 1)
                value = count(i, m, CHC, base_c + k)
                if apart:
                    wait_apart(dve, apart_tally, dve_chain, value)
                else:
                    dve.wait_ge(dve_chain, value)

            def c_row_max(i, m, n):
                h, t = ORDER8[n // 2], n % 2
                dve.wait_ge(c_max_full, count(i, m, CU, n + 1))
                if n == 0 and m:
                    dve.wait_ge(c_nm_parts, count(i, m - 1, 1, 1))
                v.tensor_reduce(cnm[:, t, h:h + 1], ps[:, t, :], AX.X, ALU.max, negate=True).then_inc(c_max_done, 1)

            def c_nm_split(i, m):
                dve.wait_ge(c_max_done, count(i, m, CU, CU))
                if m:
                    dve.wait_ge(c_nmT_psum, count(i, m - 1, 1, 1))
                v.tensor_copy(cmxs[:, :, 64:64 + H1], cnm[:, :, :]).then_inc(c_hi, 1)
                dve.wait_ge(c_hi, count(i, m, 1, 1))
                v.tensor_tensor(cmxs[:, :, 96:96 + H1], cnm[:, :, :], cmxs[:, :, 64:64 + H1].bitcast(F32),
                                ALU.subtract).then_inc(c_nm_parts, 1)

            def c_normalize(i, m):
                dve.wait_ge(c_pv, count(i, m, 2, 2))
                if m:
                    dve.wait_ge(c_ctxo, count(i, m - 1, 1, 1))
                    dve.wait_ge(c_y, count(i, m - 1, 1, 1))
                lnc(i, m, 1, v.reciprocal(crs[:], ps[:, 4 + m % 2, N:2 * N]))
                v.tensor_tensor(cctx[:], ps[:, 4 + m % 2, 0:N], crs[:], ALU.mult).then_inc(c_ctxo, 1)

            def c_add(i, m):
                b = step_index(i, m)
                x_b = x_all[:, bass.ds(TT * b, TT), :] if i is not None else x_all[:, TT * b:TT * b + TT, :]
                dve.wait_ge(c_y, count(i, m, 1, 1))
                if m:
                    dve.wait_ge(c_xn, count(i, m - 1, 1, 1))
                y = ps[:, 6 + m % 2, 0:TT * D].rearrange("p (t d) -> p t d", t=TT)
                lnc(i, m, 2, v.tensor_tensor(cx[:, :, :], y, x_b, ALU.add))
                for t in range(TT):
                    ins = v.bn_stats(st6[:, t, :], cx[:, t, :])
                lnc(i, m, 3, ins, apart=True)
                for t in range(TT):
                    ins = v.bn_aggr(mv[:, t, :], st6[:, t, :])
                ins.then_inc(c_var, 1)
                lnc(i, m, 4, v.tensor_tensor(x_b, cx[:, :, :], gb[:, 1, :].unsqueeze(1).broadcast_to((128, TT, D)), ALU.add))

            def c_ln(i, m):
                dve.wait_ge(c_rstd, count(i, m, 1, 1))
                if m:
                    dve.wait_ge(c_x3T_psum, count(i, m - 1, 1, 1))
                for t in range(TT):
                    ins = v.tensor_scalar(cxn[:, t, :], cx[:, t, :], mv[:, t, 0:1], rstd[:, t:t + 1], ALU.subtract, ALU.mult)
                ins.then_inc(c_xn, 1)

            def c_step(i, m, more):
                for n in range(CU):
                    if more:
                        c_row_max(i, m + 1, n)
                    if n == 7 and m:
                        c_normalize(i, m - 1)
                    if n == 11 and m:
                        c_add(i, m - 1)
                    if n == 15 and more:
                        c_nm_split(i, m + 1)
                    if n == 15 and m:
                        c_ln(i, m - 1)

            for n in range(CU):
                c_row_max(None, 0, n)
            c_nm_split(None, 0)
            c_step(None, 0, True)
            with dve.Fori(0, TURNS_C) as i:
                c_step(i, 1, True)
                c_step(i, 2, True)
            c_step(None, B - 1, False)
            c_normalize(None, B - 1)
            c_add(None, B - 1)
            c_ln(None, B - 1)
            dve.wait_ge(c_x3T, B)
            v.memset(cnm[:, 0, 0:1], 0.0).then_inc(loop_c_done, 1)
            chain[0] += CHC * B

            dve.wait_ge(loop_c_done, 3)
            dve.wait_ge(w_b_in, 16 * N_B)
            for c in range(NODES):
                ew = lambda n: cst[:, C_EW + 3 * c + n:C_EW + 3 * c + n + 1]
                aw = cst[:, C_AW + c:C_AW + c + 1]
                dve.wait_ge(fb_psum, c + 1)
                for n in range(3):
                    v.tensor_scalar(fw[:, c, n, :], ps[:, c % 4, 128 * n:128 * n + 128], ew(n), None, ALU.mult)
                    v.tensor_scalar(fb[:, c, n:n + 1], ps[:, c % 4, 384 + n:385 + n], ew(n), None, ALU.mult)
                v.tensor_scalar(fw[:, c, 3, :], raw[:, c, 3, :], ew(0), None, ALU.mult)
                v.tensor_scalar(fb[:, c, 3:4], cst[:, C_BE + EDGES[c][0][0]:C_BE + EDGES[c][0][0] + 1], ew(0), None, ALU.mult)
                v.tensor_scalar(fw[:, c, 4, :], raw[:, c, 7, :], aw, None, ALU.mult).then_inc(fb_done, 1)
            dve.wait_ge(fb_psum, NODES + 1)
            for c in range(NODES):
                ins = v.tensor_scalar(fb[:, c, 4:5], ps[:, 5, c:c + 1], cst[:, C_AW + c:C_AW + c + 1], None, ALU.mult)
            ins.then_inc(fb_done, 1)
            dve.wait_ge(fb_done, NODES + 1)
            dve.wait_ge(pool_const, 4)
            base_b = chain[0]
            CHB = 2 * STEPS + 3 * ROWS

            def lnb(i, ins, apart=False):
                chain[0] += 1
                ins.then_inc(dve_chain, 1)
                if apart:
                    wait_apart(dve, apart_tally, dve_chain, at(i, CHB, chain[0]))
                else:
                    dve.wait_ge(dve_chain, at(i, CHB, chain[0]))

            def lo_parts(i, s):
                c, r = divmod(s, ROWS)
                dve.wait_ge(n_hi, at(i, STEPS, s + 1))
                for n in range(2):
                    ins = v.scalar_tensor_tensor(TB["qk12"][r][:, 1, n, :], ps[:, 4 + r, N * n:N * n + N], fb[:, c, n:n + 1],
                                                 TB["qk12"][r][:, 0, n, :].bitcast(F32), ALU.add, ALU.subtract)
                ins.then_inc(n_lo, 1)

            def row_max(i, s, n):
                dve.wait_ge(n_max_full, at(i, STEPS * H1, H1 * s + n + 1))
                v.tensor_reduce(TB["bnm"][s % ROWS][:, :, n:n + 1], ps[:, n % 2, :].rearrange("p (t k) -> p t k", t=TT), AX.X, ALU.max,
                                negate=True).then_inc(n_max_done, 1)

            def nm_split(i, s):
                bnm, bmx = TB["bnm"][s % ROWS], TB["bmxs"][s % ROWS]
                dve.wait_ge(n_max_done, at(i, STEPS * H1, H1 * s + H1))
                lnb(i, v.tensor_copy(bmx[:, :, 64:64 + H1], bnm[:, :, :]))
                v.tensor_tensor(bmx[:, :, 96:96 + H1], bnm[:, :, :], bmx[:, :, 64:64 + H1].bitcast(F32), ALU.subtract).then_inc(n_nm_parts, 1)

            def normalize(i, s):
                r = s % ROWS
                dve.wait_ge(n_pv, at(i, 2 * STEPS, 2 * s + 2))
                if s:
                    dve.wait_ge(n_ctxo, at(i, STEPS, s))
                lnb(i, v.reciprocal(TB["rs"][:], ps[:, 4 + r, N:2 * N]))
                v.tensor_tensor(TB["bctx"][r][:], ps[:, 4 + r, 0:N], TB["rs"][:], ALU.mult).then_inc(n_ctxo, 1)

            def node(i, s):
                c, r = divmod(s, ROWS)
                dve.wait_ge(n_wo, at(i, STEPS, s + 1))
                v.scalar_tensor_tensor(TB["nodes"][r][:, c + 1, :], ps[:, 4 + r, 0:N], fb[:, c, 4:5], TB["qn"][r][:],
                                       ALU.add, ALU.add).then_inc(n_node, 1)

            def last_source(r):
                return [ps[:, 4 + r, N + 128 * t:N + 128 * t + 128] for t in range(TT)]

            def last_stats(i, r):
                dve.wait_ge(last_T, at(i, ROWS, r + 1))
                for t in range(TT):
                    ins = v.bn_stats(TB["bst"][r][:, t, :], last_source(r)[t])
                lnb(i, ins, apart=True)
                for t in range(TT):
                    ins = v.bn_aggr(TB["bmv"][r][:, t, :], TB["bst"][r][:, t, :])
                ins.then_inc(last_var, 1)

            def last_ln(i, r):
                o, bmv = TB["o"][r], TB["bmv"][r]
                dve.wait_ge(stored[r], at(i, 16, 16))
                dve.wait_ge(last_rstd, at(i, ROWS, r + 1))
                for t in range(TT):
                    ins = v.tensor_scalar(o[:, t, :], last_source(r)[t], bmv[:, t, 0:1], TB["brstd"][r][:, t:t + 1],
                                          ALU.subtract, ALU.mult)
                lnb(i, ins)
                lnb(i, v.tensor_tensor(o[:, :, :], o[:, :, :], gb[:, 0, :].unsqueeze(1).broadcast_to((128, TT, D)), ALU.mult))
                v.tensor_tensor(o[:, :, :], o[:, :, :], x_all[:, bass.ds(TT * (ROWS * i + r), TT), :], ALU.add).then_inc(last_out, 1)

            with dve.Fori(0, TURNS_B) as i:
                for s in range(ROWS):
                    lo_parts(i, s)
                for n in range(H1):
                    row_max(i, 0, n)
                nm_split(i, 0)
                for s in range(STEPS):
                    more = s + 1 < STEPS
                    for n in range(H1):
                        if more:
                            row_max(i, s + 1, n)
                        if n == 1 and s >= 2 and s + 2 < STEPS:
                            lo_parts(i, s + 2)
                        if n == 3 and s:
                            normalize(i, s - 1)
                        if n == 5 and s:
                            node(i, s - 1)
                    if more:
                        nm_split(i, s + 1)
                for r in range(ROWS - 1):
                    last_stats(i, r)
                normalize(i, STEPS - 1)
                last_ln(i, 0)
                node(i, STEPS - 1)
                last_ln(i, 1)
                last_stats(i, ROWS - 1)
                for r in range(2, ROWS):
                    last_ln(i, r)
                assert chain[0] - base_b == CHB, f"CHB = {chain[0] - base_b}"


def kernel(**inputs):
    import concourse.bacc as bacc
    from concourse.bass_utils import run_bass_kernel_spmd

    I = {k: np.asarray(v) for k, v in inputs.items()}
    tr = lambda a: np.ascontiguousarray(np.swapaxes(a, -1, -2))
    row = lambda a: np.broadcast_to(a.reshape(1, -1), (128, a.size))
    col = lambda a: a.reshape(128, -1)
    cst = np.zeros((128, C_ALL), np.float32)
    for c0, a in (
        (C_GX, row(I["g_xattn"])), (C_GF, row(I["g_ffn"])), (C_QA, row(I["L0_xattn_q_alpha"])),
        (C_KA, row(I["L0_xattn_k_alpha"])), (C_VA, row(I["L0_xattn_v_alpha"])), (C_OA, row(I["L0_xattn_o_alpha"])),
        (C_EW, row(I["L1_ffn_ew"])), (C_AW, row(I["L1_ffn_act_w"])),
        (C_BQ, col(I["L1_xattn_bq"])), (C_BK, col(I["L1_xattn_bk"])), (C_BV, col(I["L1_xattn_bv"])),
        (C_BE, tr(I["L1_ffn_be"])), (C_WR, tr(I["L0_ffn_Wr"])),
        (C_BO0, row(I["L0_xattn_bo"])), (C_BO1, row(I["L1_xattn_bo"])),
        (C_LG, row(I["L1_ffn_ln_g"])), (C_LB, row(I["L1_ffn_ln_b"])),
    ):
        cst[:, c0:c0 + a.shape[1]] = a
    ctx = I["ctx_768"]
    arrays = {
        "cst": cst, "x": I["x"], "ctxT": tr(ctx),
        "ctx_ipaT": np.ascontiguousarray(ctx[:, SM:, :].reshape(B * IPA, CD).T),
        "q_downT": tr(I["L0_xattn_q_down"]), "k_downT": tr(I["L0_xattn_k_down"]), "v_downT": tr(I["L0_xattn_v_down"]),
        "o_downT": tr(I["L0_xattn_o_down"]), "q_up": I["L0_xattn_q_up"], "k_up": I["L0_xattn_k_up"],
        "v_up": I["L0_xattn_v_up"], "o_up": I["L0_xattn_o_up"],
        "Wq": I["L0_xattn_Wq"], "Wk": I["L0_xattn_Wk"], "Wv": I["L0_xattn_Wv"], "Wo": I["L0_xattn_Wo"],
        "Wk_ipa": I["L0_xattn_Wk_ipa"], "Wv_ipa": I["L0_xattn_Wv_ipa"],
        "W1T": np.ascontiguousarray(I["L0_ffn_W1"].transpose(2, 0, 1).reshape(D, E * DFF)),
        "W2T": np.ascontiguousarray(I["L0_ffn_W2"].transpose(0, 2, 1).reshape(E * DFF, D)),
        "xWq": I["L1_xattn_Wq"], "xWk": I["L1_xattn_Wk"], "xWv": I["L1_xattn_Wv"], "xWo": I["L1_xattn_Wo"],
        "We": I["L1_ffn_We"], "WeT": tr(I["L1_ffn_We"]), "bWq": I["L1_ffn_Wq"], "bWk": I["L1_ffn_Wk"],
        "bWv": I["L1_ffn_Wv"], "bWo": I["L1_ffn_Wo"], "ident": np.eye(128, dtype=np.float32),
    }
    nc = bacc.Bacc("TRN2", target_bir_lowering=False, num_devices=1)
    feed, T = {}, {}
    for name, a in arrays.items():
        a = np.ascontiguousarray(a)
        feed[f"in_{name}"] = a
        T[name] = nc.dram_tensor(f"in_{name}", a.shape, mybir.dt.from_np(a.dtype), kind="ExternalInput").ap()
    out = nc.dram_tensor("out_0", (B, N, D), F32, kind="ExternalOutput").ap()
    build(nc, T, out)
    r = run_bass_kernel_spmd(nc, [feed], core_ids=[0])
    return r.results[0]["out_0"]
```
